# Optimizing a Trainium2 kernel written in Bass

```python
import numpy as np
import jax
import jax.numpy as jnp

def _softmax(x, axis=-1):
    return jax.nn.softmax(x, axis=axis)
def _gelu(x):
    return jax.nn.gelu(x, approximate=True)
def _silu(x):
    return jax.nn.silu(x)
def _sigmoid(x):
    return jax.nn.sigmoid(x)
def _layernorm(x, axis=-1, eps=1e-5):
    m = jnp.mean(x, axis=axis, keepdims=True)
    v = jnp.var(x, axis=axis, keepdims=True)
    return (x - m) / jnp.sqrt(v + eps)
def _scatter_add(tgt, idx, src, axis=0):
    return tgt.at[idx].add(src)
def _segment_sum(src, seg, n):
    return jax.ops.segment_sum(src, seg, n)

kernel_name = 'mk_conv_seq_d2_conv_nchw64_d6ac4a'

def setup_inputs(seed: int = 0):
    np.random.seed(seed)
    _w = jnp.asarray
    def _rec_inputs():
        import jax
        import jax.numpy as jnp
        _gk = jax.random.key(seed)
        x = -0.000125 + 0.9999 * jax.random.normal(jax.random.fold_in(_gk, 1), (8, 64, 256, 256), jnp.float32)
        return x
    x = _rec_inputs()
    def _L0_conv_setup():
        import jax, jax.numpy as jnp
        from jax import lax
        import numpy as np
        B, C, H, W = (8, 64, 256, 256)
        K = 9
        R = (K - 1) // 2
        HIDDEN = 32

        def _forward(x, gauss_kernel, w1, b1, w2, b2):
            Bx, Cx, Hx, Wx = x.shape
            Kx = gauss_kernel.shape[0]
            r = (Kx - 1) // 2
            h = jax.nn.relu(jnp.einsum('bchw,co->bohw', x, w1) + b1[None, :, None, None])
            ks = jax.nn.relu(jnp.einsum('bohw,o->bhw', h, w2[:, 0]) + b2[0]) * 20.0 + 1.0
            sigma = ks / 3.0
            logits = -gauss_kernel[None, None, None] / (2.0 * sigma[..., None, None] ** 2)
            wgt = jnp.exp(logits)
            wgt = wgt / jnp.sum(wgt, axis=(-2, -1), keepdims=True)
            wflat = wgt.reshape(Bx, Hx, Wx, Kx * Kx)
            xp = jnp.pad(x, ((0, 0), (0, 0), (r, r), (r, r)))

            def step(acc, idx):
                u = idx // Kx
                v = idx % Kx
                xs = lax.dynamic_slice(xp, (0, 0, u, v), (Bx, Cx, Hx, Wx))
                wk = lax.dynamic_slice_in_dim(wflat, idx, 1, axis=3)[..., 0]
                return (acc + xs * wk[:, None, :, :], None)
            low_freq, _ = lax.scan(step, jnp.zeros_like(x), jnp.arange(Kx * Kx))
            enhanced = x + low_freq
            mu = jnp.mean(enhanced, axis=(2, 3), keepdims=True)
            var = jnp.var(enhanced, axis=(2, 3), keepdims=True)
            return (enhanced - mu) / jnp.sqrt(var + 1e-05)
        key = jax.random.key(seed)
        k1, k2, k3, k4, k5 = jax.random.split(key, 5)
        x = jax.random.normal(k1, (B, C, H, W), dtype=jnp.float32)
        off = jnp.arange(K, dtype=jnp.float32) - R
        gauss_kernel = off[:, None] ** 2 + off[None, :] ** 2
        w1 = jax.random.normal(k2, (C, HIDDEN), dtype=jnp.float32) * (1.0 / np.sqrt(C))
        b1 = jax.random.normal(k3, (HIDDEN,), dtype=jnp.float32) * 0.01
        w2 = jax.random.normal(k4, (HIDDEN, 1), dtype=jnp.float32) * (1.0 / np.sqrt(HIDDEN))
        b2 = jax.random.normal(k5, (1,), dtype=jnp.float32) * 0.01
        return {'x': x, 'gauss_kernel': gauss_kernel, 'w1': w1, 'b1': b1, 'w2': w2, 'b2': b2}
    _L0_conv_all = _L0_conv_setup()
    _L0_conv_in = {k: v for k, v in _L0_conv_all.items() if k in ('gauss_kernel', 'w1', 'b1', 'w2', 'b2', )}
    del _L0_conv_all

    def _L1_conv_setup():
        import jax, jax.numpy as jnp
        import numpy as np
        K = 3
        PAD = 1
        GAIN = 1.4142135623730951
        STD_SPATIAL = GAIN / K
        EPS = 1e-10
        NEG_SLOPE = 0.1
        RES_SCALE = 1.0

        def _filter_norm_spatial(f):
            m = f.mean(axis=1, keepdims=True)
            s = f.std(axis=1, keepdims=True, ddof=1)
            return (f - m) / (s + EPS) * STD_SPATIAL

        def _filter_norm_channel(f, std_ch, C):
            B = f.shape[0]
            f = f.reshape(B, C, K * K)
            m = f.mean(axis=2, keepdims=True)
            s = f.std(axis=2, keepdims=True, ddof=1)
            f = (f - m) / (s + EPS)
            return f.reshape(B, -1) * std_ch

        def _ddf_mul(x, cf, sf):
            B, C, H, W = x.shape
            xp = jnp.pad(x, ((0, 0), (0, 0), (PAD, PAD), (PAD, PAD)))
            out = jnp.zeros_like(x)
            for t in range(K * K):
                u, v = (t // K, t % K)
                patch = xp[:, :, u:u + H, v:v + W]
                out = out + patch * cf[:, :, t, None, None] * sf[:, t:t + 1, :, :]
            return out

        def _ddfpack(x, Ws, bs, W1, b1, W2, b2, std_ch):
            B, C, H, W = x.shape
            sf = jnp.einsum('bchw,kc->bkhw', x, Ws) + bs[None, :, None, None]
            sf = _filter_norm_spatial(sf)
            pooled = x.mean(axis=(2, 3))
            h = jax.nn.relu(pooled @ W1.T + b1)
            cf = h @ W2.T + b2
            cf = _filter_norm_channel(cf, std_ch, C).reshape(B, C, K * K)
            return _ddf_mul(x, cf, sf)
        key = jax.random.key(seed)
        ks = jax.random.split(key, 10)
        B, C, H, W = (16, 64, 192, 192)
        mid = int(C * 0.2)
        return {'x': jax.random.normal(ks[0], (B, C, H, W), jnp.float32), 'Ws': jax.random.normal(ks[1], (K * K, C), jnp.float32) * 0.1, 'bs': jax.random.normal(ks[2], (K * K,), jnp.float32) * 0.1, 'W1': jax.random.normal(ks[3], (mid, C), jnp.float32) * 0.1, 'b1': jax.random.normal(ks[4], (mid,), jnp.float32) * 0.1, 'W2': jax.random.normal(ks[5], (C * K * K, mid), jnp.float32) * 0.1, 'b2': jax.random.normal(ks[6], (C * K * K,), jnp.float32) * 0.1, 'std_ch': jax.random.normal(ks[7], (C * K * K,), jnp.float32) * STD_SPATIAL, 'Wc': jax.random.normal(ks[8], (C, C, K, K), jnp.float32) * 0.05, 'bc': jax.random.normal(ks[9], (C,), jnp.float32) * 0.05}
    _L1_conv_all = _L1_conv_setup()
    _L1_conv_in = {k: v for k, v in _L1_conv_all.items() if k in ('Ws', 'bs', 'W1', 'b1', 'W2', 'b2', 'std_ch', 'Wc', 'bc', )}
    del _L1_conv_all

    return {
        "x": x,
        "L0_conv_gauss_kernel": _L0_conv_in["gauss_kernel"],
        "L0_conv_w1": _L0_conv_in["w1"],
        "L0_conv_b1": _L0_conv_in["b1"],
        "L0_conv_w2": _L0_conv_in["w2"],
        "L0_conv_b2": _L0_conv_in["b2"],
        "L1_conv_Ws": _L1_conv_in["Ws"],
        "L1_conv_bs": _L1_conv_in["bs"],
        "L1_conv_W1": _L1_conv_in["W1"],
        "L1_conv_b1": _L1_conv_in["b1"],
        "L1_conv_W2": _L1_conv_in["W2"],
        "L1_conv_b2": _L1_conv_in["b2"],
        "L1_conv_std_ch": _L1_conv_in["std_ch"],
        "L1_conv_Wc": _L1_conv_in["Wc"],
        "L1_conv_bc": _L1_conv_in["bc"],
    }

def reference(x, L0_conv_gauss_kernel, L0_conv_w1, L0_conv_b1, L0_conv_w2, L0_conv_b2, L1_conv_Ws, L1_conv_bs, L1_conv_W1, L1_conv_b1, L1_conv_W2, L1_conv_b2, L1_conv_std_ch, L1_conv_Wc, L1_conv_bc):
    import jax
    import jax.numpy as jnp
    def _L0_conv_ref(x, gauss_kernel, w1, b1, w2, b2):
        import jax, jax.numpy as jnp
        from jax import lax
        import numpy as np
        B, C, H, W = (8, 64, 256, 256)
        K = 9
        R = (K - 1) // 2
        HIDDEN = 32

        def _forward(x, gauss_kernel, w1, b1, w2, b2):
            Bx, Cx, Hx, Wx = x.shape
            Kx = gauss_kernel.shape[0]
            r = (Kx - 1) // 2
            h = jax.nn.relu(jnp.einsum('bchw,co->bohw', x, w1) + b1[None, :, None, None])
            ks = jax.nn.relu(jnp.einsum('bohw,o->bhw', h, w2[:, 0]) + b2[0]) * 20.0 + 1.0
            sigma = ks / 3.0
            logits = -gauss_kernel[None, None, None] / (2.0 * sigma[..., None, None] ** 2)
            wgt = jnp.exp(logits)
            wgt = wgt / jnp.sum(wgt, axis=(-2, -1), keepdims=True)
            wflat = wgt.reshape(Bx, Hx, Wx, Kx * Kx)
            xp = jnp.pad(x, ((0, 0), (0, 0), (r, r), (r, r)))

            def step(acc, idx):
                u = idx // Kx
                v = idx % Kx
                xs = lax.dynamic_slice(xp, (0, 0, u, v), (Bx, Cx, Hx, Wx))
                wk = lax.dynamic_slice_in_dim(wflat, idx, 1, axis=3)[..., 0]
                return (acc + xs * wk[:, None, :, :], None)
            low_freq, _ = lax.scan(step, jnp.zeros_like(x), jnp.arange(Kx * Kx))
            enhanced = x + low_freq
            mu = jnp.mean(enhanced, axis=(2, 3), keepdims=True)
            var = jnp.var(enhanced, axis=(2, 3), keepdims=True)
            return (enhanced - mu) / jnp.sqrt(var + 1e-05)
        return _forward(x, gauss_kernel, w1, b1, w2, b2)

    def _L1_conv_ref(x, Ws, bs, W1, b1, W2, b2, std_ch, Wc, bc):
        import jax, jax.numpy as jnp
        import numpy as np
        K = 3
        PAD = 1
        GAIN = 1.4142135623730951
        STD_SPATIAL = GAIN / K
        EPS = 1e-10
        NEG_SLOPE = 0.1
        RES_SCALE = 1.0

        def _filter_norm_spatial(f):
            m = f.mean(axis=1, keepdims=True)
            s = f.std(axis=1, keepdims=True, ddof=1)
            return (f - m) / (s + EPS) * STD_SPATIAL

        def _filter_norm_channel(f, std_ch, C):
            B = f.shape[0]
            f = f.reshape(B, C, K * K)
            m = f.mean(axis=2, keepdims=True)
            s = f.std(axis=2, keepdims=True, ddof=1)
            f = (f - m) / (s + EPS)
            return f.reshape(B, -1) * std_ch

        def _ddf_mul(x, cf, sf):
            B, C, H, W = x.shape
            xp = jnp.pad(x, ((0, 0), (0, 0), (PAD, PAD), (PAD, PAD)))
            out = jnp.zeros_like(x)
            for t in range(K * K):
                u, v = (t // K, t % K)
                patch = xp[:, :, u:u + H, v:v + W]
                out = out + patch * cf[:, :, t, None, None] * sf[:, t:t + 1, :, :]
            return out

        def _ddfpack(x, Ws, bs, W1, b1, W2, b2, std_ch):
            B, C, H, W = x.shape
            sf = jnp.einsum('bchw,kc->bkhw', x, Ws) + bs[None, :, None, None]
            sf = _filter_norm_spatial(sf)
            pooled = x.mean(axis=(2, 3))
            h = jax.nn.relu(pooled @ W1.T + b1)
            cf = h @ W2.T + b2
            cf = _filter_norm_channel(cf, std_ch, C).reshape(B, C, K * K)
            return _ddf_mul(x, cf, sf)
        out = _ddfpack(x, Ws, bs, W1, b1, W2, b2, std_ch)
        out = jnp.where(out >= 0, out, NEG_SLOPE * out)
        out = jax.lax.conv_general_dilated(out, Wc, window_strides=(1, 1), padding='SAME', dimension_numbers=('NCHW', 'OIHW', 'NCHW'))
        out = out + bc[None, :, None, None]
        return x + out * RES_SCALE

    def _gn(v, G=32, eps=1e-5):
        B_, C_, H_, W_ = v.shape
        g = v.reshape(B_, G, C_ // G, H_, W_)
        m = jnp.mean(g, axis=(2, 3, 4), keepdims=True)
        s = jnp.var(g, axis=(2, 3, 4), keepdims=True)
        return ((g - m) / jnp.sqrt(s + eps)).reshape(v.shape)

    def _ln_c(v, eps=1e-6):
        m = jnp.mean(v, axis=1, keepdims=True)
        s = jnp.var(v, axis=1, keepdims=True)
        return (v - m) / jnp.sqrt(s + eps)

    def _ln_t(v, eps=1e-5):
        m = jnp.mean(v, axis=-1, keepdims=True)
        s = jnp.var(v, axis=-1, keepdims=True)
        return (v - m) / jnp.sqrt(s + eps)

    def _to_tokens(v):
        B_, C_, H_, W_ = v.shape
        return v.reshape(B_, C_, H_ * W_).transpose(0, 2, 1)
    def _from_tokens(t, like):
        B_, C_, H_, W_ = like.shape
        return t.transpose(0, 2, 1).reshape(B_, C_, H_, W_)

    x = _L0_conv_ref(x, L0_conv_gauss_kernel, L0_conv_w1, L0_conv_b1, L0_conv_w2, L0_conv_b2)
    x = _L1_conv_ref(x, L1_conv_Ws, L1_conv_bs, L1_conv_W1, L1_conv_b1, L1_conv_W2, L1_conv_b2, L1_conv_std_ch, L1_conv_Wc, L1_conv_bc)
    return x


_drawn_inputs = setup_inputs


def setup_inputs(seed=0):
    import zlib

    import numpy as np

    out = dict(_drawn_inputs(seed))
    spreads = {}
    factors = {'L0_conv_b1': 5.481, 'L1_conv_W1': 8.0}
    for name, (base, spread) in spreads.items():
        noise = np.random.default_rng([zlib.crc32(name.encode()), seed]).standard_normal(out[name].shape)
        drawn = base * np.exp(spread * noise) if base else spread * noise
        out[name] = jnp.asarray(drawn.astype(out[name].dtype))
    for name, factor in factors.items():
        out[name] = (out[name] * factor).astype(out[name].dtype)
    return out
```

```python
from contextlib import ExitStack

import numpy as np

import concourse.bass as bass
from concourse import mybir

ALU = mybir.AluOpType
ACT = mybir.ActivationFunctionType
F32 = mybir.dt.float32
BF16 = mybir.dt.bfloat16
AX_X = mybir.AxisListType.X

B, C, H, W = 8, 64, 256, 256
HID, MID = 32, 12
K0, R0 = 9, 4
ROWS = H // 2
BAND = 8
NBAND = ROWS // BAND
COLS = 64
NQ = W // COLS
NT = COLS // 16
UB = 2 * NQ
XW = W + 2 * R0
ER, EW = ROWS + 4, W + 2
BLK = 2 * NT + 1
TAPS = 9
NC1 = ROWS // 2 + 1
NO1 = ROWS // 2
NPIX = H * W
STD_SPATIAL = 1.4142135623730951 / 3
EPS1 = 1e-10
FAR = -1.0e30
BF16_ONE = 0x3F80
AROWS = 96
XSLOTS = 4


def build(nc, x, graw, gin, gout, sel_a, ident, w1, w2, pair, ws, bs, center, varsum,
          sel_sf, wconv, small, mlp1, mlp2, mb2, stdch, out):
    with ExitStack() as ctx:
        def sb(name, shape, dt=F32):
            return ctx.enter_context(nc.sbuf_tensor(name, shape, dt))

        def sem(name):
            return ctx.enter_context(nc.semaphore(name))

        E = sb("image", [128, ER, EW])
        g_neg = sb("g_neg", [128, 2, 128])
        sel_a_sb = sb("sel_a_sb", [AROWS, UB, 128], BF16)
        ident_sb = sb("ident_sb", [128, 128])
        w1_sb = sb("w1_sb", [128, 2 * HID])
        w2_sb = sb("w2_sb", [2 * HID, NQ, AROWS])
        ws_sb = sb("ws_sb", [128, AROWS])
        varsum_sb = sb("varsum_sb", [AROWS, AROWS])
        stats = sb("stats", [128, NBAND * NQ, 6])
        cols = sb("cols", [128, 64])
        b1_c, b2_c, bs_c, bconv_c, mb1_c = (cols[:, i:i + 1] for i in range(5))
        mv = cols[:, 6:8]
        pv = cols[:, 8:12]
        var_c, sd_c, rstd_c, nmr_c = (cols[:, i:i + 1] for i in range(12, 16))
        sums = cols[:, 16:24]
        pooled_c, h12_c = cols[:, 24:25], cols[0:MID, 25:26]
        cf = cols[:, 26:35]
        cm_c, css_c, csd_c, cr_c = (cols[:, i:i + 1] for i in range(35, 39))
        rsum = [cols[:, 40:44], cols[:, 44:48]]
        wmean = cols[:, 48:54]
        cc = cols[:, 54:63]

        xreg = sb("xreg", [128, XSLOTS * BAND * XW])
        work = sb("work", [128, 8624])

        def carve(region, start, n):
            assert start + n <= region.shape[1]
            return region[:, start:start + n], start + n

        xr = xreg[:, :].rearrange("p (r w) -> p r w", w=XW)
        at = 0
        xt_f, at = carve(work, at, 2 * BLK * 2 * 65)
        xt = xt_f.rearrange("p (n j s c) -> p n j s c", n=2, j=BLK, s=2)
        xb_f, at = carve(work, at, 3 * 384)
        xb = xb_f.rearrange("p (g j o) -> p g j o", g=3, j=3)
        h_f, at = carve(work, at, 512)
        h_sb = h_f[0:2 * HID, :]
        ka_f, at = carve(work, at, 512)
        kb_f, at = carve(work, at, 512)
        ka, kb = ka_f[0:AROWS, :], kb_f[0:AROWS, :]
        as_f, at = carve(work, at, 2 * 256)
        a_st = as_f[0:AROWS, :].bitcast(BF16).rearrange("p (n f) -> p n f", n=2)
        band_f, at = carve(work, at, 2 * 1024)
        band = band_f.rearrange("p (n t k o) -> p n t k o", n=2, t=NT, k=2)
        low_f, at = carve(work, at, 2 * 512)
        low_t = low_f.rearrange("p (n t s c) -> p n t s c", n=2, t=NT, s=2)
        graw_sb = work[:, 0:256]
        gin_sb = work[:, 512:768]
        gout_sb = work[:, 1024:1280]
        center_sb = work[0:AROWS, 1536:1536 + AROWS]
        bs_raw = work[0:AROWS, 1700:1701]

        at = 0
        y1_f, at = carve(xreg, at, 8 * EW)
        y1 = y1_f.rearrange("p (r w) -> p r w", w=EW)
        p_f, at = carve(xreg, at, 4 * 512)
        prod = p_f.rearrange("p (n f) -> p n f", n=4)
        suma, at = carve(xreg, at, 512)
        sumb, at = carve(xreg, at, 512)
        tmp_f, at = carve(xreg, at, 1024)
        tmp = tmp_f.rearrange("p (n f) -> p n f", n=2)
        sf_f, at = carve(xreg, at, TAPS * 64)
        sel_sf_sb = sf_f[0:AROWS, :].bitcast(BF16).rearrange("p (t m) -> p t m", t=TAPS)
        stage_f, at = carve(xreg, at, 1024)
        stage = stage_f.rearrange("p (n f) -> p n f", n=2)
        at = 0
        wconv_f, at = carve(work, at, TAPS * 128)
        wconv_sb = wconv_f.rearrange("p (t m) -> p t m", t=TAPS)
        mlp2_f, at = carve(work, at, TAPS * 128)
        mlp2_sb = mlp2_f[0:MID, :].rearrange("p (t m) -> p t m", t=TAPS)
        pair_f, at = carve(work, at, 256)
        pair_sb = pair_f.rearrange("p (k m) -> p k m", k=2)
        mlp1_sb, at = carve(work, at, MID)
        mb2_sb, at = carve(work, at, TAPS)
        std_sb, at = carve(work, at, TAPS + 1)
        ss_f, at = carve(work, at, 2 * 256)
        sf_st = ss_f[0:AROWS, :].bitcast(BF16).rearrange("p (n f) -> p n f", n=2)
        fs_f, at = carve(work, at, 2 * 512)
        fs = fs_f[0:AROWS, :].rearrange("p (n f) -> p n f", n=2)
        rows_f, at = carve(work, at, 5 * 512)
        lifted, at = carve(work, at, 512)
        fsq, fsd, frec, fnorm, fres = (rows_f[0:AROWS, 512 * i:512 * i + 512] for i in range(5))

        banks = [ctx.enter_context(nc.psum_tensor(f"bank{i}", [128, 512], F32)) for i in range(8)]
        h_ps, ks_ps, xt_ps, low_ps, turn_ps = banks[0], banks[1], banks[2], banks[5:7], banks[7]
        abc_ps = banks[3:5]
        spread_ps = [banks[0], banks[3], banks[4]]
        f_ps, var_ps, conv_ps, small_ps = banks[1], banks[2], banks[5:7], banks[7]

        const_in = sem("const_in")
        setup_dve = sem("setup_dve")
        setup_pool = sem("setup_pool")
        center_ready = sem("center_ready")
        x_in = [sem(f"x_in{i}") for i in range(XSLOTS)]
        ring_free = sem("ring_free")
        pads_done = sem("pads_done")
        pad16_done = sem("pad16_done")
        h_ready, h_done = sem("h_ready"), sem("h_done")
        ks_ready, k1_done, k2_done, ksq_done, a_ready = (
            sem(n) for n in ("ks_ready", "k1_done", "k2_done", "ksq_done", "a_ready"))
        a_hi, a_res, a_mid, a_split = (sem(n) for n in ("a_hi", "a_res", "a_mid", "a_split"))
        abc_ready, arg_done, exp_done, bands_done = (
            sem(n) for n in ("abc_ready", "arg_done", "exp_done", "bands_done"))
        rsum_done, low_done, turn_ready, e_done = (
            sem(n) for n in ("rsum_done", "low_done", "turn_ready", "e_done"))
        xb_done, xt_ready, xt_done = sem("xb_done"), sem("xt_ready"), sem("xt_done")
        stats_done, mv_done, pair_ready, nd = (
            sem(n) for n in ("stats_done", "mv_done", "pair_ready", "norm_steps"))
        nvar_done, nsd_done, ncoef_done = sem("nvar_done"), sem("nsd_done"), sem("ncoef_done")
        norm_act, norm_dve, sums_dve = sem("norm_act"), sem("norm_dve"), sem("sums_dve")
        pooled_done, mlp1_ready, h12_done, mlp2_ready = (
            sem(n) for n in ("pooled_done", "mlp1_ready", "h12_done", "mlp2_ready"))
        cf_steps, css_done, csd_done = sem("cf_steps"), sem("css_done"), sem("csd_done")
        halo_in, l1_const = sem("halo_in"), sem("l1_const")
        f_ready, fs_done, fsq_done, var_ready, fsd_done = (
            sem(n) for n in ("f_ready", "fs_done", "fsq_done", "var_ready", "fsd_done"))
        feps_done, frec_done, fnorm_done, f_hi, f_res, f_mid, f_split = (
            sem(n) for n in ("feps_done", "frec_done", "fnorm_done", "f_hi", "f_res", "f_mid", "f_split"))
        spread_ready, prod_done, suma_done, sumb_done = (
            sem(n) for n in ("spread_ready", "prod_done", "suma_done", "sumb_done"))
        y1_ready, y1_edge, conv_ready, out_done = (
            sem(n) for n in ("y1_ready", "y1_edge", "conv_ready", "out_done"))
        lifted_done = sem("lifted_done")
        stored = [sem("stored0"), sem("stored1")]

        N_CONST = 12
        block = ctx.enter_context(nc.Block())

        def x_loaded(b, i, kk):
            slot = kk % XSLOTS
            per_image = 32 * (5 if slot == 0 else 4)
            return x_in[slot], b * per_image + i * 32 + 32 * (kk // XSLOTS + 1)

        def pieces8(nn):
            first = BAND * nn + R0
            if nn < XSLOTS - 1:
                return [(first, 0, BAND)]
            return [(first, 0, R0), (0, R0, R0)]

        def hold(eng, *waits):
            values = [(which, eng.to_reg(value)) for which, value in waits]
            eng.wait_ge(const_in, 16 * N_CONST)
            for which, value in values:
                eng.wait_ge(which, value)

        @block.sync
        def _(sp):
            for dst, src in ((graw_sb, graw), (gin_sb, gin), (gout_sb, gout),
                             (sel_a_sb[:, :, :].bitcast(mybir.dt.uint16), sel_a), (ident_sb[:, :], ident), (w1_sb[:, :], w1),
                             (w2_sb[:, :, :], w2), (ws_sb[:, :], ws),
                             (varsum_sb[:, :], varsum), (center_sb, center), (bs_raw, bs),
                             (cols[:, 0:5], small)):
                sp.dma_start(dst, src).then_inc(const_in, 16)

            def load_group(b, i, kk):
                static = isinstance(i, int)
                k = XSLOTS * i + kk
                slot = kk % XSLOTS
                img = x[bass.ds(b, 1)].rearrange("a c r w -> (a c) r w")
                for s in range(2):
                    lo, n, at = s * ROWS + BAND * k - R0, BAND, BAND * slot
                    if static and k == 0 and s == 0:
                        lo, n, at = 0, BAND - R0, at + R0
                    if static and k == NBAND and s == 1:
                        n = BAND - R0
                    src = img[:, lo:lo + n, :] if static else img[:, bass.ds(lo, n), :]
                    sp.dma_start(xr[C * s:C * s + C, at:at + n, R0:R0 + W], src).then_inc(x_in[slot], 16)

            with sp.Fori(0, B) as b:
                sp.nop().then_inc(ring_free, 1)
                for k in range(4):
                    load_group(b, 0, k)

                def refill(i, kk):
                    hold(sp, (e_done, b * (NBAND * NQ) + i * (4 * NQ) + (kk - 4 + 1) * NQ))
                    load_group(b, i, kk)

                with sp.Fori(1, 4) as i:
                    for kk in range(4):
                        refill(i, kk)
                refill(4, 0)

                hold(sp, (e_done, (b + 1) * (NBAND * NQ)))
                for dst, src in ((pair_sb, pair), (wconv_sb, wconv), (mlp1_sb, mlp1), (mlp2_sb, mlp2), (mb2_sb, mb2),
                                 (std_sb[:, 0:TAPS], stdch), (sel_sf_sb.bitcast(mybir.dt.uint16), sel_sf)):
                    sp.dma_start(dst, src).then_inc(l1_const, 16)
                hold(sp, (norm_act, 5 * b + 5), (norm_dve, 3 * b + 3))
                sp.dma_start(E[0:C, ROWS + 2:ROWS + 4, 1:1 + W], E[C:2 * C, 2:4, 1:1 + W]).then_inc(halo_in, 16)
                sp.dma_start(E[C:2 * C, 0:2, 1:1 + W], E[0:C, ROWS:ROWS + 2, 1:1 + W]).then_inc(halo_in, 16)

                with sp.Fori(0, NO1 // 2) as i:
                    for j in range(2):
                        hold(sp, (out_done, b * NO1 + 2 * i + (1 + j)))
                        dst = out[bass.ds(b, 1)].rearrange("a c r w -> (a c) r w")
                        for s in range(2):
                            src = stage[C * s:C * s + C, j, :].rearrange("p (r w) -> p r w", w=W)
                            sp.dma_start(dst[:, bass.ds(i * 4 + (s * ROWS + 2 * j), 2), :], src)\
                              .then_inc(stored[j], 16)
                hold(sp, *((stored[j], (b + 1) * (32 * NO1 // 2)) for j in range(2)))

        @block.tensor
        def _(pe):
            pe.wait_ge(const_in, 16 * N_CONST)
            pe.matmul(small_ps[0:AROWS, 0:1], center_sb, bs_raw, start=True, stop=True)\
              .then_inc(center_ready, 1)
            pe.wait_ge(setup_dve, 3)

            def hidden(b, i, nn, q):
                if not (isinstance(i, int) and 16 * i + 4 * nn + q == 0):
                    pe.wait_ge(h_done, b * 64 + i * 16 + (nn * 4 + q))
                dst = h_ps[0:2 * HID, :].rearrange("p (g r c) -> p g r c", g=8, r=BAND)
                parts = pieces8(nn % XSLOTS)
                for ring, row, n in parts:
                    src = xr[:, ring:ring + n, R0 + COLS * q:R0 + COLS * q + COLS]
                    mm = pe.matmul(dst[:, :, row:row + n, :], w1_sb[:, :],
                                   src.rearrange("p r (g c) -> p g r c", c=8), start=True, stop=True)
                mm.then_inc(h_ready, 1)

            def width(b, i, nn, q):
                pe.wait_ge(h_done, b * 64 + i * 16 + (nn * 4 + q + 1))
                if q == 0 and not (isinstance(i, int) and i == 0 and nn == 0):
                    pe.wait_ge(k1_done, b * NBAND + i * 4 + nn)
                mm = pe.matmul(ks_ps[0:AROWS, :], w2_sb[:, q, :], h_sb,
                               start=(q == 0), stop=(q == NQ - 1))
                if q == NQ - 1:
                    mm.then_inc(ks_ready, 1)

            def turn_blocks(b, i, nn, q, g):
                first = isinstance(i, int) and 4 * i + nn == 0 and q == 0 and g == 0
                if not first:
                    pe.wait_ge(xt_done, b * 192 + i * 48 + (nn * 12 + q * 3 + g))
                pe.wait_ge(xb_done, b * 192 + i * 48 + (nn * 12 + q * 3 + g + 1))
                for j in range(3):
                    mm = pe.transpose(xt_ps[:, 128 * j:128 * j + 128], xb[:, g, j, :], ident_sb[:, :])
                mm.then_inc(xt_ready, 1)

            def spread_a(b, i, nn, u, fresh=False):
                if not fresh:
                    pe.wait_ge(arg_done, b * 128 + i * 32 + (nn * 8 + u - 1))
                if u == 0 or fresh:
                    pe.wait_ge(a_split, b * NBAND + i * 4 + (nn + 1))
                pe.matmul(abc_ps[u % 2][:, :], sel_a_sb[:, u, :], a_st[:, nn % 2, :],
                          start=True, stop=True).then_inc(abc_ready, 1)

            def blur(b, i, nn, u, fresh):
                s, q = u % 2, u // 2
                lp = low_ps[u % 2]
                pe.wait_ge(exp_done, b * 128 + i * 32 + (nn * 8 + u + 1))
                if s == 0:
                    pe.wait_ge(xt_done, b * 192 + i * 48 + (nn * 12 + q * 3 + 3))
                if not fresh:
                    pe.wait_ge(low_done, b * 128 + i * 32 + (nn * 8 + u - 1))
                for t in range(NT):
                    o = lp[:, 65 * t:65 * t + 65]
                    lhs = band[:, u % 2, t]
                    pe.matmul(o, lhs[:, 0, :], xt[:, q % 2, 2 * t + 1, s, :], start=True, stop=False)
                    pe.matmul(o[0:64], lhs[:, 1, 0:64], xt[:, q % 2, 2 * t, s, :], start=False, stop=True)
                    mm = pe.matmul(o[64:128], lhs[:, 1, 64:128], xt[:, q % 2, 2 * t + 2, s, :],
                                   start=False, stop=True)
                mm.then_inc(bands_done, 1)

            def turn_back(b, i, nn, q, fresh):
                pe.wait_ge(low_done, b * 128 + i * 32 + (nn * 8 + 2 * q + 2))
                if not fresh:
                    pe.wait_ge(e_done, b * 64 + i * 16 + (nn * 4 + q))
                for t in range(NT):
                    mm = pe.transpose(turn_ps[:, 128 * t:128 * t + 128],
                                      low_t[:, q % 2, t].rearrange("p s c -> p (s c)"), ident_sb[:, :])
                mm.then_inc(turn_ready, 1)

            def band_steps(b, i, nn, last):
                if not last:
                    pe.wait_ge(*x_loaded(b, i, nn + 2))
                    if isinstance(i, int) and 4 * i + nn + 2 == NBAND:
                        pe.wait_ge(pad16_done, b + 1)
                for u in range(UB):
                    first = isinstance(i, int) and 4 * i + nn == 0
                    if u + 2 < UB:
                        spread_a(b, i, nn, u + 2)
                    elif not last:
                        spread_a(b, i, nn + 1, u + 2 - UB)
                    if not last:
                        if u == 0:
                            hidden(b, i, nn + 1, 0)
                        if u == 1:
                            width(b, i, nn + 1, 1)
                            hidden(b, i, nn + 1, 2)
                        if u == 2:
                            width(b, i, nn + 1, 3)
                    blur(b, i, nn, u, fresh=first and u < 2)
                    if not last:
                        if u == 0:
                            width(b, i, nn + 1, 0)
                            hidden(b, i, nn + 1, 1)
                        if u == 1:
                            width(b, i, nn + 1, 2)
                            hidden(b, i, nn + 1, 3)
                    q = u // 2
                    nq, nb = (q + 1, nn) if q + 1 < NQ else (0, nn + 1)
                    if not (last and q + 1 == NQ):
                        for g in ((0, 1) if u % 2 == 0 else (2,)):
                            turn_blocks(b, i, nb, nq, g)
                    if u % 2:
                        turn_back(b, i, nn, q, fresh=first and q == 0)

            def filters(b, i, kk):
                if not (isinstance(i, int) and 4 * i + kk == 0):
                    pe.wait_ge(fs_done, b * NC1 + i * 4 + kk)
                rows = E[:, bass.ds(i * 8 + (2 * kk + 1), 2), 1:1 + W] if not isinstance(i, int) else \
                    E[:, 8 * i + 2 * kk + 1:8 * i + 2 * kk + 3, 1:1 + W]
                pe.matmul(f_ps[0:AROWS, :], ws_sb[:, :], rows, start=True, stop=True).then_inc(f_ready, 1)

            def variance(b, i, kk):
                pe.wait_ge(fsq_done, b * NC1 + i * 4 + (kk + 1))
                if not (isinstance(i, int) and 4 * i + kk == 0):
                    pe.wait_ge(fsd_done, b * NC1 + i * 4 + kk)
                pe.matmul(var_ps[0:AROWS, :], varsum_sb[:, :], fsq, start=True, stop=True)\
                  .then_inc(var_ready, 1)

            def spread_filter(b, i, kk, t, fresh):
                if t == 0:
                    pe.wait_ge(f_split, b * NC1 + i * 4 + (kk + 1))
                if not (fresh and t < 3):
                    pe.wait_ge(prod_done, b * (NC1 * TAPS) + i * (4 * TAPS) + (kk * TAPS + t - 2))
                pe.matmul(spread_ps[t % 3][:, :], sel_sf_sb[:, t, :], sf_st[:, kk % 2, :],
                          start=True, stop=True).then_inc(spread_ready, 1)

            def conv_tap(b, i, kk, t):
                if t == 0:
                    if isinstance(i, int) and 4 * i + kk == 1:
                        pe.wait_ge(y1_edge, 4 * b + 3)
                        pe.wait_ge(l1_const, 112 * (b + 1))
                    if not (isinstance(i, int) and 4 * i + kk < 3):
                        pe.wait_ge(out_done, b * NO1 + i * 4 + (kk - 2))
                if t == 3:
                    pe.wait_ge(y1_ready, b * NC1 + i * 4 + (kk + 1))
                    if isinstance(i, int) and 4 * i + kk == NO1:
                        pe.wait_ge(y1_edge, 4 * b + 4)
                dy, dx = t // 3, t % 3
                r = (2 * ((kk - 1) % 4) + dy) % 8
                cp = conv_ps[kk % 2]
                for row, n in ([(0, 2)] if r < 7 else [(0, 1), (1, 1)]):
                    ring = (r + row) % 8
                    mm = pe.matmul(cp[:, W * row:W * row + W * n], wconv_sb[:, t, :],
                                   y1[:, ring:ring + n, dx:dx + W],
                                   start=(t == 0), stop=(t == TAPS - 1), skip_group_check=True)
                if t == TAPS - 1:
                    mm.then_inc(conv_ready, 1)

            def l1_step(b, i, kk):
                k = 4 * i + kk if isinstance(i, int) else None
                if k != NC1 - 1:
                    filters(b, i, kk + 1)
                for t in range(TAPS):
                    spread_filter(b, i, kk, t, fresh=(k == 0))
                    if k is None or k >= 2:
                        conv_tap(b, i, kk - 1, t)
                    if t == 2 and k != NC1 - 1:
                        variance(b, i, kk + 1)

            with pe.Fori(0, B) as b:
                pe.wait_ge(pads_done, 3 * b + 3)
                pe.wait_ge(setup_pool, b + 5)
                pe.wait_ge(*x_loaded(b, 0, 0))
                pe.wait_ge(*x_loaded(b, 0, 1))
                for q in range(NQ):
                    hidden(b, 0, 0, q)
                    width(b, 0, 0, q)
                for g in range(3):
                    turn_blocks(b, 0, 0, 0, g)
                for u in range(2):
                    spread_a(b, 0, 0, u, fresh=True)
                for nn in range(4):
                    band_steps(b, 0, nn, False)
                with pe.Fori(1, 3) as i:
                    for nn in range(4):
                        band_steps(b, i, nn, False)
                for nn in range(4):
                    band_steps(b, 3, nn, nn == 3)

                pe.wait_ge(mv_done, b + 1)
                pe.wait_ge(l1_const, 112 * (b + 1))
                pe.matmul(small_ps[:, 0:2], pair_sb[:, 0, :], mv, start=True, stop=True)
                pe.matmul(small_ps[:, 2:4], pair_sb[:, 1, :], mv, start=True, stop=True)\
                  .then_inc(pair_ready, 1)
                pe.wait_ge(pooled_done, b + 1)
                pe.wait_ge(l1_const, 112 * (b + 1))
                pe.matmul(small_ps[0:MID, 8:9], mlp1_sb, pooled_c, start=True, stop=True)\
                  .then_inc(mlp1_ready, 1)
                pe.wait_ge(halo_in, 32 * (b + 1))
                filters(b, 0, 0)
                pe.wait_ge(h12_done, b + 1)
                for t in range(TAPS):
                    mm = pe.matmul(small_ps[:, 16 + t:17 + t], mlp2_sb[:, t, :], h12_c, start=True, stop=True)
                mm.then_inc(mlp2_ready, 1)
                variance(b, 0, 0)
                l1_step(b, 0, 0)
                for kk in range(1, 5):
                    l1_step(b, 0, kk)
                with pe.Fori(1, 15) as i:
                    for kk in range(1, 5):
                        l1_step(b, i, kk)
                for kk in range(1, 5):
                    l1_step(b, 15, kk)
                for t in range(TAPS):
                    conv_tap(b, 15, 4, t)

        @block.scalar
        def _(act):
            act.wait_ge(const_in, 16 * N_CONST)

            def relu(b, i, nn, q):
                act.wait_ge(h_ready, b * 64 + i * 16 + (nn * 4 + q + 1))
                act.activation(h_sb, h_ps[0:2 * HID, :], ACT.Relu,
                               bias=b1_c[0:2 * HID]).then_inc(h_done, 1)

            def square(b, i, nn):
                act.wait_ge(k2_done, b * NBAND + i * 4 + (nn + 1))
                act.activation(ka, kb, ACT.Square, scale=float(4.5 ** -0.5)).then_inc(ksq_done, 1)

            def keep_block(b, i, nn, q, g):
                act.wait_ge(xt_ready, b * 192 + i * 48 + (nn * 12 + q * 3 + g + 1))
                act.activation(xt[:, q % 2, 3 * g:3 * g + 3, :, 0:C],
                               xt_ps[:, 0:384].rearrange("p (j s c) -> p j s c", j=3, s=2),
                               ACT.Copy).then_inc(xt_done, 1)

            def weights(b, i, nn, u):
                act.wait_ge(arg_done, b * 128 + i * 32 + (nn * 8 + u + 1))
                t = band[:, u % 2].rearrange("p t k o -> p (t k o)")
                act.activation(t, t, ACT.Exp).then_inc(exp_done, 1)

            def band_steps(b, i, nn, last):
                for u in range(UB):
                    if not last:
                        if u == 0:
                            relu(b, i, nn + 1, 0)
                            relu(b, i, nn + 1, 1)
                        if u == 1:
                            relu(b, i, nn + 1, 2)
                            relu(b, i, nn + 1, 3)
                        if u == 3:
                            square(b, i, nn + 1)
                    q = u // 2
                    nq, nb = (q + 1, nn) if q + 1 < NQ else (0, nn + 1)
                    more = not (last and q + 1 == NQ)
                    if more:
                        keep_block(b, i, nb, nq, 0 if u % 2 == 0 else 2)
                    if u + 2 < UB:
                        weights(b, i, nn, u + 2)
                    elif not last:
                        weights(b, i, nn + 1, u + 2 - UB)
                    if more and u % 2 == 0:
                        keep_block(b, i, nb, nq, 1)

            def filt_a(b, i, kk):
                act.wait_ge(f_ready, b * NC1 + i * 4 + (kk + 1))
                act.activation(fs[:, kk % 2, :], f_ps[0:AROWS, :], ACT.Identity, bias=bs_c[0:AROWS],
                               scale=STD_SPATIAL).then_inc(fs_done, 1)
                act.wait_ge(fs_done, b * NC1 + i * 4 + (kk + 1))
                act.activation(fsq, fs[:, kk % 2, :], ACT.Square).then_inc(fsq_done, 1)

            def filt_b(b, i, kk):
                act.wait_ge(var_ready, b * NC1 + i * 4 + (kk + 1))
                act.activation(fsd, var_ps[0:AROWS, :], ACT.Sqrt,
                               scale=1.0 / ((TAPS - 1) * STD_SPATIAL ** 2)).then_inc(fsd_done, 1)

            def filt_c(b, i, kk):
                act.wait_ge(fnorm_done, b * NC1 + i * 4 + (kk + 1))
                act.activation(sf_st[:, kk % 2, :], fnorm, ACT.Copy).then_inc(f_hi, 1)
                act.wait_ge(f_res, b * NC1 + i * 4 + (kk + 1))
                act.activation(sf_st[0:64, kk % 2, :], fres[0:64], ACT.Copy).then_inc(f_mid, 1)

            def lift(b, i, kk):
                act.wait_ge(sumb_done, b * (5 * NC1) + i * 20 + (kk * 5 + 5))
                if not (isinstance(i, int) and 4 * i + kk == 0):
                    act.wait_ge(y1_ready, b * NC1 + i * 4 + kk)
                act.activation(lifted, sumb, ACT.Relu, scale=-0.9).then_inc(lifted_done, 1)

            def l1_step(b, i, kk):
                last = isinstance(i, int) and 4 * i + kk == NC1 - 1
                if not last:
                    filt_a(b, i, kk + 1)
                    filt_b(b, i, kk + 1)
                    filt_c(b, i, kk + 1)
                lift(b, i, kk)

            with act.Fori(0, B) as b:
                for q in range(NQ):
                    relu(b, 0, 0, q)
                square(b, 0, 0)
                for g in range(3):
                    keep_block(b, 0, 0, 0, g)
                for u in range(2):
                    weights(b, 0, 0, u)
                for nn in range(4):
                    band_steps(b, 0, nn, False)
                with act.Fori(1, 3) as i:
                    for nn in range(4):
                        band_steps(b, i, nn, False)
                for nn in range(4):
                    band_steps(b, 3, nn, nn == 3)
                act.wait_ge(nvar_done, b + 1)
                act.activation(sd_c, var_c, ACT.Sqrt).then_inc(nsd_done, 1)
                act.wait_ge(ncoef_done, b + 1)
                for j in range(5):
                    rows = E[:, 2 + 16 * j:18 + 16 * j, 1:1 + W]
                    act.activation(rows, rows, ACT.Identity, bias=nmr_c, scale=rstd_c,
                                   accum_out=sums[:, j:j + 1]).then_inc(norm_act, 1)
                act.wait_ge(mlp1_ready, b + 1)
                act.activation(h12_c, small_ps[0:MID, 8:9], ACT.Relu, bias=mb1_c[0:MID],
                               scale=1.0 / NPIX).then_inc(h12_done, 1)
                filt_a(b, 0, 0)
                act.wait_ge(css_done, b + 1)
                act.activation(csd_c, css_c, ACT.Sqrt, scale=1.0 / (TAPS - 1)).then_inc(csd_done, 1)
                filt_b(b, 0, 0)
                filt_c(b, 0, 0)
                for kk in range(5):
                    l1_step(b, 0, kk)
                with act.Fori(1, 15) as i:
                    for kk in range(1, 5):
                        l1_step(b, i, kk)
                for kk in range(1, 5):
                    l1_step(b, 15, kk)

        @block.vector
        def _(dve):
            dve.wait_ge(const_in, 16 * N_CONST)
            gflat = g_neg[:, :, :].rearrange("p k o -> p (k o)")
            dve.tensor_tensor(gflat, graw_sb, gin_sb, ALU.mult).then_inc(setup_dve, 1)
            wv = ws_sb[:, :].rearrange("p (g k) -> p g k", g=3)[:, :, 0:2 * TAPS]\
                .rearrange("p g (s t) -> p g s t", t=TAPS)
            wm = wmean.rearrange("p (g s) -> p g s", g=3)
            dve.tensor_reduce(wm, wv, AX_X, ALU.add).then_inc(nd, 1)
            dve.wait_ge(setup_dve, 1)
            dve.scalar_tensor_tensor(gflat, gflat, -1.0, gout_sb, ALU.mult, ALU.add).then_inc(setup_dve, 1)
            dve.wait_ge(nd, 1)
            dve.tensor_scalar(wm, wm, -1.0 / TAPS, None, ALU.mult).then_inc(nd, 1)
            dve.wait_ge(nd, 2)
            dve.tensor_tensor(wv, wv, wm.unsqueeze(3).to_broadcast([128, 3, 2, TAPS]), ALU.add)\
               .then_inc(setup_dve, 1)
            dve.wait_ge(center_ready, 1)
            dve.tensor_scalar(bs_c[0:AROWS], small_ps[0:AROWS, 0:1], STD_SPATIAL, None, ALU.mult)\
               .then_inc(nd, 1)
            dve.wait_ge(setup_dve, 3)
            dve.wait_ge(nd, 3)

            def width_a(b, i, nn):
                dve.wait_ge(ks_ready, b * NBAND + i * 4 + (nn + 1))
                if not (isinstance(i, int) and 4 * i + nn == 0):
                    dve.wait_ge(a_split, b * NBAND + i * 4 + nn)
                dve.tensor_scalar(ka, ks_ps[0:AROWS, :], b2_c[0:AROWS], 0.0, ALU.add, ALU.max)\
                   .then_inc(k1_done, 1)
                dve.wait_ge(k1_done, b * NBAND + i * 4 + (nn + 1))
                dve.tensor_scalar(kb, ka, 20.0, 1.0, ALU.mult, ALU.add).then_inc(k2_done, 1)

            def width_b(b, i, nn):
                dve.wait_ge(ksq_done, b * NBAND + i * 4 + (nn + 1))
                dve.reciprocal(kb, ka).then_inc(a_ready, 1)

            def argument(b, i, nn, u):
                dve.wait_ge(abc_ready, b * 128 + i * 32 + (nn * 8 + u + 1))
                if not (isinstance(i, int) and 32 * i + 8 * nn + u < 2):
                    dve.wait_ge(bands_done, b * 128 + i * 32 + (nn * 8 + u - 1))
                a = abc_ps[u % 2][:, :].rearrange("p (t o) -> p t o", t=NT)
                dve.tensor_tensor(band[:, u % 2], g_neg[:, :, :].unsqueeze(1).to_broadcast([128, NT, 2, 128]),
                                  a.unsqueeze(2).to_broadcast([128, NT, 2, 128]), ALU.mult)\
                   .then_inc(arg_done, 1)

            def normalise(b, i, nn, u):
                s, q = u % 2, u // 2
                done = b * 128 + i * 32 + (nn * 8 + u + 1)
                lp = low_ps[u % 2][:, 0:65 * NT].rearrange("p (t c) -> p t c", c=65)
                dve.wait_ge(bands_done, done)
                dve.reciprocal(rsum[u % 2], lp[:, :, C]).then_inc(rsum_done, 1)
                dve.wait_ge(rsum_done, done)
                dve.tensor_tensor(low_t[:, q % 2, :, s, :], lp[:, :, 0:C],
                                  rsum[u % 2].unsqueeze(2).to_broadcast([128, NT, C]), ALU.mult)\
                   .then_inc(low_done, 1)

            def enhance(b, i, nn, q):
                dve.wait_ge(turn_ready, b * 64 + i * 16 + (nn * 4 + q + 1))
                src = turn_ps[:, :].rearrange("p (g r c) -> p g r c", g=8, r=BAND)
                parts = pieces8(nn % XSLOTS)
                c0 = COLS * q
                for j, (ring, row, n) in enumerate(parts):
                    res = xr[:, ring:ring + n, R0 + c0:R0 + c0 + COLS].rearrange("p r (g c) -> p g r c", c=8)
                    r0 = BAND * nn + row + 2
                    rows = slice(4 * BAND * i + r0, 4 * BAND * i + r0 + n) if isinstance(i, int) else \
                        bass.ds(i * (4 * BAND) + r0, n)
                    dst = E[:, rows, 1 + c0:1 + c0 + COLS].rearrange("p r (g c) -> p g r c", c=8)
                    op = dve.tensor_tensor(dst, src[:, :, row:row + n, :], res, ALU.add)
                op.then_inc(e_done, 1)
                dve.wait_ge(e_done, b * 64 + i * 16 + (nn * 4 + q + 1))
                r0 = BAND * nn + 2
                rows = slice(4 * BAND * i + r0, 4 * BAND * i + r0 + BAND) if isinstance(i, int) else \
                    bass.ds(i * (4 * BAND) + r0, BAND)
                at = slice(16 * i + 4 * nn + q, 16 * i + 4 * nn + q + 1) if isinstance(i, int) else \
                    bass.ds(i * 16 + (4 * nn + q), 1)
                dve.bn_stats(stats[:, at, :].rearrange("p a s -> p (a s)"), E[:, rows, 1 + c0:1 + c0 + COLS])\
                   .then_inc(stats_done, 1)

            def band_steps(b, i, nn, last):
                for u in range(UB):
                    if not last and u == 3:
                        width_a(b, i, nn + 1)
                    if not last and u == 4:
                        width_b(b, i, nn + 1)
                    normalise(b, i, nn, u)
                    if u + 2 < UB:
                        argument(b, i, nn, u + 2)
                    elif not last:
                        argument(b, i, nn + 1, u + 2 - UB)
                    if u % 2:
                        enhance(b, i, nn, u // 2)

            def reciprocal(b, i, kk):
                n = b * NC1 + i * 4 + (kk + 1)
                dve.wait_ge(fsd_done, n)
                dve.tensor_scalar(fsd, fsd, EPS1, None, ALU.add).then_inc(feps_done, 1)
                dve.wait_ge(feps_done, n)
                dve.reciprocal(frec, fsd).then_inc(frec_done, 1)

            def tap(b, i, kk, t):
                k0 = b * (NC1 * TAPS) + i * (4 * TAPS) + kk * TAPS
                dve.wait_ge(spread_ready, k0 + (t + 1))
                if t == 4 and not (isinstance(i, int) and 4 * i + kk == 0):
                    dve.wait_ge(y1_ready, b * NC1 + i * 4 + kk)
                if t >= 7:
                    dve.wait_ge(sumb_done, b * (5 * NC1) + i * 20 + (5 * kk + t - 6))
                dst = prod[:, t, :] if t < 4 else sumb if t == 4 else tmp[:, t % 2, :]
                dy, dx = t // 3, t % 3
                r0 = 2 * kk + dy
                rows = slice(8 * i + r0, 8 * i + r0 + 2) if isinstance(i, int) else bass.ds(i * 8 + r0, 2)
                dve.scalar_tensor_tensor(dst.rearrange("p (r w) -> p r w", w=W),
                                         spread_ps[t % 3][:, :].rearrange("p (r w) -> p r w", w=W),
                                         cf[:, t:t + 1], E[:, rows, dx:dx + W], ALU.mult, ALU.mult)\
                   .then_inc(prod_done, 1)

            def add(b, i, kk, n, src, t):
                dve.wait_ge(prod_done, b * (NC1 * TAPS) + i * (4 * TAPS) + (kk * TAPS + t + 1))
                if n:
                    dve.wait_ge(sumb_done, b * (5 * NC1) + i * 20 + (5 * kk + n))
                dve.tensor_tensor(sumb, sumb, src, ALU.add).then_inc(sumb_done, 1)

            def final(b, i, kk):
                dve.wait_ge(conv_ready, b * NO1 + i * 4 + kk)
                if not (isinstance(i, int) and 4 * i + kk < 3):
                    dve.wait_ge(stored[(kk - 1) % 2], b * (16 * NO1) + i * 64 + 32 * ((kk - 1) // 2))
                r0 = 2 * kk
                rows = slice(8 * i + r0, 8 * i + r0 + 2) if isinstance(i, int) else bass.ds(i * 8 + r0, 2)
                dve.scalar_tensor_tensor(stage[:, (kk - 1) % 2, :].rearrange("p (r w) -> p r w", w=W),
                                         conv_ps[kk % 2][:, :].rearrange("p (r w) -> p r w", w=W),
                                         bconv_c, E[:, rows, 1:1 + W], ALU.add, ALU.add)\
                   .then_inc(out_done, 1)

            def l1_step(b, i, kk):
                k = 4 * i + kk if isinstance(i, int) else None
                for t in range(TAPS):
                    tap(b, i, kk, t)
                    if t == 1 and (k is None or k >= 3):
                        final(b, i, kk - 2)
                    if t == 4 and k != NC1 - 1:
                        reciprocal(b, i, kk + 1)
                    if t == 6:
                        add(b, i, kk, 0, tmp[:, 1, :], 5)
                    if t == 7:
                        add(b, i, kk, 1, tmp[:, 0, :], 6)
                add(b, i, kk, 2, tmp[:, 1, :], 7)
                add(b, i, kk, 3, tmp[:, 0, :], 8)
                dve.wait_ge(suma_done, b * (3 * NC1) + i * 12 + (3 * kk + 3))
                add(b, i, kk, 4, suma, 8)

            with dve.Fori(0, B) as b:
                width_a(b, 0, 0)
                width_b(b, 0, 0)
                for u in range(2):
                    argument(b, 0, 0, u)
                for nn in range(4):
                    band_steps(b, 0, nn, False)
                with dve.Fori(1, 3) as i:
                    for nn in range(4):
                        band_steps(b, i, nn, False)
                for nn in range(4):
                    band_steps(b, 3, nn, nn == 3)
                n0 = b * 5 + 3
                hold(dve, (stats_done, b * 64 + 64))
                dve.bn_aggr(mv, stats[:, :, :].rearrange("p a s -> p (a s)")).then_inc(mv_done, 1)
                dve.wait_ge(pair_ready, b + 1)
                dve.tensor_copy(pv, small_ps[:, 0:4]).then_inc(nd, 1)
                dve.wait_ge(nd, n0 + 1)
                dve.tensor_tensor(var_c, pv[:, 2:3], pv[:, 2:3], ALU.mult).then_inc(nd, 1)
                dve.wait_ge(nd, n0 + 2)
                dve.tensor_tensor(var_c, var_c, pv[:, 1:2], ALU.add).then_inc(nd, 1)
                dve.wait_ge(nd, n0 + 3)
                dve.tensor_scalar(var_c, var_c, 1e-5, None, ALU.add).then_inc(nvar_done, 1)
                dve.wait_ge(nsd_done, b + 1)
                dve.reciprocal(rstd_c, sd_c).then_inc(nd, 1)
                dve.wait_ge(nd, n0 + 4)
                dve.tensor_scalar(nmr_c, pv[:, 0:1], -1.0, rstd_c, ALU.mult, ALU.mult).then_inc(ncoef_done, 1)
                dve.wait_ge(ncoef_done, b + 1)
                for j in range(5, 8):
                    rows = E[:, 2 + 16 * j:18 + 16 * j, 1:1 + W]
                    dve.tensor_scalar(rows, rows, rstd_c, nmr_c, ALU.mult, ALU.add).then_inc(norm_dve, 1)
                for j in range(5, 8):
                    dve.wait_ge(norm_dve, 3 * b + (j - 4))
                    dve.tensor_reduce(sums[:, j:j + 1], E[:, 2 + 16 * j:18 + 16 * j, 1:1 + W],
                                      mybir.AxisListType.XY, ALU.add).then_inc(sums_dve, 1)
                dve.wait_ge(norm_act, 5 * b + 5)
                dve.wait_ge(sums_dve, 3 * b + 3)
                dve.tensor_reduce(pooled_c, sums, AX_X, ALU.add).then_inc(pooled_done, 1)
                c0 = b * 7
                dve.wait_ge(mlp2_ready, b + 1)
                dve.tensor_tensor(cc, small_ps[:, 16:16 + TAPS], mb2_sb, ALU.add).then_inc(cf_steps, 1)
                dve.wait_ge(cf_steps, c0 + 1)
                dve.tensor_reduce(cm_c, cc, AX_X, ALU.add).then_inc(cf_steps, 1)
                dve.wait_ge(cf_steps, c0 + 2)
                dve.tensor_scalar(cm_c, cm_c, -1.0 / TAPS, None, ALU.mult).then_inc(cf_steps, 1)
                dve.wait_ge(cf_steps, c0 + 3)
                dve.tensor_scalar(cc, cc, cm_c, None, ALU.add).then_inc(cf_steps, 1)
                dve.wait_ge(cf_steps, c0 + 4)
                dve.tensor_tensor(cf, cc, cc, ALU.mult).then_inc(cf_steps, 1)
                dve.wait_ge(cf_steps, c0 + 5)
                dve.tensor_reduce(css_c, cf, AX_X, ALU.add).then_inc(css_done, 1)
                dve.wait_ge(csd_done, b + 1)
                dve.tensor_scalar(csd_c, csd_c, EPS1, None, ALU.add).then_inc(cf_steps, 1)
                dve.wait_ge(cf_steps, c0 + 6)
                dve.reciprocal(cr_c, csd_c).then_inc(cf_steps, 1)
                dve.wait_ge(cf_steps, c0 + 7)
                dve.scalar_tensor_tensor(cf, cc, cr_c, std_sb[:, 0:TAPS], ALU.mult, ALU.mult)\
                   .then_inc(nd, 1)
                reciprocal(b, 0, 0)
                dve.wait_ge(nd, n0 + 5)
                for kk in range(5):
                    l1_step(b, 0, kk)
                with dve.Fori(1, 15) as i:
                    for kk in range(1, 5):
                        l1_step(b, i, kk)
                for kk in range(1, 5):
                    l1_step(b, 15, kk)
                final(b, 15, 3)
                final(b, 15, 4)

        @block.gpsimd
        def _(pool):
            pool.wait_ge(setup_dve, 3)
            pool.wait_ge(center_ready, 1)
            pool.memset(E[:, 0:2, :], 0.0).then_inc(setup_pool, 1)
            pool.memset(E[:, ER - 2:ER, :], 0.0).then_inc(setup_pool, 1)
            pool.memset(E[:, 2:ER - 2, 0:1], 0.0).then_inc(setup_pool, 1)
            pool.memset(E[:, 2:ER - 2, EW - 1:EW], 0.0).then_inc(setup_pool, 1)

            def split_a(b, i, nn):
                n = b * NBAND + i * 4 + (nn + 1)
                st = a_st[:, nn % 2, :]
                hold(pool, (a_ready, n))
                pool.tensor_copy(st, kb).then_inc(a_hi, 1)
                pool.wait_ge(a_hi, n)
                pool.tensor_tensor(ka[0:64], kb[0:64], st[0:64], ALU.subtract).then_inc(a_res, 1)
                hold(pool, (a_res, n))
                pool.tensor_copy(st[0:64], ka[0:64]).then_inc(a_mid, 1)
                pool.wait_ge(a_mid, n)
                pool.tensor_tensor(st[0:32], ka[0:32], st[0:32], ALU.subtract).then_inc(a_split, 1)

            def pack(b, i, nn, q):
                for g in range(3):
                    first = isinstance(i, int) and 4 * i + nn == 0 and q == 0
                    if not first:
                        hold(pool, (xt_ready, b * 192 + i * 48 + (nn * 12 + q * 3 + g - 2)))
                    c0 = COLS * q + 24 * g
                    dst = xb[:, g].rearrange("p j (r c) -> p j r c", c=8)
                    lo = BAND * (nn % XSLOTS)
                    parts = [(lo, 0, 16)] if nn % XSLOTS < XSLOTS - 1 else [(lo, 0, 8), (0, 8, 8)]
                    for ring, row, n in parts:
                        src = xr[:, ring:ring + n, c0:c0 + 24].rearrange("p r (j c) -> p j r c", c=8)
                        op = pool.tensor_copy(dst[:, :, row:row + n, :], src)
                    op.then_inc(xb_done, 1)

            def band_steps(b, i, nn, last):
                for q in range(NQ):
                    nq, nb = (q + 1, nn) if q + 1 < NQ else (0, nn + 1)
                    if nq == 0 and not last:
                        split_a(b, i, nn + 1)
                        pool.wait_ge(*x_loaded(b, i, nb + 1))
                        if isinstance(i, int) and 4 * i + nb + 1 == NBAND:
                            pool.wait_ge(pad16_done, b + 1)
                    if not (last and nq == 0):
                        pack(b, i, nb, nq)
                    if isinstance(i, int) and 4 * i + nn == 13 and q == 0:
                        hold(pool, (e_done, b * 64 + 13 * NQ), (xb_done, b * 192 + (13 * 12 + 6)))
                        pool.memset(xr[C:2 * C, R0:BAND, R0:R0 + W], 0.0).then_inc(pad16_done, 1)
                        pool.wait_ge(pad16_done, b + 1)

            def split_f(b, i, kk):
                n = b * NC1 + i * 4 + (kk + 1)
                st = sf_st[:, kk % 2, :]
                pool.wait_ge(frec_done, n)
                pool.tensor_tensor(fnorm, fs[:, kk % 2, :], frec, ALU.mult).then_inc(fnorm_done, 1)
                pool.wait_ge(f_hi, n)
                pool.tensor_tensor(fres[0:64], fnorm[0:64], st[0:64], ALU.subtract).then_inc(f_res, 1)
                pool.wait_ge(f_mid, n)
                pool.tensor_tensor(st[0:32], fres[0:32], st[0:32], ALU.subtract).then_inc(f_split, 1)

            def sum_a(b, i, kk):
                p0 = b * (NC1 * TAPS) + i * (4 * TAPS) + kk * TAPS
                s0 = b * (3 * NC1) + i * 12 + 3 * kk
                pool.wait_ge(prod_done, p0 + 2)
                if not (isinstance(i, int) and 4 * i + kk == 0):
                    pool.wait_ge(sumb_done, b * (5 * NC1) + i * 20 + 5 * kk)
                pool.tensor_tensor(suma, prod[:, 0, :], prod[:, 1, :], ALU.add).then_inc(suma_done, 1)
                for t in (2, 3):
                    pool.wait_ge(prod_done, p0 + (t + 1))
                    pool.wait_ge(suma_done, s0 + (t - 1))
                    pool.tensor_tensor(suma, suma, prod[:, t, :], ALU.add).then_inc(suma_done, 1)

            def leaky(b, i, kk):
                pool.wait_ge(lifted_done, b * NC1 + i * 4 + (kk + 1))
                r = 2 * (kk % 4)
                pool.tensor_tensor(y1[:, r:r + 2, 1:1 + W], sumb.rearrange("p (r w) -> p r w", w=W),
                                   lifted.rearrange("p (r w) -> p r w", w=W), ALU.add).then_inc(y1_ready, 1)

            def l1_step(b, i, kk):
                sum_a(b, i, kk)
                if not (isinstance(i, int) and 4 * i + kk == NC1 - 1):
                    split_f(b, i, kk + 1)
                leaky(b, i, kk)

            with pool.Fori(0, B) as b:
                hold(pool, (ring_free, b + 1))
                pool.memset(xr[:, :, 0:R0], 0.0).then_inc(pads_done, 1)
                pool.memset(xr[:, :, R0 + W:XW], 0.0).then_inc(pads_done, 1)
                pool.memset(xr[0:C, 0:R0, R0:R0 + W], 0.0).then_inc(pads_done, 1)
                pool.memset(xt[:, :, :, :, C:C + 1], 1.0).then_inc(setup_pool, 1)
                hold(pool, (pads_done, 3 * b + 3), x_loaded(b, 0, 0), x_loaded(b, 0, 1))
                pack(b, 0, 0, 0)
                split_a(b, 0, 0)
                for nn in range(4):
                    band_steps(b, 0, nn, False)
                with pool.Fori(1, 3) as i:
                    for nn in range(4):
                        band_steps(b, i, nn, False)
                for nn in range(4):
                    band_steps(b, 3, nn, nn == 3)
                hold(pool, (e_done, b * 64 + 64))
                pool.memset(y1[:, :, 0:1], 0.0).then_inc(y1_edge, 1)
                pool.memset(y1[:, :, EW - 1:EW], 0.0).then_inc(y1_edge, 1)
                split_f(b, 0, 0)
                sum_a(b, 0, 0)
                split_f(b, 0, 1)
                leaky(b, 0, 0)
                hold(pool, (y1_ready, b * NC1 + 1))
                pool.memset(y1[0:C, 0:1, 1:1 + W], 0.0).then_inc(y1_edge, 1)
                for kk in range(1, 5):
                    l1_step(b, 0, kk)
                with pool.Fori(1, 15) as i:
                    for kk in range(1, 5):
                        l1_step(b, i, kk)
                for kk in range(1, 5):
                    l1_step(b, 15, kk)
                hold(pool, (y1_ready, b * NC1 + NC1), (suma_done, b * (3 * NC1) + 3 * NC1))
                pool.memset(y1[C:2 * C, 1:2, 1:1 + W], 0.0).then_inc(y1_edge, 1)


def _window_index():
    p, o = np.arange(128), np.arange(128)
    xh, r, c = o // 64, (o // 8) % 8, o % 8
    ir, ic = p // 8, p % 8
    u = ir[:, None] - r[None, :]
    index = np.zeros((128, 2, 128), np.int64)
    inside = np.zeros((128, 2, 128), bool)
    for kind in range(2):
        left = (xh == 1) if kind == 0 else (xh == 0)
        v = (ic[:, None] - c[None, :]) + np.where(left, 0, 8)[None, :]
        ok = (u >= 0) & (u < K0) & (v >= 0) & (v < K0)
        inside[:, kind] = ok
        index[:, kind] = np.where(ok, u * K0 + v, 0)
    return index.reshape(128, 256), inside.reshape(128, 256)


def _layout(i):
    f = np.float32
    index, inside = _window_index()
    d = {"x": np.asarray(i["x"])}
    d["graw"] = np.asarray(i["L0_conv_gauss_kernel"]).reshape(-1)[index]
    d["gin"] = inside.astype(f)
    d["gout"] = np.where(inside, f(0), f(FAR)).astype(f)
    sel = np.zeros((AROWS, UB, 128), np.uint16)
    for u in range(UB):
        for g in range(3):
            sel[32 * g + u, u, :] = BF16_ONE
    d["sel_a"] = sel
    d["ident"] = np.eye(128, dtype=f)
    w1 = np.zeros((128, 2 * HID), f)
    w2 = np.zeros((2 * HID, NQ, AROWS), f)
    for s in range(2):
        w1[C * s:C * s + C, HID * s:HID * s + HID] = np.asarray(i["L0_conv_w1"])
        for q in range(NQ):
            for g in range(3):
                w2[HID * s:HID * s + HID, q, 32 * g + 2 * q + s] = np.asarray(i["L0_conv_w2"])[:, 0]
    d["w1"], d["w2"] = w1, w2
    pair = np.zeros((128, 2, 128), f)
    for m in range(128):
        pair[m, 0, m] = pair[(m + 64) % 128, 0, m] = 0.5
        pair[m, 1, m], pair[(m + 64) % 128, 1, m] = 0.5, -0.5
    d["pair"] = pair
    ws = np.zeros((128, AROWS), f)
    bs = np.zeros((AROWS, 1), f)
    center = np.zeros((AROWS, AROWS), f)
    varsum = np.zeros((AROWS, AROWS), f)
    varsum[0:TAPS, :] = 1
    sel_sf = np.zeros((AROWS, TAPS, 128), np.uint16)
    for g in range(3):
        for s in range(2):
            r = slice(32 * g + TAPS * s, 32 * g + TAPS * s + TAPS)
            ws[C * s:C * s + C, r] = np.asarray(i["L1_conv_Ws"]).T
            bs[r, 0] = np.asarray(i["L1_conv_bs"])
            center[r, r] = np.eye(TAPS, dtype=f) - f(1.0 / TAPS)
            varsum[:, r] = 0
            varsum[r, r] = 1
            for t in range(TAPS):
                sel_sf[32 * g + TAPS * s + t, t, C * s:C * s + C] = BF16_ONE
    d["ws"], d["bs"], d["center"], d["varsum"], d["sel_sf"] = ws, bs, center, varsum, sel_sf
    wc = np.zeros((128, TAPS, 128), f)
    for s in range(2):
        wc[C * s:C * s + C, :, C * s:C * s + C] = \
            np.asarray(i["L1_conv_Wc"]).transpose(1, 2, 3, 0).reshape(C, TAPS, C)
    d["wconv"] = wc
    small = np.zeros((128, 5), f)
    small[0:HID, 0] = small[HID:2 * HID, 0] = np.asarray(i["L0_conv_b1"])
    small[:, 1] = np.asarray(i["L0_conv_b2"])[0]
    small[0:C, 3] = small[C:, 3] = np.asarray(i["L1_conv_bc"])
    small[0:MID, 4] = np.asarray(i["L1_conv_b1"])
    d["small"] = small
    d["mlp1"] = np.concatenate([np.asarray(i["L1_conv_W1"]).T] * 2, axis=0)
    w2t = np.asarray(i["L1_conv_W2"]).reshape(C, TAPS, MID).transpose(2, 1, 0)
    d["mlp2"] = np.concatenate([w2t, w2t], axis=2)
    d["mb2"] = np.concatenate([np.asarray(i["L1_conv_b2"]).reshape(C, TAPS)] * 2, axis=0)
    d["stdch"] = np.concatenate([np.asarray(i["L1_conv_std_ch"]).reshape(C, TAPS)] * 2, axis=0)
    return d


_ORDER = ["x", "graw", "gin", "gout", "sel_a", "ident", "w1", "w2", "pair", "ws", "bs", "center",
          "varsum", "sel_sf", "wconv", "small", "mlp1", "mlp2", "mb2", "stdch"]


def kernel(**inputs):
    import concourse.bacc as _bacc
    from concourse.bass_utils import run_bass_kernel_spmd as _run

    nc = _bacc.Bacc("TRN2", target_bir_lowering=False, num_devices=1)
    laid = _layout(inputs)
    arrays, args = {}, {}
    for name in _ORDER:
        a = np.ascontiguousarray(laid[name])
        arrays[f"in_{name}"] = a
        args[name] = nc.dram_tensor(f"in_{name}", a.shape, mybir.dt.from_np(a.dtype), kind="ExternalInput").ap()
    o = nc.dram_tensor("out_0", (B, C, H, W), F32, kind="ExternalOutput").ap()
    build(nc, out=o, **args)
    r = _run(nc, [arrays], core_ids=[0])
    return r.results[0]["out_0"]
```

```python
from contextlib import ExitStack

import numpy as np

import concourse.bass as bass
from concourse import mybir

ALU = mybir.AluOpType
ACT = mybir.ActivationFunctionType
F32 = mybir.dt.float32
BF16 = mybir.dt.bfloat16
AX_X = mybir.AxisListType.X

B, C, H, W = 8, 64, 256, 256
HID, MID = 32, 12
K0, R0 = 9, 4
ROWS = H // 2
BAND = 8
NBAND = ROWS // BAND
COLS = 64
NQ = W // COLS
NT = COLS // 16
NG = 2 * NT
UB = 2 * NQ
NV = 2 * NT * NQ
FR = 18
XW = W + 2 * R0
ER, EW = ROWS + 4, W + 2
BLK = 2 * NT + 1
TAPS = 9
NC1 = ROWS // 2 + 1
NO1 = ROWS // 2
NPIX = H * W
STD_SPATIAL = 1.4142135623730951 / 3
EPS1 = 1e-10
NPOOL = 5
NDVE = TAPS - NPOOL
FAR = -1.0e30
BF16_ONE = 0x3F80
AROWS = 96
XSLOTS = 4


def build(nc, x, graw, gin, gout, g81, sel_a, ident, ident16, w1, w2, pair, ws, bs, center,
          sel_sf, wconv, small, mlp1, mlp2, mb2, stdch, out):
    with ExitStack() as ctx:
        def sb(name, shape, dt=F32):
            return ctx.enter_context(nc.sbuf_tensor(name, shape, dt))

        def sem(name):
            return ctx.enter_context(nc.semaphore(name))

        E = sb("image", [128, ER, EW])
        g_neg = sb("g_neg", [128, 2, 64])
        g81_neg = sb("g81_neg", [128, K0 * K0])
        sel_a_sb = sb("sel_a_sb", [AROWS, NV], BF16)
        ident_sb = sb("ident_sb", [128, 128])
        ident16_sb = sb("ident16_sb", [128, 128], BF16)
        w1_sb = sb("w1_sb", [128, 2 * HID])
        w2_sb = sb("w2_sb", [2 * HID, 2])
        ws_sb = sb("ws_sb", [128, FR])
        stats = sb("stats", [128, NBAND * NQ, 6])
        cols = sb("cols", [128, 64])
        b1_c, b2_c, bs_c, bconv_c, mb1_c = (cols[:, i:i + 1] for i in range(5))
        mv = cols[:, 6:8]
        pv = cols[:, 8:12]
        var_c, sd_c, rstd_c, nmr_c = (cols[:, i:i + 1] for i in range(12, 16))
        sums = cols[:, 16:24]
        pooled_c, h12_c = cols[:, 24:25], cols[0:MID, 25:26]
        cf = cols[:, 26:35]
        cm_c, css_c, csd_c, cr_c = (cols[:, i:i + 1] for i in range(35, 39))
        wmean = cols[:, 48:50]
        cc = cols[:, 54:63]

        xreg = sb("xreg", [128, XSLOTS * BAND * XW])
        work = sb("work", [128, 8192])

        def carve(region, start, n):
            assert start + n <= region.shape[1]
            return region[:, start:start + n], start + n

        xr = xreg[:, :].rearrange("p (r w) -> p r w", w=XW)
        at = 0
        xt_f, at = carve(work, at, 2 * BLK * 128)
        xt = xt_f.rearrange("p (n j s c) -> p n j s c", n=2, j=BLK, s=2)
        xb_f, at = carve(work, at, 3 * 384)
        xb = xb_f.rearrange("p (g j o) -> p g j o", g=3, j=3)
        h_f, at = carve(work, at, 512)
        h_sb = h_f[0:2 * HID, :]
        band_f, at = carve(work, at, 2 * 1024)
        band = band_f.rearrange("p (n g k o) -> p n g k o", n=2, g=NG, k=2)
        rs_sb, at = carve(work, at, 512)
        blur_sb, at = carve(work, at, 512)
        as_f, at = carve(work, at, 2 * 2 * 64)
        a_st = as_f[0:AROWS, :].bitcast(BF16).rearrange("p (n k o) -> p n k o", n=2, k=2)
        sp_f, at = carve(work, at, 96)
        a_parts = sp_f.bitcast(BF16).rearrange("p (k g v) -> p k g v", k=2, g=3)
        pix_f, at = carve(work, at, 6 * NV)
        ka, kb, a_pix, s_pix, r_pix, res_pix = (pix_f[:, NV * j:NV * j + NV] for j in range(6))
        junk_f, at = carve(work, at, 4 * K0 * K0)
        junk = junk_f.rearrange("p (n w) -> p n w", n=4)
        graw_sb = work[:, 0:128]
        gin_sb = work[:, 128:256]
        gout_sb = work[:, 256:384]
        center_sb = work[0:FR, 1536:1536 + FR]
        bs_raw = work[0:FR, 1700:1701]

        at = 0
        y1_f, at = carve(xreg, at, 8 * EW)
        y1 = y1_f.rearrange("p (r w) -> p r w", w=EW)
        p_f, at = carve(xreg, at, NPOOL * 512)
        prod = p_f.rearrange("p (n f) -> p n f", n=NPOOL)
        suma, at = carve(xreg, at, 512)
        sumb, at = carve(xreg, at, 512)
        tmp_f, at = carve(xreg, at, 1024)
        tmp = tmp_f.rearrange("p (n f) -> p n f", n=2)
        sf_f, at = carve(xreg, at, TAPS * 64)
        sel_sf_sb = sf_f[0:AROWS, :].bitcast(BF16).rearrange("p (t m) -> p t m", t=TAPS)
        stage_f, at = carve(xreg, at, 1024)
        stage = stage_f.rearrange("p (n f) -> p n f", n=2)
        at = 0
        wconv_f, at = carve(work, at, TAPS * 128)
        wconv_sb = wconv_f.rearrange("p (t m) -> p t m", t=TAPS)
        mlp2_f, at = carve(work, at, TAPS * 128)
        mlp2_sb = mlp2_f[0:MID, :].rearrange("p (t m) -> p t m", t=TAPS)
        pair_f, at = carve(work, at, 256)
        pair_sb = pair_f.rearrange("p (k m) -> p k m", k=2)
        mlp1_sb, at = carve(work, at, MID)
        mb2_sb, at = carve(work, at, TAPS)
        std_sb, at = carve(work, at, TAPS + 1)
        ss_f, at = carve(work, at, 2 * 256)
        sf_st = ss_f[0:AROWS, :].bitcast(BF16).rearrange("p (n f) -> p n f", n=2)
        fs_f, at = carve(work, at, 512)
        fs = fs_f[0:FR, :]
        lifted, at = carve(work, at, 512)
        fx_f, at = carve(work, at, 2 * 72)
        fx = fx_f.rearrange("p (n v t) -> p n v t", n=2, t=TAPS)
        fq_f, at = carve(work, at, 3 * 72)
        fq, fn, fres = (fq_f[:, 72 * j:72 * j + 72] for j in range(3))
        fsum, at = carve(work, at, 8)
        fsd_f, at = carve(work, at, 16)
        fsd = fsd_f.rearrange("p (n v) -> p n v", n=2)
        frec, at = carve(work, at, 8)
        fp_f, at = carve(work, at, 192)
        f_parts = fp_f.bitcast(BF16).rearrange("p (j g v) -> p j g v", j=4, g=3)

        banks = [ctx.enter_context(nc.psum_tensor(f"bank{i}", [128, 512], F32)) for i in range(8)]
        h_ps, pix_ps, xt_ps, low_ps, rs_ps = banks[0], banks[1], banks[2], banks[5:7], banks[7]
        abc_ps = banks[3:5]
        k_ps = pix_ps[:, 0:NV]
        turned_a = [ps[:, 0:64].bitcast(BF16)[0:AROWS] for ps in (h_ps, rs_ps)]
        spread_ps = [banks[0], banks[3], banks[4]]
        f_ps, conv_ps, small_ps = banks[1], banks[5:7], banks[7]
        fx_ps = banks[2][:, 0:72]
        fst_ps = banks[2][:, 128:384].bitcast(BF16)[0:AROWS]

        const_in = sem("const_in")
        setup_dve = sem("setup_dve")
        setup_pool = sem("setup_pool")
        center_ready = sem("center_ready")
        x_in = [sem(f"x_in{i}") for i in range(XSLOTS)]
        ring_free = sem("ring_free")
        pads_done = sem("pads_done")
        pad16_done = sem("pad16_done")
        h_ready, h_done = sem("h_ready"), sem("h_done")
        ks_ready, k1_done, k2_done, ksq_done, a_ready = (
            sem(n) for n in ("ks_ready", "k1_done", "k2_done", "ksq_done", "a_ready"))
        s_ready, r_ready = sem("s_ready"), sem("r_ready")
        hi_done, res_done, mid_done = ([sem(f"{n}{k}") for k in range(2)] for n in ("hi_done", "res_done", "mid_done"))
        parts_done, parts_turned, stack_done = (
            [sem(f"{n}{k}") for k in range(2)] for n in ("parts_done", "parts_turned", "stack_done"))
        abc_ready, arg_done, exp_done, bands_done = (
            sem(n) for n in ("abc_ready", "arg_done", "exp_done", "bands_done"))
        rs_ready, rs_done, blur_done, e_done = (
            sem(n) for n in ("rs_ready", "rs_done", "blur_done", "e_done"))
        xb_done, xt_ready, xt_done = sem("xb_done"), sem("xt_ready"), sem("xt_done")
        stats_done, mv_done, pair_ready, nd = (
            sem(n) for n in ("stats_done", "mv_done", "pair_ready", "norm_steps"))
        nvar_done, nsd_done, ncoef_done = sem("nvar_done"), sem("nsd_done"), sem("ncoef_done")
        norm_act, norm_dve, sums_dve = sem("norm_act"), sem("norm_dve"), sem("sums_dve")
        pooled_done, mlp1_ready, h12_done, mlp2_ready = (
            sem(n) for n in ("pooled_done", "mlp1_ready", "h12_done", "mlp2_ready"))
        cf_steps, css_done, csd_done = sem("cf_steps"), sem("css_done"), sem("csd_done")
        fpad_done = sem("fpad_done")
        halo_in, l1_const = sem("halo_in"), sem("l1_const")
        f_ready, fs_done, fx_ready, fx_done, fq_done, fsum_done, fsd_done = (
            sem(n) for n in ("f_ready", "fs_done", "fx_ready", "fx_done", "fq_done", "fsum_done", "fsd_done"))
        feps_done, frec_done, fnorm_done, f_hi, f_res, f_mid, f_parts_done, f_turned, f_split = (
            sem(n) for n in ("feps_done", "frec_done", "fnorm_done", "f_hi", "f_res", "f_mid",
                             "f_parts_done", "f_turned", "f_split"))
        spread_ready, prod_done, suma_done, sumb_done = (
            sem(n) for n in ("spread_ready", "prod_done", "suma_done", "sumb_done"))
        y1_ready, y1_edge, conv_ready, out_done = (
            sem(n) for n in ("y1_ready", "y1_edge", "conv_ready", "out_done"))
        lifted_done = sem("lifted_done")
        stored = [sem("stored0"), sem("stored1")]

        N_CONST = 13
        block = ctx.enter_context(nc.Block())

        def x_loaded(b, i, kk):
            slot = kk % XSLOTS
            per_image = 32 * (5 if slot == 0 else 4)
            return x_in[slot], b * per_image + i * 32 + 32 * (kk // XSLOTS + 1)

        def pieces8(nn):
            first = BAND * nn + R0
            if nn < XSLOTS - 1:
                return [(first, 0, BAND)]
            return [(first, 0, R0), (0, R0, R0)]

        def hold(eng, *waits):
            values = [(which, eng.to_reg(value)) for which, value in waits]
            eng.wait_ge(const_in, 16 * N_CONST)
            for which, value in values:
                eng.wait_ge(which, value)

        @block.sync
        def _(sp):
            for dst, src in ((graw_sb, graw), (gin_sb, gin), (gout_sb, gout), (g81_neg[:, :], g81),
                             (sel_a_sb[:, :].bitcast(mybir.dt.uint16), sel_a), (ident_sb[:, :], ident),
                             (ident16_sb[:, :].bitcast(mybir.dt.uint16), ident16), (w1_sb[:, :], w1),
                             (w2_sb[:, :], w2), (ws_sb[:, :], ws), (center_sb, center), (bs_raw, bs),
                             (cols[:, 0:5], small)):
                sp.dma_start(dst, src).then_inc(const_in, 16)

            def load_group(b, i, kk):
                static = isinstance(i, int)
                k = XSLOTS * i + kk
                slot = kk % XSLOTS
                img = x[bass.ds(b, 1)].rearrange("a c r w -> (a c) r w")
                for s in range(2):
                    lo, n, at = s * ROWS + BAND * k - R0, BAND, BAND * slot
                    if static and k == 0 and s == 0:
                        lo, n, at = 0, BAND - R0, at + R0
                    if static and k == NBAND and s == 1:
                        n = BAND - R0
                    src = img[:, lo:lo + n, :] if static else img[:, bass.ds(lo, n), :]
                    sp.dma_start(xr[C * s:C * s + C, at:at + n, R0:R0 + W], src).then_inc(x_in[slot], 16)

            with sp.Fori(0, B) as b:
                sp.nop().then_inc(ring_free, 1)
                for k in range(4):
                    load_group(b, 0, k)

                def refill(i, kk):
                    hold(sp, (e_done, b * (NBAND * NQ) + i * (4 * NQ) + (kk - 4 + 1) * NQ))
                    load_group(b, i, kk)

                with sp.Fori(1, 4) as i:
                    for kk in range(4):
                        refill(i, kk)
                refill(4, 0)

                hold(sp, (e_done, (b + 1) * (NBAND * NQ)))
                for dst, src in ((pair_sb, pair), (wconv_sb, wconv), (mlp1_sb, mlp1), (mlp2_sb, mlp2), (mb2_sb, mb2),
                                 (std_sb[:, 0:TAPS], stdch), (sel_sf_sb.bitcast(mybir.dt.uint16), sel_sf)):
                    sp.dma_start(dst, src).then_inc(l1_const, 16)
                hold(sp, (norm_act, 5 * b + 5), (norm_dve, 3 * b + 3))
                sp.dma_start(E[0:C, ROWS + 2:ROWS + 4, 1:1 + W], E[C:2 * C, 2:4, 1:1 + W]).then_inc(halo_in, 16)
                sp.dma_start(E[C:2 * C, 0:2, 1:1 + W], E[0:C, ROWS:ROWS + 2, 1:1 + W]).then_inc(halo_in, 16)

                with sp.Fori(0, NO1 // 2) as i:
                    for j in range(2):
                        hold(sp, (out_done, b * NO1 + 2 * i + (1 + j)))
                        dst = out[bass.ds(b, 1)].rearrange("a c r w -> (a c) r w")
                        for s in range(2):
                            src = stage[C * s:C * s + C, j, :].rearrange("p (r w) -> p r w", w=W)
                            sp.dma_start(dst[:, bass.ds(i * 4 + (s * ROWS + 2 * j), 2), :], src)\
                              .then_inc(stored[j], 16)
                hold(sp, *((stored[j], (b + 1) * (32 * NO1 // 2)) for j in range(2)))

        @block.tensor
        def _(pe):
            pe.wait_ge(const_in, 16 * N_CONST)
            pe.matmul(small_ps[0:FR, 0:1], center_sb, bs_raw, start=True, stop=True)\
              .then_inc(center_ready, 1)
            pe.wait_ge(setup_dve, 4)

            def hidden(b, i, nn, q):
                if not (isinstance(i, int) and 16 * i + 4 * nn + q == 0):
                    pe.wait_ge(h_done, b * 64 + i * 16 + (nn * 4 + q))
                dst = h_ps[0:2 * HID, :].rearrange("p (g r c) -> p g r c", g=8, r=BAND)
                parts = pieces8(nn % XSLOTS)
                for ring, row, n in parts:
                    src = xr[:, ring:ring + n, R0 + COLS * q:R0 + COLS * q + COLS]
                    mm = pe.matmul(dst[:, :, row:row + n, :], w1_sb[:, :],
                                   src.rearrange("p r (g c) -> p g r c", c=8), start=True, stop=True)
                mm.then_inc(h_ready, 1)

            def width(b, i, nn, q):
                pe.wait_ge(h_done, b * 64 + i * 16 + (nn * 4 + q + 1))
                if q == 0 and not (isinstance(i, int) and i == 0 and nn == 0):
                    pe.wait_ge(k1_done, b * NBAND + i * 4 + nn)
                for t in range(NT):
                    v = 2 * (NT * q + t)
                    mm = pe.matmul(k_ps[:, v:v + 2], h_sb[:, 128 * t:128 * t + 128], w2_sb[:, :],
                                   start=True, stop=True)
                if q == NQ - 1:
                    mm.then_inc(ks_ready, 1)

            def turn_parts(b, i, nn, k):
                pe.wait_ge(parts_done[k], b * NBAND + i * 4 + (nn + 1))
                if k and not (isinstance(i, int) and 4 * i + nn == 0):
                    pe.wait_ge(rs_done, b * 64 + i * 16 + nn * 4)
                pe.transpose(turned_a[k], a_parts[:, k].rearrange("p g v -> p (g v)"), ident16_sb[:, :])\
                  .then_inc(parts_turned[k], 1)

            def turn_blocks(b, i, nn, q, g):
                first = isinstance(i, int) and 4 * i + nn == 0 and q == 0 and g == 0
                if not first:
                    pe.wait_ge(xt_done, b * 192 + i * 48 + (nn * 12 + q * 3 + g))
                pe.wait_ge(xb_done, b * 192 + i * 48 + (nn * 12 + q * 3 + g + 1))
                for j in range(3):
                    mm = pe.transpose(xt_ps[:, 128 * j:128 * j + 128], xb[:, g, j, :], ident_sb[:, :])
                mm.then_inc(xt_ready, 1)

            def spread_a(b, i, nn, u, fresh=False):
                s, q = u % 2, u // 2
                if not fresh:
                    pe.wait_ge(arg_done, b * 128 + i * 32 + (nn * 8 + u - 1))
                if u == 0 or fresh:
                    pe.wait_ge(stack_done[0], b * NBAND + i * 4 + (nn + 1))
                for t in range(NT):
                    v = 2 * (NT * q + t) + s
                    mm = pe.matmul(abc_ps[u % 2][:, 128 * t:128 * t + 128],
                                   sel_a_sb[:, v:v + 1].to_broadcast([AROWS, 128]), a_st[:, nn % 2, 0, :],
                                   start=True, stop=True)
                mm.then_inc(abc_ready, 1)

            def spread_r(b, i, nn, q, first):
                if not first:
                    pe.wait_ge(rs_done, b * 64 + i * 16 + (nn * 4 + q))
                if q == 0:
                    pe.wait_ge(stack_done[1], b * NBAND + i * 4 + (nn + 1))
                for t in range(NT):
                    for s in range(2):
                        v = 2 * (NT * q + t) + s
                        mm = pe.matmul(rs_ps[C * s:C * s + C, 128 * t:128 * t + 128],
                                       sel_a_sb[:, v:v + 1].to_broadcast([AROWS, C]), a_st[:, nn % 2, 1, :],
                                       start=True, stop=True)
                mm.then_inc(rs_ready, 1)

            def blur(b, i, nn, u, first):
                s, q = u % 2, u // 2
                pe.wait_ge(exp_done, b * 128 + i * 32 + (nn * 8 + u + 1))
                if s == 0:
                    pe.wait_ge(xt_done, b * 192 + i * 48 + (nn * 12 + q * 3 + 3))
                    if not (first and q < 2):
                        pe.wait_ge(blur_done, b * 64 + i * 16 + (nn * 4 + q - 1))
                moving = band[:, u % 2].rearrange("p g k o -> p (g k o)")
                for j in range(BLK):
                    lo, hi = max(0, 128 * j - 64), min(128 * NG, 128 * j + 64)
                    out_lo, out_hi = max(0, 64 * (j - 1)), min(64 * NG, 64 * (j + 1))
                    mm = pe.matmul(low_ps[q % 2][C * s:C * s + C, out_lo:out_hi], xt[:, q % 2, j, s, :],
                                   moving[:, lo:hi], start=(j == 0), stop=(j == BLK - 1),
                                   skip_group_check=True)
                mm.then_inc(bands_done, 1)

            def band_steps(b, i, nn, last):
                first = isinstance(i, int) and 4 * i + nn == 0
                if not last:
                    pe.wait_ge(*x_loaded(b, i, nn + 2))
                    if isinstance(i, int) and 4 * i + nn + 2 == NBAND:
                        pe.wait_ge(pad16_done, b + 1)
                for u in range(UB):
                    if u + 2 < UB:
                        spread_a(b, i, nn, u + 2)
                    elif not last:
                        spread_a(b, i, nn + 1, u + 2 - UB)
                    if u == 1:
                        turn_parts(b, i, nn, 1)
                    if u % 2 == 0 and u:
                        spread_r(b, i, nn, u // 2 - 1, first and u == 2)
                    elif u == 0 and not first:
                        spread_r(b, i, nn - 1, NQ - 1, False)
                    if not last:
                        if u == 0:
                            hidden(b, i, nn + 1, 0)
                        if u == 1:
                            width(b, i, nn + 1, 1)
                            hidden(b, i, nn + 1, 2)
                        if u == 2:
                            width(b, i, nn + 1, 3)
                        if u == 5:
                            turn_parts(b, i, nn + 1, 0)
                    blur(b, i, nn, u, first)
                    if not last:
                        if u == 0:
                            width(b, i, nn + 1, 0)
                            hidden(b, i, nn + 1, 1)
                        if u == 1:
                            width(b, i, nn + 1, 2)
                            hidden(b, i, nn + 1, 3)
                    q = u // 2
                    nq, nb = (q + 1, nn) if q + 1 < NQ else (0, nn + 1)
                    if not (last and q + 1 == NQ):
                        for g in ((0, 1) if u % 2 == 0 else (2,)):
                            turn_blocks(b, i, nb, nq, g)

            def filters(b, i, kk):
                if not (isinstance(i, int) and 4 * i + kk == 0):
                    pe.wait_ge(fs_done, b * NC1 + i * 4 + kk)
                rows = E[:, bass.ds(i * 8 + (2 * kk + 1), 2), 1:1 + W] if not isinstance(i, int) else \
                    E[:, 8 * i + 2 * kk + 1:8 * i + 2 * kk + 3, 1:1 + W]
                pe.matmul(f_ps[0:FR, :], ws_sb[:, :], rows, start=True, stop=True).then_inc(f_ready, 1)

            def turn_filters(b, i, kk):
                waits = [(fs_done, b * NC1 + i * 4 + (kk + 1))]
                if not (isinstance(i, int) and 4 * i + kk == 0):
                    waits.append((fq_done, b * NC1 + i * 4 + kk))
                hold(pe, *waits)
                for j in range(4):
                    mm = pe.transpose(fx_ps[:, FR * j:FR * j + FR], fs[:, 128 * j:128 * j + 128],
                                      ident_sb[0:FR, 0:FR])
                mm.then_inc(fx_ready, 1)

            def turn_split(b, i, kk):
                pe.wait_ge(f_parts_done, b * NC1 + i * 4 + (kk + 1))
                if not (isinstance(i, int) and 4 * i + kk == 0):
                    pe.wait_ge(f_split, b * NC1 + i * 4 + kk)
                if not (isinstance(i, int) and 4 * i + kk == NC1 - 1):
                    pe.wait_ge(fq_done, b * NC1 + i * 4 + (kk + 2))
                for j in range(4):
                    mm = pe.transpose(fst_ps[:, 128 * j:128 * j + 128],
                                      f_parts[:, j].rearrange("p g v -> p (g v)"), ident16_sb[:, :])
                mm.then_inc(f_turned, 1)

            def spread_filter(b, i, kk, t, fresh):
                if t == 0:
                    pe.wait_ge(f_split, b * NC1 + i * 4 + (kk + 1))
                if not (fresh and t < 3):
                    pe.wait_ge(prod_done, b * (NC1 * TAPS) + i * (4 * TAPS) + (kk * TAPS + t - 2))
                pe.matmul(spread_ps[t % 3][:, :], sel_sf_sb[:, t, :], sf_st[:, kk % 2, :],
                          start=True, stop=True).then_inc(spread_ready, 1)

            def conv_tap(b, i, kk, t):
                if t == 0:
                    if isinstance(i, int) and 4 * i + kk == 1:
                        pe.wait_ge(y1_edge, 4 * b + 3)
                        pe.wait_ge(l1_const, 112 * (b + 1))
                    if not (isinstance(i, int) and 4 * i + kk < 3):
                        pe.wait_ge(out_done, b * NO1 + i * 4 + (kk - 2))
                if t == 3:
                    pe.wait_ge(y1_ready, b * NC1 + i * 4 + (kk + 1))
                    if isinstance(i, int) and 4 * i + kk == NO1:
                        pe.wait_ge(y1_edge, 4 * b + 4)
                dy, dx = t // 3, t % 3
                r = (2 * ((kk - 1) % 4) + dy) % 8
                cp = conv_ps[kk % 2]
                for row, n in ([(0, 2)] if r < 7 else [(0, 1), (1, 1)]):
                    ring = (r + row) % 8
                    mm = pe.matmul(cp[:, W * row:W * row + W * n], wconv_sb[:, t, :],
                                   y1[:, ring:ring + n, dx:dx + W],
                                   start=(t == 0), stop=(t == TAPS - 1), skip_group_check=True)
                if t == TAPS - 1:
                    mm.then_inc(conv_ready, 1)

            def l1_step(b, i, kk):
                k = 4 * i + kk if isinstance(i, int) else None
                if k is None or k + 2 < NC1:
                    filters(b, i, kk + 2)
                for t in range(TAPS):
                    spread_filter(b, i, kk, t, fresh=(k == 0))
                    if k is None or k >= 2:
                        conv_tap(b, i, kk - 1, t)
                    if t == 1 and (k is None or k + 2 < NC1):
                        turn_filters(b, i, kk + 2)
                    if t == 5 and (k is None or k + 1 < NC1):
                        turn_split(b, i, kk + 1)

            with pe.Fori(0, B) as b:
                pe.wait_ge(pads_done, 3 * b + 3)
                pe.wait_ge(setup_pool, 4)
                pe.wait_ge(*x_loaded(b, 0, 0))
                pe.wait_ge(*x_loaded(b, 0, 1))
                for q in range(NQ):
                    hidden(b, 0, 0, q)
                    width(b, 0, 0, q)
                for g in range(3):
                    turn_blocks(b, 0, 0, 0, g)
                turn_parts(b, 0, 0, 0)
                for u in range(2):
                    spread_a(b, 0, 0, u, fresh=True)
                for nn in range(4):
                    band_steps(b, 0, nn, False)
                with pe.Fori(1, 3) as i:
                    for nn in range(4):
                        band_steps(b, i, nn, False)
                for nn in range(4):
                    band_steps(b, 3, nn, nn == 3)
                spread_r(b, 3, 3, NQ - 1, False)

                pe.wait_ge(mv_done, b + 1)
                pe.wait_ge(l1_const, 112 * (b + 1))
                pe.matmul(small_ps[:, 0:2], pair_sb[:, 0, :], mv, start=True, stop=True)
                pe.matmul(small_ps[:, 2:4], pair_sb[:, 1, :], mv, start=True, stop=True)\
                  .then_inc(pair_ready, 1)
                pe.wait_ge(pooled_done, b + 1)
                pe.wait_ge(l1_const, 112 * (b + 1))
                pe.matmul(small_ps[0:MID, 8:9], mlp1_sb, pooled_c, start=True, stop=True)\
                  .then_inc(mlp1_ready, 1)
                pe.wait_ge(halo_in, 32 * (b + 1))
                filters(b, 0, 0)
                turn_filters(b, 0, 0)
                filters(b, 0, 1)
                pe.wait_ge(h12_done, b + 1)
                for t in range(TAPS):
                    mm = pe.matmul(small_ps[:, 16 + t:17 + t], mlp2_sb[:, t, :], h12_c, start=True, stop=True)
                mm.then_inc(mlp2_ready, 1)
                turn_filters(b, 0, 1)
                pe.wait_ge(fpad_done, b + 1)
                turn_split(b, 0, 0)
                l1_step(b, 0, 0)
                for kk in range(1, 5):
                    l1_step(b, 0, kk)
                with pe.Fori(1, 15) as i:
                    for kk in range(1, 5):
                        l1_step(b, i, kk)
                for kk in range(1, 5):
                    l1_step(b, 15, kk)
                for t in range(TAPS):
                    conv_tap(b, 15, 4, t)

        @block.scalar
        def _(act):
            act.wait_ge(const_in, 16 * N_CONST)

            def relu(b, i, nn, q):
                act.wait_ge(h_ready, b * 64 + i * 16 + (nn * 4 + q + 1))
                act.activation(h_sb, h_ps[0:2 * HID, :], ACT.Relu,
                               bias=b1_c[0:2 * HID]).then_inc(h_done, 1)

            def square(b, i, nn):
                act.wait_ge(k2_done, b * NBAND + i * 4 + (nn + 1))
                act.activation(ka, kb, ACT.Square, scale=float(4.5 ** -0.5)).then_inc(ksq_done, 1)

            def weight_sums(b, i, nn, v0, v1):
                if v0 == 0:
                    act.wait_ge(a_ready, b * NBAND + i * 4 + (nn + 1))
                for v in range(v0, v1):
                    if not (isinstance(i, int) and 4 * i + nn == 0 and v < 4):
                        act.wait_ge(s_ready, b * (NBAND * NV) + i * (4 * NV) + (nn * NV + v - 3))
                    act.activation(junk[:, v % 4], g81_neg[:, :], ACT.Exp, scale=a_pix[:, v:v + 1],
                                   accum_out=s_pix[:, v:v + 1]).then_inc(s_ready, 1)

            def keep_r(b, i, nn, q, first):
                act.wait_ge(rs_ready, b * 64 + i * 16 + (nn * 4 + q + 1))
                if not first:
                    act.wait_ge(blur_done, b * 64 + i * 16 + (nn * 4 + q))
                act.activation(rs_sb, rs_ps[:, :], ACT.Copy).then_inc(rs_done, 1)

            def keep_block(b, i, nn, q, g):
                act.wait_ge(xt_ready, b * 192 + i * 48 + (nn * 12 + q * 3 + g + 1))
                act.activation(xt[:, q % 2, 3 * g:3 * g + 3, :, 0:C],
                               xt_ps[:, 0:384].rearrange("p (j s c) -> p j s c", j=3, s=2),
                               ACT.Copy).then_inc(xt_done, 1)

            def weights(b, i, nn, u):
                act.wait_ge(arg_done, b * 128 + i * 32 + (nn * 8 + u + 1))
                t = band[:, u % 2].rearrange("p g k o -> p (g k o)")
                act.activation(t, t, ACT.Exp).then_inc(exp_done, 1)

            def band_steps(b, i, nn, last):
                first = isinstance(i, int) and 4 * i + nn == 0
                for u in range(UB):
                    if u % 2 == 0 and u:
                        keep_r(b, i, nn, u // 2 - 1, first and u == 2)
                    elif u == 0 and not first:
                        keep_r(b, i, nn - 1, NQ - 1, False)
                    if not last:
                        if u == 0:
                            relu(b, i, nn + 1, 0)
                            relu(b, i, nn + 1, 1)
                        if u == 1:
                            relu(b, i, nn + 1, 2)
                            relu(b, i, nn + 1, 3)
                        if u == 3:
                            square(b, i, nn + 1)
                    q = u // 2
                    nq, nb = (q + 1, nn) if q + 1 < NQ else (0, nn + 1)
                    more = not (last and q + 1 == NQ)
                    if more:
                        keep_block(b, i, nb, nq, 0 if u % 2 == 0 else 2)
                    if u + 2 < UB:
                        weights(b, i, nn, u + 2)
                    elif not last:
                        weights(b, i, nn + 1, u + 2 - UB)
                    if more and u % 2 == 0:
                        keep_block(b, i, nb, nq, 1)
                    if not last and u >= 4:
                        weight_sums(b, i, nn + 1, 8 * (u - 4), 8 * (u - 3))

            def filt_bias(b, i, kk):
                act.wait_ge(f_ready, b * NC1 + i * 4 + (kk + 1))
                if not (isinstance(i, int) and 4 * i + kk == 0):
                    act.wait_ge(fx_ready, b * NC1 + i * 4 + kk)
                act.activation(fs, f_ps[0:FR, :], ACT.Identity, bias=bs_c[0:FR],
                               scale=STD_SPATIAL).then_inc(fs_done, 1)

            def filt_square(b, i, kk):
                act.wait_ge(fx_ready, b * NC1 + i * 4 + (kk + 1))
                act.activation(fx[:, kk % 2].rearrange("p v t -> p (v t)"), fx_ps, ACT.Copy).then_inc(fx_done, 1)
                if not (isinstance(i, int) and 4 * i + kk == 0):
                    act.wait_ge(fsum_done, b * NC1 + i * 4 + kk)
                act.activation(fq, fx_ps, ACT.Square).then_inc(fq_done, 1)

            def filt_sqrt(b, i, kk):
                act.wait_ge(fsum_done, b * NC1 + i * 4 + (kk + 1))
                act.activation(fsd[:, kk % 2], fsum, ACT.Sqrt,
                               scale=1.0 / ((TAPS - 1) * STD_SPATIAL ** 2)).then_inc(fsd_done, 1)

            def filt_split(b, i, kk):
                act.wait_ge(fnorm_done, b * NC1 + i * 4 + (kk + 1))
                if not (isinstance(i, int) and 4 * i + kk == 0):
                    act.wait_ge(f_turned, b * NC1 + i * 4 + kk)
                v = fn.rearrange("p (j v) -> p j v", j=4)
                act.activation(f_parts[:, :, 0, 0:FR], v, ACT.Copy).then_inc(f_hi, 1)
                act.wait_ge(f_res, b * NC1 + i * 4 + (kk + 1))
                act.activation(f_parts[:, :, 1, 0:FR], fres.rearrange("p (j v) -> p j v", j=4), ACT.Copy)\
                   .then_inc(f_mid, 1)

            def filt_keep(b, i, kk):
                act.wait_ge(f_turned, b * NC1 + i * 4 + (kk + 1))
                act.activation(sf_st[:, kk % 2, :], fst_ps, ACT.Copy).then_inc(f_split, 1)

            def lift(b, i, kk):
                act.wait_ge(sumb_done, b * (NDVE * NC1) + i * (4 * NDVE) + (kk * NDVE + NDVE))
                if not (isinstance(i, int) and 4 * i + kk == 0):
                    act.wait_ge(y1_ready, b * NC1 + i * 4 + kk)
                act.activation(lifted, sumb, ACT.Relu, scale=-0.9).then_inc(lifted_done, 1)

            def l1_step(b, i, kk):
                k = 4 * i + kk if isinstance(i, int) else 0
                if k + 2 < NC1:
                    filt_bias(b, i, kk + 2)
                if k + 1 < NC1:
                    filt_split(b, i, kk + 1)
                if k + 2 < NC1:
                    filt_square(b, i, kk + 2)
                    filt_sqrt(b, i, kk + 2)
                if k + 1 < NC1:
                    filt_keep(b, i, kk + 1)
                lift(b, i, kk)

            with act.Fori(0, B) as b:
                for q in range(NQ):
                    relu(b, 0, 0, q)
                square(b, 0, 0)
                weight_sums(b, 0, 0, 0, NV)
                for g in range(3):
                    keep_block(b, 0, 0, 0, g)
                for u in range(2):
                    weights(b, 0, 0, u)
                for nn in range(4):
                    band_steps(b, 0, nn, False)
                with act.Fori(1, 3) as i:
                    for nn in range(4):
                        band_steps(b, i, nn, False)
                for nn in range(4):
                    band_steps(b, 3, nn, nn == 3)
                keep_r(b, 3, 3, NQ - 1, False)
                act.wait_ge(nvar_done, b + 1)
                act.activation(sd_c, var_c, ACT.Sqrt).then_inc(nsd_done, 1)
                act.wait_ge(ncoef_done, b + 1)
                for j in range(5):
                    rows = E[:, 2 + 16 * j:18 + 16 * j, 1:1 + W]
                    act.activation(rows, rows, ACT.Identity, bias=nmr_c, scale=rstd_c,
                                   accum_out=sums[:, j:j + 1]).then_inc(norm_act, 1)
                act.wait_ge(mlp1_ready, b + 1)
                act.activation(h12_c, small_ps[0:MID, 8:9], ACT.Relu, bias=mb1_c[0:MID],
                               scale=1.0 / NPIX).then_inc(h12_done, 1)
                filt_bias(b, 0, 0)
                filt_bias(b, 0, 1)
                filt_square(b, 0, 0)
                filt_sqrt(b, 0, 0)
                act.wait_ge(css_done, b + 1)
                act.activation(csd_c, css_c, ACT.Sqrt, scale=1.0 / (TAPS - 1)).then_inc(csd_done, 1)
                filt_square(b, 0, 1)
                filt_sqrt(b, 0, 1)
                filt_split(b, 0, 0)
                filt_keep(b, 0, 0)
                for kk in range(5):
                    l1_step(b, 0, kk)
                with act.Fori(1, 15) as i:
                    for kk in range(1, 5):
                        l1_step(b, i, kk)
                for kk in range(1, 5):
                    l1_step(b, 15, kk)

        @block.vector
        def _(dve):
            dve.wait_ge(const_in, 16 * N_CONST)
            gflat = g_neg[:, :, :].rearrange("p k o -> p (k o)")
            dve.tensor_tensor(gflat, graw_sb, gin_sb, ALU.mult).then_inc(setup_dve, 1)
            dve.tensor_scalar(g81_neg[:, :], g81_neg[:, :], -1.0, None, ALU.mult).then_inc(setup_dve, 1)
            wv = ws_sb[:, :].rearrange("p (s t) -> p s t", t=TAPS)
            dve.tensor_reduce(wmean, wv, AX_X, ALU.add).then_inc(nd, 1)
            dve.wait_ge(setup_dve, 2)
            dve.scalar_tensor_tensor(gflat, gflat, -1.0, gout_sb, ALU.mult, ALU.add).then_inc(setup_dve, 1)
            dve.wait_ge(nd, 1)
            dve.tensor_scalar(wmean, wmean, -1.0 / TAPS, None, ALU.mult).then_inc(nd, 1)
            dve.wait_ge(nd, 2)
            dve.tensor_tensor(wv, wv, wmean.unsqueeze(2).to_broadcast([128, 2, TAPS]), ALU.add)\
               .then_inc(setup_dve, 1)
            dve.wait_ge(center_ready, 1)
            dve.tensor_scalar(bs_c[0:FR], small_ps[0:FR, 0:1], STD_SPATIAL, None, ALU.mult)\
               .then_inc(nd, 1)
            dve.wait_ge(setup_dve, 4)
            dve.wait_ge(nd, 3)

            def width_a(b, i, nn):
                dve.wait_ge(ks_ready, b * NBAND + i * 4 + (nn + 1))
                dve.tensor_scalar(ka, k_ps, b2_c, 0.0, ALU.add, ALU.max).then_inc(k1_done, 1)
                dve.wait_ge(k1_done, b * NBAND + i * 4 + (nn + 1))
                dve.tensor_scalar(kb, ka, 20.0, 1.0, ALU.mult, ALU.add).then_inc(k2_done, 1)

            def split(b, i, nn, k, src):
                n = b * NBAND + i * 4 + (nn + 1)
                if not (isinstance(i, int) and 4 * i + nn == 0):
                    dve.wait_ge(parts_turned[k], b * NBAND + i * 4 + nn)
                dve.tensor_copy(a_parts[:, k, 0], src).then_inc(hi_done[k], 1)
                dve.wait_ge(hi_done[k], n)
                dve.tensor_tensor(res_pix, src, a_parts[:, k, 0], ALU.subtract).then_inc(res_done[k], 1)
                dve.wait_ge(res_done[k], n)
                dve.tensor_copy(a_parts[:, k, 1], res_pix).then_inc(mid_done[k], 1)
                dve.wait_ge(mid_done[k], n)
                dve.tensor_tensor(a_parts[:, k, 2], res_pix, a_parts[:, k, 1], ALU.subtract)\
                   .then_inc(parts_done[k], 1)

            def width_b(b, i, nn):
                dve.wait_ge(ksq_done, b * NBAND + i * 4 + (nn + 1))
                dve.reciprocal(a_pix, ka).then_inc(a_ready, 1)
                dve.wait_ge(a_ready, b * NBAND + i * 4 + (nn + 1))
                split(b, i, nn, 0, a_pix)

            def sum_reciprocal(b, i, nn):
                dve.wait_ge(s_ready, b * (NBAND * NV) + i * (4 * NV) + (nn + 1) * NV)
                dve.reciprocal(r_pix, s_pix).then_inc(r_ready, 1)
                dve.wait_ge(r_ready, b * NBAND + i * 4 + (nn + 1))
                split(b, i, nn, 1, r_pix)

            def keep_parts(b, i, nn, k):
                dve.wait_ge(parts_turned[k], b * NBAND + i * 4 + (nn + 1))
                dve.tensor_copy(a_st[:, nn % 2, k, :], turned_a[k]).then_inc(stack_done[k], 1)

            def argument(b, i, nn, u):
                dve.wait_ge(abc_ready, b * 128 + i * 32 + (nn * 8 + u + 1))
                if not (isinstance(i, int) and 32 * i + 8 * nn + u < 2):
                    dve.wait_ge(bands_done, b * 128 + i * 32 + (nn * 8 + u - 1))
                a = abc_ps[u % 2][:, :].rearrange("p (g o) -> p g o", g=NG)
                dve.tensor_tensor(band[:, u % 2], g_neg[:, :, :].unsqueeze(1).to_broadcast([128, NG, 2, 64]),
                                  a.unsqueeze(2).to_broadcast([128, NG, 2, 64]), ALU.mult)\
                   .then_inc(arg_done, 1)

            def enhance(b, i, nn, q):
                done = b * 64 + i * 16 + (nn * 4 + q + 1)
                dve.wait_ge(rs_done, done)
                dve.wait_ge(bands_done, b * 128 + i * 32 + (nn * 8 + 2 * q + 2))
                dve.tensor_tensor(blur_sb, low_ps[q % 2][:, :], rs_sb, ALU.mult).then_inc(blur_done, 1)
                dve.wait_ge(blur_done, done)
                src = blur_sb.rearrange("p (g r c) -> p g r c", g=8, r=BAND)
                c0 = COLS * q
                for ring, row, n in pieces8(nn % XSLOTS):
                    res = xr[:, ring:ring + n, R0 + c0:R0 + c0 + COLS].rearrange("p r (g c) -> p g r c", c=8)
                    r0 = BAND * nn + row + 2
                    rows = slice(4 * BAND * i + r0, 4 * BAND * i + r0 + n) if isinstance(i, int) else \
                        bass.ds(i * (4 * BAND) + r0, n)
                    dst = E[:, rows, 1 + c0:1 + c0 + COLS].rearrange("p r (g c) -> p g r c", c=8)
                    op = dve.tensor_tensor(dst, src[:, :, row:row + n, :], res, ALU.add)
                op.then_inc(e_done, 1)
                dve.wait_ge(e_done, done)
                r0 = BAND * nn + 2
                rows = slice(4 * BAND * i + r0, 4 * BAND * i + r0 + BAND) if isinstance(i, int) else \
                    bass.ds(i * (4 * BAND) + r0, BAND)
                at = slice(16 * i + 4 * nn + q, 16 * i + 4 * nn + q + 1) if isinstance(i, int) else \
                    bass.ds(i * 16 + (4 * nn + q), 1)
                dve.bn_stats(stats[:, at, :].rearrange("p a s -> p (a s)"), E[:, rows, 1 + c0:1 + c0 + COLS])\
                   .then_inc(stats_done, 1)

            def band_steps(b, i, nn, last):
                first = isinstance(i, int) and 4 * i + nn == 0
                for u in range(UB):
                    if u == 0:
                        sum_reciprocal(b, i, nn)
                    if u == 1:
                        keep_parts(b, i, nn, 1)
                    if not last:
                        if u == 3:
                            width_a(b, i, nn + 1)
                        if u == 4:
                            width_b(b, i, nn + 1)
                        if u == 5:
                            keep_parts(b, i, nn + 1, 0)
                    if u + 2 < UB:
                        argument(b, i, nn, u + 2)
                    elif not last:
                        argument(b, i, nn + 1, u + 2 - UB)
                    if u % 2 and u > 1:
                        enhance(b, i, nn, (u - 3) // 2)
                    elif u == 1 and not first:
                        enhance(b, i, nn - 1, NQ - 1)

            def square_sum(b, i, kk):
                dve.wait_ge(fq_done, b * NC1 + i * 4 + (kk + 1))
                if not (isinstance(i, int) and 4 * i + kk == 0):
                    dve.wait_ge(fsd_done, b * NC1 + i * 4 + kk)
                dve.tensor_reduce(fsum, fq.rearrange("p (v t) -> p v t", t=TAPS), AX_X, ALU.add)\
                   .then_inc(fsum_done, 1)

            def reciprocal(b, i, kk):
                n = b * NC1 + i * 4 + (kk + 1)
                dve.wait_ge(fsd_done, n)
                dve.tensor_scalar(fsd[:, kk % 2], fsd[:, kk % 2], EPS1, None, ALU.add).then_inc(feps_done, 1)
                dve.wait_ge(feps_done, n)
                if not (isinstance(i, int) and 4 * i + kk == 0):
                    dve.wait_ge(fnorm_done, b * NC1 + i * 4 + kk)
                dve.reciprocal(frec, fsd[:, kk % 2]).then_inc(frec_done, 1)

            def tap(b, i, kk, t):
                k0 = b * (NC1 * TAPS) + i * (4 * TAPS) + kk * TAPS
                dve.wait_ge(spread_ready, k0 + (t + 1))
                if t == NPOOL and not (isinstance(i, int) and 4 * i + kk == 0):
                    dve.wait_ge(y1_ready, b * NC1 + i * 4 + kk)
                if t > NPOOL + 2:
                    dve.wait_ge(sumb_done, b * (NDVE * NC1) + i * (4 * NDVE) + (NDVE * kk + t - NPOOL - 2))
                dst = prod[:, t, :] if t < NPOOL else sumb if t == NPOOL else tmp[:, t % 2, :]
                dy, dx = t // 3, t % 3
                r0 = 2 * kk + dy
                rows = slice(8 * i + r0, 8 * i + r0 + 2) if isinstance(i, int) else bass.ds(i * 8 + r0, 2)
                dve.scalar_tensor_tensor(dst.rearrange("p (r w) -> p r w", w=W),
                                         spread_ps[t % 3][:, :].rearrange("p (r w) -> p r w", w=W),
                                         cf[:, t:t + 1], E[:, rows, dx:dx + W], ALU.mult, ALU.mult)\
                   .then_inc(prod_done, 1)

            def add(b, i, kk, n, src, t):
                dve.wait_ge(prod_done, b * (NC1 * TAPS) + i * (4 * TAPS) + (kk * TAPS + t + 1))
                if n:
                    dve.wait_ge(sumb_done, b * (NDVE * NC1) + i * (4 * NDVE) + (NDVE * kk + n))
                dve.tensor_tensor(sumb, sumb, src, ALU.add).then_inc(sumb_done, 1)

            def final(b, i, kk):
                dve.wait_ge(conv_ready, b * NO1 + i * 4 + kk)
                if not (isinstance(i, int) and 4 * i + kk < 3):
                    dve.wait_ge(stored[(kk - 1) % 2], b * (16 * NO1) + i * 64 + 32 * ((kk - 1) // 2))
                r0 = 2 * kk
                rows = slice(8 * i + r0, 8 * i + r0 + 2) if isinstance(i, int) else bass.ds(i * 8 + r0, 2)
                dve.scalar_tensor_tensor(stage[:, (kk - 1) % 2, :].rearrange("p (r w) -> p r w", w=W),
                                         conv_ps[kk % 2][:, :].rearrange("p (r w) -> p r w", w=W),
                                         bconv_c, E[:, rows, 1:1 + W], ALU.add, ALU.add)\
                   .then_inc(out_done, 1)

            def l1_step(b, i, kk):
                k = 4 * i + kk if isinstance(i, int) else None
                for t in range(TAPS):
                    tap(b, i, kk, t)
                    if t == 0 and (k is None or k + 1 < NC1):
                        reciprocal(b, i, kk + 1)
                    if t == 1 and (k is None or k >= 3):
                        final(b, i, kk - 2)
                    if t == 4 and (k is None or k + 2 < NC1):
                        square_sum(b, i, kk + 2)
                    if t > NPOOL + 1:
                        add(b, i, kk, t - NPOOL - 2, tmp[:, (t - 1) % 2, :], t - 1)
                add(b, i, kk, NDVE - 2, tmp[:, (TAPS - 1) % 2, :], TAPS - 1)
                dve.wait_ge(suma_done, b * ((NPOOL - 1) * NC1) + i * (4 * (NPOOL - 1)) + (NPOOL - 1) * (kk + 1))
                add(b, i, kk, NDVE - 1, suma, TAPS - 1)

            with dve.Fori(0, B) as b:
                width_a(b, 0, 0)
                width_b(b, 0, 0)
                keep_parts(b, 0, 0, 0)
                for u in range(2):
                    argument(b, 0, 0, u)
                for nn in range(4):
                    band_steps(b, 0, nn, False)
                with dve.Fori(1, 3) as i:
                    for nn in range(4):
                        band_steps(b, i, nn, False)
                for nn in range(4):
                    band_steps(b, 3, nn, nn == 3)
                enhance(b, 3, 3, NQ - 1)
                n0 = b * 5 + 3
                hold(dve, (stats_done, b * 64 + 64))
                dve.bn_aggr(mv, stats[:, :, :].rearrange("p a s -> p (a s)")).then_inc(mv_done, 1)
                dve.wait_ge(pair_ready, b + 1)
                dve.tensor_copy(pv, small_ps[:, 0:4]).then_inc(nd, 1)
                dve.wait_ge(nd, n0 + 1)
                dve.tensor_tensor(var_c, pv[:, 2:3], pv[:, 2:3], ALU.mult).then_inc(nd, 1)
                dve.wait_ge(nd, n0 + 2)
                dve.tensor_tensor(var_c, var_c, pv[:, 1:2], ALU.add).then_inc(nd, 1)
                dve.wait_ge(nd, n0 + 3)
                dve.tensor_scalar(var_c, var_c, 1e-5, None, ALU.add).then_inc(nvar_done, 1)
                dve.wait_ge(nsd_done, b + 1)
                dve.reciprocal(rstd_c, sd_c).then_inc(nd, 1)
                dve.wait_ge(nd, n0 + 4)
                dve.tensor_scalar(nmr_c, pv[:, 0:1], -1.0, rstd_c, ALU.mult, ALU.mult).then_inc(ncoef_done, 1)
                dve.wait_ge(ncoef_done, b + 1)
                for j in range(5, 8):
                    rows = E[:, 2 + 16 * j:18 + 16 * j, 1:1 + W]
                    dve.tensor_scalar(rows, rows, rstd_c, nmr_c, ALU.mult, ALU.add).then_inc(norm_dve, 1)
                for j in range(5, 8):
                    dve.wait_ge(norm_dve, 3 * b + (j - 4))
                    dve.tensor_reduce(sums[:, j:j + 1], E[:, 2 + 16 * j:18 + 16 * j, 1:1 + W],
                                      mybir.AxisListType.XY, ALU.add).then_inc(sums_dve, 1)
                dve.wait_ge(norm_act, 5 * b + 5)
                dve.wait_ge(sums_dve, 3 * b + 3)
                dve.tensor_reduce(pooled_c, sums, AX_X, ALU.add).then_inc(pooled_done, 1)
                square_sum(b, 0, 0)
                c0 = b * 7
                dve.wait_ge(mlp2_ready, b + 1)
                dve.tensor_tensor(cc, small_ps[:, 16:16 + TAPS], mb2_sb, ALU.add).then_inc(cf_steps, 1)
                dve.wait_ge(cf_steps, c0 + 1)
                dve.tensor_reduce(cm_c, cc, AX_X, ALU.add).then_inc(cf_steps, 1)
                dve.wait_ge(cf_steps, c0 + 2)
                dve.tensor_scalar(cm_c, cm_c, -1.0 / TAPS, None, ALU.mult).then_inc(cf_steps, 1)
                dve.wait_ge(cf_steps, c0 + 3)
                dve.tensor_scalar(cc, cc, cm_c, None, ALU.add).then_inc(cf_steps, 1)
                dve.wait_ge(cf_steps, c0 + 4)
                dve.tensor_tensor(cf, cc, cc, ALU.mult).then_inc(cf_steps, 1)
                dve.wait_ge(cf_steps, c0 + 5)
                dve.tensor_reduce(css_c, cf, AX_X, ALU.add).then_inc(css_done, 1)
                dve.wait_ge(csd_done, b + 1)
                dve.tensor_scalar(csd_c, csd_c, EPS1, None, ALU.add).then_inc(cf_steps, 1)
                dve.wait_ge(cf_steps, c0 + 6)
                dve.reciprocal(cr_c, csd_c).then_inc(cf_steps, 1)
                dve.wait_ge(cf_steps, c0 + 7)
                dve.scalar_tensor_tensor(cf, cc, cr_c, std_sb[:, 0:TAPS], ALU.mult, ALU.mult)\
                   .then_inc(nd, 1)
                square_sum(b, 0, 1)
                reciprocal(b, 0, 0)
                dve.wait_ge(nd, n0 + 5)
                for kk in range(5):
                    l1_step(b, 0, kk)
                with dve.Fori(1, 15) as i:
                    for kk in range(1, 5):
                        l1_step(b, i, kk)
                for kk in range(1, 5):
                    l1_step(b, 15, kk)
                final(b, 15, 3)
                final(b, 15, 4)

        @block.gpsimd
        def _(pool):
            pool.wait_ge(setup_dve, 4)
            pool.wait_ge(center_ready, 1)
            pool.memset(E[:, 0:2, :], 0.0).then_inc(setup_pool, 1)
            pool.memset(E[:, ER - 2:ER, :], 0.0).then_inc(setup_pool, 1)
            pool.memset(E[:, 2:ER - 2, 0:1], 0.0).then_inc(setup_pool, 1)
            pool.memset(E[:, 2:ER - 2, EW - 1:EW], 0.0).then_inc(setup_pool, 1)

            def pack(b, i, nn, q):
                for g in range(3):
                    first = isinstance(i, int) and 4 * i + nn == 0 and q == 0
                    if not first:
                        hold(pool, (xt_ready, b * 192 + i * 48 + (nn * 12 + q * 3 + g - 2)))
                    c0 = COLS * q + 24 * g
                    dst = xb[:, g].rearrange("p j (r c) -> p j r c", c=8)
                    lo = BAND * (nn % XSLOTS)
                    parts = [(lo, 0, 16)] if nn % XSLOTS < XSLOTS - 1 else [(lo, 0, 8), (0, 8, 8)]
                    for ring, row, n in parts:
                        src = xr[:, ring:ring + n, c0:c0 + 24].rearrange("p r (j c) -> p j r c", c=8)
                        op = pool.tensor_copy(dst[:, :, row:row + n, :], src)
                    op.then_inc(xb_done, 1)

            def band_steps(b, i, nn, last):
                for q in range(NQ):
                    nq, nb = (q + 1, nn) if q + 1 < NQ else (0, nn + 1)
                    if nq == 0 and not last:
                        pool.wait_ge(*x_loaded(b, i, nb + 1))
                        if isinstance(i, int) and 4 * i + nb + 1 == NBAND:
                            pool.wait_ge(pad16_done, b + 1)
                    if not (last and nq == 0):
                        pack(b, i, nb, nq)
                    if isinstance(i, int) and 4 * i + nn == 13 and q == 0:
                        hold(pool, (e_done, b * 64 + 13 * NQ), (xb_done, b * 192 + (13 * 12 + 6)))
                        pool.memset(xr[C:2 * C, R0:BAND, R0:R0 + W], 0.0).then_inc(pad16_done, 1)
                        pool.wait_ge(pad16_done, b + 1)

            def split_f(b, i, kk):
                n = b * NC1 + i * 4 + (kk + 1)
                pool.wait_ge(frec_done, n)
                pool.tensor_tensor(fn.rearrange("p (v t) -> p v t", t=TAPS), fx[:, kk % 2],
                                   frec.unsqueeze(2).to_broadcast([128, 8, TAPS]), ALU.mult)\
                    .then_inc(fnorm_done, 1)
                pool.wait_ge(f_hi, n)
                res = fres.rearrange("p (j v) -> p j v", j=4)
                pool.tensor_tensor(res, fn.rearrange("p (j v) -> p j v", j=4), f_parts[:, :, 0, 0:FR],
                                   ALU.subtract).then_inc(f_res, 1)
                pool.wait_ge(f_mid, n)
                pool.tensor_tensor(f_parts[:, :, 2, 0:FR], res, f_parts[:, :, 1, 0:FR], ALU.subtract)\
                    .then_inc(f_parts_done, 1)

            def sum_a(b, i, kk):
                p0 = b * (NC1 * TAPS) + i * (4 * TAPS) + kk * TAPS
                s0 = b * ((NPOOL - 1) * NC1) + i * (4 * (NPOOL - 1)) + (NPOOL - 1) * kk
                pool.wait_ge(prod_done, p0 + 2)
                if not (isinstance(i, int) and 4 * i + kk == 0):
                    pool.wait_ge(sumb_done, b * (NDVE * NC1) + i * (4 * NDVE) + NDVE * kk)
                pool.tensor_tensor(suma, prod[:, 0, :], prod[:, 1, :], ALU.add).then_inc(suma_done, 1)
                for t in range(2, NPOOL):
                    pool.wait_ge(prod_done, p0 + (t + 1))
                    pool.wait_ge(suma_done, s0 + (t - 1))
                    pool.tensor_tensor(suma, suma, prod[:, t, :], ALU.add).then_inc(suma_done, 1)

            def leaky(b, i, kk):
                pool.wait_ge(lifted_done, b * NC1 + i * 4 + (kk + 1))
                r = 2 * (kk % 4)
                pool.tensor_tensor(y1[:, r:r + 2, 1:1 + W], sumb.rearrange("p (r w) -> p r w", w=W),
                                   lifted.rearrange("p (r w) -> p r w", w=W), ALU.add).then_inc(y1_ready, 1)

            def l1_step(b, i, kk):
                if not (isinstance(i, int) and 4 * i + kk == NC1 - 1):
                    split_f(b, i, kk + 1)
                sum_a(b, i, kk)
                leaky(b, i, kk)

            with pool.Fori(0, B) as b:
                hold(pool, (ring_free, b + 1))
                pool.memset(xr[:, :, 0:R0], 0.0).then_inc(pads_done, 1)
                pool.memset(xr[:, :, R0 + W:XW], 0.0).then_inc(pads_done, 1)
                pool.memset(xr[0:C, 0:R0, R0:R0 + W], 0.0).then_inc(pads_done, 1)
                hold(pool, (pads_done, 3 * b + 3), x_loaded(b, 0, 0), x_loaded(b, 0, 1))
                pack(b, 0, 0, 0)
                for nn in range(4):
                    band_steps(b, 0, nn, False)
                with pool.Fori(1, 3) as i:
                    for nn in range(4):
                        band_steps(b, i, nn, False)
                for nn in range(4):
                    band_steps(b, 3, nn, nn == 3)
                hold(pool, (e_done, b * 64 + 64))
                pool.memset(y1[:, :, 0:1], 0.0).then_inc(y1_edge, 1)
                pool.memset(y1[:, :, EW - 1:EW], 0.0).then_inc(y1_edge, 1)
                pool.memset(f_parts[:, :, :, FR:32], 0.0).then_inc(fpad_done, 1)
                split_f(b, 0, 0)
                split_f(b, 0, 1)
                sum_a(b, 0, 0)
                leaky(b, 0, 0)
                hold(pool, (y1_ready, b * NC1 + 1))
                pool.memset(y1[0:C, 0:1, 1:1 + W], 0.0).then_inc(y1_edge, 1)
                for kk in range(1, 5):
                    l1_step(b, 0, kk)
                with pool.Fori(1, 15) as i:
                    for kk in range(1, 5):
                        l1_step(b, i, kk)
                for kk in range(1, 5):
                    l1_step(b, 15, kk)
                hold(pool, (y1_ready, b * NC1 + NC1), (suma_done, (b + 1) * ((NPOOL - 1) * NC1)))
                pool.memset(y1[C:2 * C, 1:2, 1:1 + W], 0.0).then_inc(y1_edge, 1)


def _window_index():
    p, o = np.arange(128), np.arange(64)
    ir, ic, r, c = p // 8, p % 8, o // 8, o % 8
    u = ir[:, None] - r[None, :]
    index = np.zeros((128, 2, 64), np.int64)
    inside = np.zeros((128, 2, 64), bool)
    for kind in range(2):
        v = (ic[:, None] - c[None, :]) + 8 * kind
        ok = (u >= 0) & (u < K0) & (v >= 0) & (v < K0)
        inside[:, kind] = ok
        index[:, kind] = np.where(ok, u * K0 + v, 0)
    return index.reshape(128, 128), inside.reshape(128, 128)


def _layout(i):
    f = np.float32
    index, inside = _window_index()
    d = {"x": np.asarray(i["x"])}
    d["graw"] = np.asarray(i["L0_conv_gauss_kernel"]).reshape(-1)[index]
    d["gin"] = inside.astype(f)
    d["gout"] = np.where(inside, f(0), f(FAR)).astype(f)
    d["g81"] = np.broadcast_to(np.asarray(i["L0_conv_gauss_kernel"]).reshape(1, K0 * K0), (128, K0 * K0))
    sel = np.zeros((AROWS, NV), np.uint16)
    for g in range(3):
        for v in range(NV):
            sel[32 * g + v, v] = BF16_ONE
    d["sel_a"] = sel
    d["ident16"] = np.where(np.eye(128, dtype=bool), np.uint16(BF16_ONE), np.uint16(0))
    d["ident"] = np.eye(128, dtype=f)
    w1 = np.zeros((128, 2 * HID), f)
    w2 = np.zeros((2 * HID, 2), f)
    for s in range(2):
        w1[C * s:C * s + C, HID * s:HID * s + HID] = np.asarray(i["L0_conv_w1"])
        w2[HID * s:HID * s + HID, s] = np.asarray(i["L0_conv_w2"])[:, 0]
    d["w1"], d["w2"] = w1, w2
    pair = np.zeros((128, 2, 128), f)
    for m in range(128):
        pair[m, 0, m] = pair[(m + 64) % 128, 0, m] = 0.5
        pair[m, 1, m], pair[(m + 64) % 128, 1, m] = 0.5, -0.5
    d["pair"] = pair
    ws = np.zeros((128, FR), f)
    bs = np.zeros((FR, 1), f)
    center = np.zeros((FR, FR), f)
    sel_sf = np.zeros((AROWS, TAPS, 128), np.uint16)
    for s in range(2):
        r = slice(TAPS * s, TAPS * s + TAPS)
        ws[C * s:C * s + C, r] = np.asarray(i["L1_conv_Ws"]).T
        bs[r, 0] = np.asarray(i["L1_conv_bs"])
        center[r, r] = np.eye(TAPS, dtype=f) - f(1.0 / TAPS)
        for g in range(3):
            for t in range(TAPS):
                sel_sf[32 * g + TAPS * s + t, t, C * s:C * s + C] = BF16_ONE
    d["ws"], d["bs"], d["center"], d["sel_sf"] = ws, bs, center, sel_sf
    wc = np.zeros((128, TAPS, 128), f)
    for s in range(2):
        wc[C * s:C * s + C, :, C * s:C * s + C] = \
            np.asarray(i["L1_conv_Wc"]).transpose(1, 2, 3, 0).reshape(C, TAPS, C)
    d["wconv"] = wc
    small = np.zeros((128, 5), f)
    small[0:HID, 0] = small[HID:2 * HID, 0] = np.asarray(i["L0_conv_b1"])
    small[:, 1] = np.asarray(i["L0_conv_b2"])[0]
    small[0:C, 3] = small[C:, 3] = np.asarray(i["L1_conv_bc"])
    small[0:MID, 4] = np.asarray(i["L1_conv_b1"])
    d["small"] = small
    d["mlp1"] = np.concatenate([np.asarray(i["L1_conv_W1"]).T] * 2, axis=0)
    w2t = np.asarray(i["L1_conv_W2"]).reshape(C, TAPS, MID).transpose(2, 1, 0)
    d["mlp2"] = np.concatenate([w2t, w2t], axis=2)
    d["mb2"] = np.concatenate([np.asarray(i["L1_conv_b2"]).reshape(C, TAPS)] * 2, axis=0)
    d["stdch"] = np.concatenate([np.asarray(i["L1_conv_std_ch"]).reshape(C, TAPS)] * 2, axis=0)
    return d


_ORDER = ["x", "graw", "gin", "gout", "g81", "sel_a", "ident", "ident16", "w1", "w2", "pair", "ws", "bs", "center",
          "sel_sf", "wconv", "small", "mlp1", "mlp2", "mb2", "stdch"]


def kernel(**inputs):
    import concourse.bacc as _bacc
    from concourse.bass_utils import run_bass_kernel_spmd as _run

    nc = _bacc.Bacc("TRN2", target_bir_lowering=False, num_devices=1)
    laid = _layout(inputs)
    arrays, args = {}, {}
    for name in _ORDER:
        a = np.ascontiguousarray(laid[name])
        arrays[f"in_{name}"] = a
        args[name] = nc.dram_tensor(f"in_{name}", a.shape, mybir.dt.from_np(a.dtype), kind="ExternalInput").ap()
    o = nc.dram_tensor("out_0", (B, C, H, W), F32, kind="ExternalOutput").ap()
    build(nc, out=o, **args)
    r = _run(nc, [arrays], core_ids=[0])
    return r.results[0]["out_0"]
```

```python
from contextlib import ExitStack

import numpy as np

import concourse.bass as bass
from concourse import mybir

ALU = mybir.AluOpType
ACT = mybir.ActivationFunctionType
F32 = mybir.dt.float32
BF16 = mybir.dt.bfloat16
AX_X = mybir.AxisListType.X

B, C, H, W = 8, 64, 256, 256
HID, MID = 32, 12
K0, R0 = 9, 4
ROWS = H // 2
BAND = 8
NBAND = ROWS // BAND
COLS = 64
NQ = W // COLS
NT = COLS // 16
NG = 2 * NT
UB = 2 * NQ
NV = 2 * NT * NQ
VA = 8
VP = 8
NP = (NV - VA) // VP
FR = 18
XW = W + 2 * R0
ER, EW = ROWS + 4, W + 2
BLK = 2 * NT + 1
TAPS = 9
NC1 = ROWS // 2 + 1
NO1 = ROWS // 2
NPIX = H * W
STD_SPATIAL = 1.4142135623730951 / 3
EPS1 = 1e-10
NPOOL = 6
LAST_ADD = 1
NDVE = TAPS - NPOOL
FAR = -1.0e30
BF16_ONE = 0x3F80
AROWS = 96
XSLOTS = 4
YSLOTS = 4
CONV_AT = (0, 1, 3, 5, 6, 8)
CTAPS = 6
NBUF = 4


def build(nc, x, graw, gin, gout, g81, sel_a, ident, ident16, w1, w2, pair, ws, bs, center,
          sel_sf, wconv, small, mlp1, mlp2, mb2, stdch, out):
    with ExitStack() as ctx:
        def sb(name, shape, dt=F32):
            return ctx.enter_context(nc.sbuf_tensor(name, shape, dt))

        def sem(name):
            return ctx.enter_context(nc.semaphore(name))

        E = sb("image", [128, ER, EW])
        g_neg = sb("g_neg", [128, 2, 64])
        g81_neg = sb("g81_neg", [128, K0 * K0])
        sel_a_sb = sb("sel_a_sb", [AROWS, NV], BF16)
        ident_sb = sb("ident_sb", [128, 128])
        ident16_sb = sb("ident16_sb", [128, 128], BF16)
        w1_sb = sb("w1_sb", [128, 2 * HID])
        w2_sb = sb("w2_sb", [2 * HID, 2])
        ws_sb = sb("ws_sb", [128, FR])
        stats = sb("stats", [128, NBAND * NQ, 6])
        cols = sb("cols", [128, 64])
        b1_c, b2_c, bs_c, bconv_c, mb1_c = (cols[:, i:i + 1] for i in range(5))
        mv = cols[:, 6:8]
        pv = cols[:, 8:12]
        var_c, sd_c, rstd_c, nmr_c = (cols[:, i:i + 1] for i in range(12, 16))
        sums = cols[:, 16:24]
        pooled_c, h12_c = cols[:, 24:25], cols[0:MID, 25:26]
        cf = cols[:, 26:35]
        cm_c, css_c, csd_c, cr_c = (cols[:, i:i + 1] for i in range(35, 39))
        wmean = cols[:, 48:50]
        cc = cols[:, 54:63]

        xreg = sb("xreg", [128, XSLOTS * BAND * XW])
        work = sb("work", [128, 9728])

        def carve(region, start, n):
            assert start + n <= region.shape[1]
            return region[:, start:start + n], start + n

        xr = xreg[:, :].rearrange("p (r w) -> p r w", w=XW)
        at = 0
        xt_f, at = carve(work, at, 2 * BLK * 128)
        xt = xt_f.rearrange("p (n j s c) -> p n j s c", n=2, j=BLK, s=2)
        xb_f, at = carve(work, at, 2 * 384)
        xb = xb_f.rearrange("p (g j o) -> p g j o", g=2, j=3)
        h_f, at = carve(work, at, 512)
        h_sb = h_f[0:2 * HID, :]
        band_f, at = carve(work, at, NBUF * 1024)
        band = band_f.rearrange("p (n g k o) -> p n g k o", n=NBUF, g=NG, k=2)
        as_f, at = carve(work, at, 2 * 2 * 64)
        a_st = as_f[0:AROWS, :].bitcast(BF16).rearrange("p (n k o) -> p n k o", n=2, k=2)
        sp_f, at = carve(work, at, 96)
        a_parts = sp_f.bitcast(BF16).rearrange("p (k g v) -> p k g v", k=2, g=3)
        pix_f, at = carve(work, at, 6 * NV)
        ka, kb, a_pix, s_pix, r_pix, res_pix = (pix_f[:, NV * j:NV * j + NV] for j in range(6))
        taps_f, at = carve(work, at, 2 * VP * K0 * K0)
        taps = taps_f.rearrange("p (n v w) -> p n v w", n=2, v=VP)
        junk_f, at = carve(work, at, 2 * K0 * K0)
        junk = junk_f.rearrange("p (n w) -> p n w", n=2)
        graw_sb = work[:, 0:128]
        gin_sb = work[:, 128:256]
        gout_sb = work[:, 256:384]
        center_sb = work[0:FR, 1536:1536 + FR]
        bs_raw = work[0:FR, 1700:1701]

        at = 0
        y1_f, at = carve(xreg, at, YSLOTS * 2 * EW)
        y1 = y1_f.rearrange("p (n s w) -> p n s w", n=YSLOTS, s=2)
        p_f, at = carve(xreg, at, NPOOL * 512)
        prod = p_f.rearrange("p (n f) -> p n f", n=NPOOL)
        suma, at = carve(xreg, at, 512)
        sumb, at = carve(xreg, at, 512)
        tmp_f, at = carve(xreg, at, 1024)
        tmp = tmp_f.rearrange("p (n f) -> p n f", n=2)
        sf_f, at = carve(xreg, at, TAPS * 64)
        sel_sf_sb = sf_f[0:AROWS, :].bitcast(BF16).rearrange("p (t m) -> p t m", t=TAPS)
        at = 0
        wconv_f, at = carve(work, at, CTAPS * 128)
        wconv_sb = wconv_f.rearrange("p (t m) -> p t m", t=CTAPS)
        leaked, at = carve(work, at, 512)
        mlp2_f, at = carve(work, at, TAPS * 128)
        mlp2_sb = mlp2_f[0:MID, :].rearrange("p (t m) -> p t m", t=TAPS)
        pair_f, at = carve(work, at, 256)
        pair_sb = pair_f.rearrange("p (k m) -> p k m", k=2)
        mlp1_sb, at = carve(work, at, MID)
        mb2_sb, at = carve(work, at, TAPS)
        std_sb, at = carve(work, at, TAPS + 1)
        ss_f, at = carve(work, at, 2 * 256)
        sf_st = ss_f[0:AROWS, :].bitcast(BF16).rearrange("p (n f) -> p n f", n=2)
        fs_f, at = carve(work, at, 512)
        fs = fs_f[0:FR, :]
        lifted, at = carve(work, at, 512)
        fx_f, at = carve(work, at, 2 * 72)
        fx = fx_f.rearrange("p (n v t) -> p n v t", n=2, t=TAPS)
        fq_f, at = carve(work, at, 3 * 72)
        fq, fn, fres = (fq_f[:, 72 * j:72 * j + 72] for j in range(3))
        fsum, at = carve(work, at, 8)
        fsd_f, at = carve(work, at, 16)
        fsd = fsd_f.rearrange("p (n v) -> p n v", n=2)
        frec, at = carve(work, at, 8)
        fp_f, at = carve(work, at, 192)
        stage_f, at = carve(work, at, 1024)
        stage = stage_f.rearrange("p (n f) -> p n f", n=2)
        f_parts = fp_f.bitcast(BF16).rearrange("p (j g v) -> p j g v", j=4, g=3)

        banks = [ctx.enter_context(nc.psum_tensor(f"bank{i}", [128, 512], F32)) for i in range(8)]
        h_ps, k_ps, xt_ps, low_ps, rs_ps = banks[0], banks[1][:, 0:NV], banks[2], banks[5:7], banks[7]
        abc_ps = banks[3:5]
        turned_a = [ps[:, 0:64].bitcast(BF16)[0:AROWS] for ps in (h_ps, rs_ps)]
        spread_ps = [banks[0], banks[3], banks[4]]
        f_ps, conv_ps, small_ps = banks[1], banks[5:7], banks[7]
        fx_ps = banks[2][:, 0:72]
        fst_ps = banks[2][:, 128:384].bitcast(BF16)[0:AROWS]

        const_in = sem("const_in")
        setup_dve = sem("setup_dve")
        setup_pool = sem("setup_pool")
        center_ready = sem("center_ready")
        x_in = [sem(f"x_in{i}") for i in range(XSLOTS)]
        ring_free = sem("ring_free")
        pads_done = sem("pads_done")
        pad16_done = sem("pad16_done")
        h_ready, h_done = sem("h_ready"), sem("h_done")
        ks_ready, k1_done, k2_done, ksq_done, a_ready = (
            sem(n) for n in ("ks_ready", "k1_done", "k2_done", "ksq_done", "a_ready"))
        taparg_done, tapexp_done, s_ready, s_act, r_ready = (
            sem(n) for n in ("taparg_done", "tapexp_done", "s_ready", "s_act", "r_ready"))
        hi_done, res_done, mid_done = ([sem(f"{n}{k}") for k in range(2)] for n in ("hi_done", "res_done", "mid_done"))
        parts_done, parts_turned, stack_done = (
            [sem(f"{n}{k}") for k in range(2)] for n in ("parts_done", "parts_turned", "stack_done"))
        abc_ready, arg_done, exp_done, bands_done = (
            sem(n) for n in ("abc_ready", "arg_done", "exp_done", "bands_done"))
        rs_ready, rs_done, blur_done, e_done = (
            sem(n) for n in ("rs_ready", "rs_done", "blur_done", "e_done"))
        xb_done, xt_ready, xt_done = sem("xb_done"), sem("xt_ready"), sem("xt_done")
        stats_done, mv_done, pair_ready, nd = (
            sem(n) for n in ("stats_done", "mv_done", "pair_ready", "norm_steps"))
        nvar_done, nsd_done, ncoef_done = sem("nvar_done"), sem("nsd_done"), sem("ncoef_done")
        norm_act, norm_dve, sums_dve = sem("norm_act"), sem("norm_dve"), sem("sums_dve")
        pooled_done, mlp1_ready, h12_done, mlp2_ready = (
            sem(n) for n in ("pooled_done", "mlp1_ready", "h12_done", "mlp2_ready"))
        cf_steps, css_done, csd_done = sem("cf_steps"), sem("css_done"), sem("csd_done")
        fpad_done = sem("fpad_done")
        halo_in, l1_const = sem("halo_in"), sem("l1_const")
        f_ready, fs_done, fx_ready, fx_done, fq_done, fsum_done, fsd_done = (
            sem(n) for n in ("f_ready", "fs_done", "fx_ready", "fx_done", "fq_done", "fsum_done", "fsd_done"))
        feps_done, frec_done, fnorm_done, f_hi, f_res, f_mid, f_parts_done, f_turned, f_split = (
            sem(n) for n in ("feps_done", "frec_done", "fnorm_done", "f_hi", "f_res", "f_mid",
                             "f_parts_done", "f_turned", "f_split"))
        spread_ready, prod_done, suma_done, sumb_done = (
            sem(n) for n in ("spread_ready", "prod_done", "suma_done", "sumb_done"))
        leaked_done, y1_ready, y1_edge, conv_ready, conv_kept, out_done = (
            sem(n) for n in ("leaked_done", "y1_ready", "y1_edge", "conv_ready", "conv_kept", "out_done"))
        lifted_done = sem("lifted_done")
        stored = [sem("stored0"), sem("stored1")]

        N_CONST = 13
        block = ctx.enter_context(nc.Block())

        def x_loaded(b, i, kk):
            slot = kk % XSLOTS
            per_image = 32 * (5 if slot == 0 else 4)
            return x_in[slot], b * per_image + i * 32 + 32 * (kk // XSLOTS + 1)

        def pieces8(nn):
            first = BAND * nn + R0
            if nn < XSLOTS - 1:
                return [(first, 0, BAND)]
            return [(first, 0, R0), (0, R0, R0)]

        def buffer(nn, u):
            return (UB * nn + u) % NBUF

        def place(i, nn, q, row, n):
            r0, c0 = BAND * nn + row + 2, COLS * q
            rows = slice(4 * BAND * i + r0, 4 * BAND * i + r0 + n) if isinstance(i, int) else \
                bass.ds(i * (4 * BAND) + r0, n)
            return E[:, rows, 1 + c0:1 + c0 + COLS].rearrange("p r (g c) -> p g r c", c=8)

        def hold(eng, *waits):
            values = [(which, eng.to_reg(value)) for which, value in waits]
            eng.wait_ge(const_in, 16 * N_CONST)
            for which, value in values:
                eng.wait_ge(which, value)

        def all_stored(eng, b):
            hold(eng, *((stored[j], (b + 1) * (32 * NO1 // 2)) for j in range(2)))

        @block.sync
        def _(sp):
            for dst, src in ((graw_sb, graw), (gin_sb, gin), (gout_sb, gout), (g81_neg[:, :], g81),
                             (sel_a_sb[:, :].bitcast(mybir.dt.uint16), sel_a), (ident_sb[:, :], ident),
                             (ident16_sb[:, :].bitcast(mybir.dt.uint16), ident16), (w1_sb[:, :], w1),
                             (w2_sb[:, :], w2), (ws_sb[:, :], ws), (center_sb, center), (bs_raw, bs),
                             (cols[:, 0:5], small)):
                sp.dma_start(dst, src).then_inc(const_in, 16)

            def load_group(b, i, kk):
                static = isinstance(i, int)
                k = XSLOTS * i + kk
                slot = kk % XSLOTS
                img = x[bass.ds(b, 1)].rearrange("a c r w -> (a c) r w")
                for s in range(2):
                    lo, n, at = s * ROWS + BAND * k - R0, BAND, BAND * slot
                    if static and k == 0 and s == 0:
                        lo, n, at = 0, BAND - R0, at + R0
                    if static and k == NBAND and s == 1:
                        n = BAND - R0
                    src = img[:, lo:lo + n, :] if static else img[:, bass.ds(lo, n), :]
                    sp.dma_start(xr[C * s:C * s + C, at:at + n, R0:R0 + W], src).then_inc(x_in[slot], 16)

            with sp.Fori(0, B) as b:
                hold(sp, (ring_free, b + 1))
                for k in range(4):
                    load_group(b, 0, k)

                def refill(i, kk):
                    hold(sp, (e_done, b * (NBAND * NQ) + i * (4 * NQ) + (kk - 4 + 1) * NQ))
                    load_group(b, i, kk)

                with sp.Fori(1, 4) as i:
                    for kk in range(4):
                        refill(i, kk)
                refill(4, 0)

                hold(sp, (e_done, (b + 1) * (NBAND * NQ)))
                for dst, src in ((pair_sb, pair), (wconv_sb, wconv), (mlp1_sb, mlp1), (mlp2_sb, mlp2), (mb2_sb, mb2),
                                 (std_sb[:, 0:TAPS], stdch), (sel_sf_sb.bitcast(mybir.dt.uint16), sel_sf)):
                    sp.dma_start(dst, src).then_inc(l1_const, 16)
                hold(sp, (norm_act, 5 * b + 1), (norm_dve, 3 * b + 1))
                sp.dma_start(E[0:C, ROWS + 2:ROWS + 4, 1:1 + W], E[C:2 * C, 2:4, 1:1 + W]).then_inc(halo_in, 16)
                sp.dma_start(E[C:2 * C, 0:2, 1:1 + W], E[0:C, ROWS:ROWS + 2, 1:1 + W]).then_inc(halo_in, 16)

                with sp.Fori(0, NO1 // 2) as i:
                    for j in range(2):
                        hold(sp, (out_done, b * NO1 + 2 * i + (1 + j)))
                        dst = out[bass.ds(b, 1)].rearrange("a c r w -> (a c) r w")
                        for s in range(2):
                            src = stage[C * s:C * s + C, j, :].rearrange("p (r w) -> p r w", w=W)
                            sp.dma_start(dst[:, bass.ds(i * 4 + (s * ROWS + 2 * j), 2), :], src)\
                              .then_inc(stored[j], 16)
            for j in range(2):
                sp.wait_ge(stored[j], B * (32 * NO1 // 2))

        @block.tensor
        def _(pe):
            pe.nop().then_inc(ring_free, 1)
            pe.wait_ge(const_in, 16 * N_CONST)
            pe.matmul(small_ps[0:FR, 0:1], center_sb, bs_raw, start=True, stop=True)\
              .then_inc(center_ready, 1)
            pe.wait_ge(setup_dve, 4)
            pe.wait_ge(nd, 3)

            def hidden(b, i, nn, q):
                if not (isinstance(i, int) and 16 * i + 4 * nn + q == 0):
                    pe.wait_ge(h_done, b * 64 + i * 16 + (nn * 4 + q))
                dst = h_ps[0:2 * HID, :].rearrange("p (g r c) -> p g r c", g=8, r=BAND)
                parts = pieces8(nn % XSLOTS)
                for ring, row, n in parts:
                    src = xr[:, ring:ring + n, R0 + COLS * q:R0 + COLS * q + COLS]
                    mm = pe.matmul(dst[:, :, row:row + n, :], w1_sb[:, :],
                                   src.rearrange("p r (g c) -> p g r c", c=8), start=True, stop=True)
                mm.then_inc(h_ready, 1)

            def width(b, i, nn, q):
                pe.wait_ge(h_done, b * 64 + i * 16 + (nn * 4 + q + 1))
                if q == 0 and not (isinstance(i, int) and i == 0 and nn == 0):
                    pe.wait_ge(k1_done, b * NBAND + i * 4 + nn)
                for t in range(NT):
                    v = 2 * (NT * q + t)
                    mm = pe.matmul(k_ps[:, v:v + 2], h_sb[:, 128 * t:128 * t + 128], w2_sb[:, :],
                                   start=True, stop=True)
                if q == NQ - 1:
                    mm.then_inc(ks_ready, 1)

            def turn_parts(b, i, nn, k):
                pe.wait_ge(parts_done[k], b * NBAND + i * 4 + (nn + 1))
                if k and not (isinstance(i, int) and 4 * i + nn == 0):
                    pe.wait_ge(rs_done, b * 64 + i * 16 + nn * 4)
                pe.transpose(turned_a[k], a_parts[:, k].rearrange("p g v -> p (g v)"), ident16_sb[:, :])\
                  .then_inc(parts_turned[k], 1)

            def turn_blocks(b, i, nn, q, g):
                turn = 12 * nn + 3 * q + g
                if not (isinstance(i, int) and 48 * i + turn == 0):
                    pe.wait_ge(xt_done, b * 192 + i * 48 + turn)
                pe.wait_ge(xb_done, b * 192 + i * 48 + (nn * 12 + q * 3 + g + 1))
                for j in range(3):
                    mm = pe.transpose(xt_ps[:, 128 * j:128 * j + 128], xb[:, (q + g) % 2, j, :], ident_sb[:, :])
                mm.then_inc(xt_ready, 1)

            def spread_a(b, i, nn, u, fresh=False):
                s, q = u % 2, u // 2
                if not fresh:
                    pe.wait_ge(arg_done, b * 128 + i * 32 + (nn * 8 + u - 1))
                if u == 0 or fresh:
                    pe.wait_ge(stack_done[0], b * NBAND + i * 4 + (nn + 1))
                for t in range(NT):
                    v = 2 * (NT * q + t) + s
                    mm = pe.matmul(abc_ps[u % 2][:, 128 * t:128 * t + 128],
                                   sel_a_sb[:, v:v + 1].to_broadcast([AROWS, 128]), a_st[:, nn % 2, 0, :],
                                   start=True, stop=True)
                mm.then_inc(abc_ready, 1)

            def spread_r(b, i, nn, q, first):
                if not first:
                    pe.wait_ge(rs_done, b * 64 + i * 16 + (nn * 4 + q))
                if q == 0:
                    pe.wait_ge(stack_done[1], b * NBAND + i * 4 + (nn + 1))
                for t in range(NT):
                    for s in range(2):
                        v = 2 * (NT * q + t) + s
                        mm = pe.matmul(rs_ps[C * s:C * s + C, 128 * t:128 * t + 128],
                                       sel_a_sb[:, v:v + 1].to_broadcast([AROWS, C]), a_st[:, nn % 2, 1, :],
                                       start=True, stop=True)
                mm.then_inc(rs_ready, 1)

            def blur(b, i, nn, u, first, blocks):
                s, q = u % 2, u // 2
                if blocks[0] == 0:
                    pe.wait_ge(exp_done, b * 128 + i * 32 + (nn * 8 + u + 1))
                if s == 0 and blocks[0] == 0:
                    pe.wait_ge(xt_done, b * 192 + i * 48 + (nn * 12 + q * 3 + 3))
                    if not (first and q < 2):
                        pe.wait_ge(blur_done, b * 64 + i * 16 + (nn * 4 + q - 1))
                moving = band[:, buffer(nn, u)].rearrange("p g k o -> p (g k o)")
                for j in range(*blocks):
                    lo, hi = max(0, 128 * j - 64), min(128 * NG, 128 * j + 64)
                    out_lo, out_hi = max(0, 64 * (j - 1)), min(64 * NG, 64 * (j + 1))
                    mm = pe.matmul(low_ps[q % 2][C * s:C * s + C, out_lo:out_hi], xt[:, q % 2, j, s, :],
                                   moving[:, lo:hi], start=(j == 0), stop=(j == BLK - 1),
                                   skip_group_check=True)
                if blocks[1] == BLK:
                    mm.then_inc(bands_done, 1)

            def band_steps(b, i, nn, last):
                first = isinstance(i, int) and 4 * i + nn == 0
                for u in range(UB):
                    q = u // 2
                    nq, nb = (q + 1, nn) if q + 1 < NQ else (0, nn + 1)
                    more = not (last and q + 1 == NQ)
                    blur(b, i, nn, u, first, (0, 5))
                    if u + 3 < UB:
                        spread_a(b, i, nn, u + 3)
                    elif not last:
                        spread_a(b, i, nn + 1, u + 3 - UB)
                    if u == 1:
                        turn_parts(b, i, nn, 1)
                    if u == 1 and not last:
                        width(b, i, nn + 1, NQ - 1)
                    if u == 3 and not last:
                        turn_parts(b, i, nn + 1, 0)
                    if more:
                        turn_blocks(b, i, nb, nq, 0 if u % 2 == 0 else 2)
                    blur(b, i, nn, u, first, (5, BLK))
                    if u % 2 == 0 and u:
                        spread_r(b, i, nn, q - 1, first and u == 2)
                    elif u == 0 and not first:
                        spread_r(b, i, nn - 1, NQ - 1, False)
                    if more and u % 2 == 0:
                        turn_blocks(b, i, nb, nq, 1)
                    if u >= 5 and not (isinstance(i, int) and 4 * i + nn + 2 >= NBAND):
                        mlp(b, i, nn + 2, u - 5)
                    if u == 0 and not last:
                        mlp(b, i, nn + 1, 3)

            def mlp(b, i, nn, q):
                if q == 0:
                    pe.wait_ge(*x_loaded(b, i, nn + 1))
                    if isinstance(i, int) and 4 * i + nn + 1 == NBAND:
                        pe.wait_ge(pad16_done, b + 1)
                else:
                    width(b, i, nn, q - 1)
                hidden(b, i, nn, q)

            def filters(b, i, kk):
                if not (isinstance(i, int) and 4 * i + kk == 0):
                    pe.wait_ge(fs_done, b * NC1 + i * 4 + kk)
                rows = E[:, bass.ds(i * 8 + (2 * kk + 1), 2), 1:1 + W] if not isinstance(i, int) else \
                    E[:, 8 * i + 2 * kk + 1:8 * i + 2 * kk + 3, 1:1 + W]
                pe.matmul(f_ps[0:FR, :], ws_sb[:, :], rows, start=True, stop=True).then_inc(f_ready, 1)

            def turn_filters(b, i, kk):
                waits = [(fs_done, b * NC1 + i * 4 + (kk + 1))]
                if not (isinstance(i, int) and 4 * i + kk == 0):
                    waits.append((fq_done, b * NC1 + i * 4 + kk))
                hold(pe, *waits)
                for j in range(4):
                    mm = pe.transpose(fx_ps[:, FR * j:FR * j + FR], fs[:, 128 * j:128 * j + 128],
                                      ident_sb[0:FR, 0:FR])
                mm.then_inc(fx_ready, 1)

            def turn_split(b, i, kk):
                pe.wait_ge(f_parts_done, b * NC1 + i * 4 + (kk + 1))
                if not (isinstance(i, int) and 4 * i + kk == 0):
                    pe.wait_ge(f_split, b * NC1 + i * 4 + kk)
                if not (isinstance(i, int) and 4 * i + kk == NC1 - 1):
                    pe.wait_ge(fq_done, b * NC1 + i * 4 + (kk + 2))
                for j in range(4):
                    mm = pe.transpose(fst_ps[:, 128 * j:128 * j + 128],
                                      f_parts[:, j].rearrange("p g v -> p (g v)"), ident16_sb[:, :])
                mm.then_inc(f_turned, 1)

            def spread_filter(b, i, kk, t, fresh):
                if t == 0:
                    pe.wait_ge(f_split, b * NC1 + i * 4 + (kk + 1))
                if not (fresh and t < 3):
                    pe.wait_ge(prod_done, b * (NC1 * TAPS) + i * (4 * TAPS) + (kk * TAPS + t - 2))
                pe.matmul(spread_ps[t % 3][:, :], sel_sf_sb[:, t, :], sf_st[:, kk % 2, :],
                          start=True, stop=True).then_inc(spread_ready, 1)

            def conv_tap(b, i, kk, t):
                if t == 0:
                    if isinstance(i, int) and 4 * i + kk == 1:
                        pe.wait_ge(y1_edge, 4 * b + 3)
                        pe.wait_ge(l1_const, 112 * (b + 1))
                    if not (isinstance(i, int) and 4 * i + kk < 3):
                        pe.wait_ge(conv_kept, b * NO1 + i * 4 + (kk - 2))
                if t == 3:
                    pe.wait_ge(y1_ready, b * NC1 + i * 4 + (kk + 1))
                    if isinstance(i, int) and 4 * i + kk == NO1:
                        pe.wait_ge(y1_edge, 4 * b + 4)
                pair, dx = t // 3, t % 3
                mm = pe.matmul(conv_ps[kk % 2][:, :], wconv_sb[:, t, :],
                               y1[:, (kk - 1 + pair) % YSLOTS, :, dx:dx + W],
                               start=(t == 0), stop=(t == CTAPS - 1))
                if t == CTAPS - 1:
                    mm.then_inc(conv_ready, 1)

            def l1_step(b, i, kk):
                k = 4 * i + kk if isinstance(i, int) else None
                if k is None or k + 2 < NC1:
                    filters(b, i, kk + 2)
                for t in range(TAPS):
                    spread_filter(b, i, kk, t, fresh=(k == 0))
                    if t in CONV_AT and (k is None or k >= 3):
                        conv_tap(b, i, kk - 2, CONV_AT.index(t))
                    if t == 4 and (k is None or k + 2 < NC1):
                        turn_filters(b, i, kk + 2)
                    if t == 5 and (k is None or k + 1 < NC1):
                        turn_split(b, i, kk + 1)

            with pe.Fori(0, B) as b:
                pe.wait_ge(pads_done, 3 * b + 3)
                pe.wait_ge(setup_pool, 4)
                pe.wait_ge(*x_loaded(b, 0, 0))
                pe.wait_ge(*x_loaded(b, 0, 1))
                for q in range(NQ):
                    hidden(b, 0, 0, q)
                    width(b, 0, 0, q)
                for g in range(3):
                    turn_blocks(b, 0, 0, 0, g)
                turn_parts(b, 0, 0, 0)
                for u in range(2):
                    spread_a(b, 0, 0, u, fresh=True)
                spread_a(b, 0, 0, 2)
                for q in range(3):
                    mlp(b, 0, 1, q)
                for nn in range(4):
                    band_steps(b, 0, nn, False)
                with pe.Fori(1, 3) as i:
                    for nn in range(4):
                        band_steps(b, i, nn, False)
                for nn in range(4):
                    band_steps(b, 3, nn, nn == 3)
                spread_r(b, 3, 3, NQ - 1, False)

                pe.wait_ge(mv_done, b + 1)
                pe.wait_ge(l1_const, 112 * (b + 1))
                pe.matmul(small_ps[:, 0:2], pair_sb[:, 0, :], mv, start=True, stop=True)
                pe.matmul(small_ps[:, 2:4], pair_sb[:, 1, :], mv, start=True, stop=True)\
                  .then_inc(pair_ready, 1)
                pe.wait_ge(halo_in, 32 * (b + 1))
                filters(b, 0, 0)
                turn_filters(b, 0, 0)
                filters(b, 0, 1)
                turn_filters(b, 0, 1)
                pe.wait_ge(pooled_done, b + 1)
                pe.wait_ge(l1_const, 112 * (b + 1))
                pe.matmul(small_ps[0:MID, 8:9], mlp1_sb, pooled_c, start=True, stop=True)\
                  .then_inc(mlp1_ready, 1)
                pe.wait_ge(h12_done, b + 1)
                for t in range(TAPS):
                    mm = pe.matmul(small_ps[:, 16 + t:17 + t], mlp2_sb[:, t, :], h12_c, start=True, stop=True)
                mm.then_inc(mlp2_ready, 1)
                pe.wait_ge(fpad_done, b + 1)
                turn_split(b, 0, 0)
                l1_step(b, 0, 0)
                for kk in range(1, 5):
                    l1_step(b, 0, kk)
                with pe.Fori(1, 15) as i:
                    for kk in range(1, 5):
                        l1_step(b, i, kk)
                for kk in range(1, 5):
                    l1_step(b, 15, kk)
                for kk in range(3, 5):
                    for t in range(CTAPS):
                        conv_tap(b, 15, kk, t)
                hold(pe, (conv_ready, (b + 1) * NO1))
                pe.nop().then_inc(ring_free, 1)

        @block.scalar
        def _(act):
            act.wait_ge(const_in, 16 * N_CONST)

            def relu(b, i, nn, q):
                act.wait_ge(h_ready, b * 64 + i * 16 + (nn * 4 + q + 1))
                act.activation(h_sb, h_ps[0:2 * HID, :], ACT.Relu,
                               bias=b1_c[0:2 * HID]).then_inc(h_done, 1)

            def square(b, i, nn):
                act.wait_ge(k2_done, b * NBAND + i * 4 + (nn + 1))
                act.activation(ka, kb, ACT.Square, scale=float(4.5 ** -0.5)).then_inc(ksq_done, 1)

            def weight_sums(b, i, nn, v0, v1):
                if v0 == 0:
                    act.wait_ge(a_ready, b * NBAND + i * 4 + (nn + 1))
                for v in range(v0, v1):
                    if not (isinstance(i, int) and 4 * i + nn == 0 and v < 2):
                        act.wait_ge(s_act, b * (NBAND * VA) + i * (4 * VA) + (nn * VA + v - 1))
                    act.activation(junk[:, v % 2], g81_neg[:, :], ACT.Exp, scale=a_pix[:, v:v + 1],
                                   accum_out=s_pix[:, v:v + 1]).then_inc(s_act, 1)

            def tap_weights(b, i, nn, k):
                act.wait_ge(taparg_done, b * (NBAND * NP) + i * (4 * NP) + (nn * NP + k + 1))
                t = taps[:, k % 2].rearrange("p v w -> p (v w)")
                act.activation(t, t, ACT.Exp).then_inc(tapexp_done, 1)

            def keep_r(b, i, nn, q):
                act.wait_ge(rs_ready, b * 64 + i * 16 + (nn * 4 + q + 1))
                act.activation(place(i, nn, q, 0, BAND), rs_ps[:, :].rearrange("p (g r c) -> p g r c", g=8, r=BAND),
                               ACT.Copy).then_inc(rs_done, 1)

            def keep_block(b, i, nn, q, g):
                act.wait_ge(xt_ready, b * 192 + i * 48 + (nn * 12 + q * 3 + g + 1))
                act.activation(xt[:, q % 2, 3 * g:3 * g + 3, :, 0:C],
                               xt_ps[:, 0:384].rearrange("p (j s c) -> p j s c", j=3, s=2),
                               ACT.Copy).then_inc(xt_done, 1)

            def weights(b, i, nn, u):
                act.wait_ge(arg_done, b * 128 + i * 32 + (nn * 8 + u + 1))
                t = band[:, buffer(nn % 4, u)].rearrange("p g k o -> p (g k o)")
                act.activation(t, t, ACT.Exp).then_inc(exp_done, 1)

            def band_steps(b, i, nn, last):
                first = isinstance(i, int) and 4 * i + nn == 0
                for u in range(UB):
                    q = u // 2
                    nq, nb = (q + 1, nn) if q + 1 < NQ else (0, nn + 1)
                    more = not (last and q + 1 == NQ)
                    if more:
                        keep_block(b, i, nb, nq, 0 if u % 2 == 0 else 2)
                    if u + 2 < UB:
                        weights(b, i, nn, u + 2)
                    elif not last:
                        weights(b, i, nn + 1, u + 2 - UB)
                    if u % 2 == 0 and u:
                        keep_r(b, i, nn, q - 1)
                    elif u == 0 and not first:
                        keep_r(b, i, nn - 1, NQ - 1)
                    if more and u % 2 == 0:
                        keep_block(b, i, nb, nq, 1)
                    if u == 0 and not last:
                        relu(b, i, nn + 1, 3)
                    if u >= 5 and not (isinstance(i, int) and 4 * i + nn + 2 >= NBAND):
                        relu(b, i, nn + 2, u - 5)
                    if u == 1 and not last:
                        square(b, i, nn + 1)
                    if 3 <= u < 3 + NP and not last:
                        tap_weights(b, i, nn + 1, u - 3)
                    if 3 <= u < 7 and not last:
                        weight_sums(b, i, nn + 1, (u - 3) * VA // 4, (u - 2) * VA // 4)

            def filt_bias(b, i, kk):
                act.wait_ge(f_ready, b * NC1 + i * 4 + (kk + 1))
                if not (isinstance(i, int) and 4 * i + kk == 0):
                    act.wait_ge(fx_ready, b * NC1 + i * 4 + kk)
                act.activation(fs, f_ps[0:FR, :], ACT.Identity, bias=bs_c[0:FR],
                               scale=STD_SPATIAL).then_inc(fs_done, 1)

            def filt_square(b, i, kk):
                act.wait_ge(fx_ready, b * NC1 + i * 4 + (kk + 1))
                act.activation(fx[:, kk % 2].rearrange("p v t -> p (v t)"), fx_ps, ACT.Copy).then_inc(fx_done, 1)
                if not (isinstance(i, int) and 4 * i + kk == 0):
                    act.wait_ge(fsum_done, b * NC1 + i * 4 + kk)
                act.activation(fq, fx_ps, ACT.Square).then_inc(fq_done, 1)

            def filt_sqrt(b, i, kk):
                act.wait_ge(fsum_done, b * NC1 + i * 4 + (kk + 1))
                act.activation(fsd[:, kk % 2], fsum, ACT.Sqrt,
                               scale=1.0 / ((TAPS - 1) * STD_SPATIAL ** 2)).then_inc(fsd_done, 1)

            def filt_split(b, i, kk):
                act.wait_ge(fnorm_done, b * NC1 + i * 4 + (kk + 1))
                if not (isinstance(i, int) and 4 * i + kk == 0):
                    act.wait_ge(f_turned, b * NC1 + i * 4 + kk)
                v = fn.rearrange("p (j v) -> p j v", j=4)
                act.activation(f_parts[:, :, 0, 0:FR], v, ACT.Copy).then_inc(f_hi, 1)
                act.wait_ge(f_res, b * NC1 + i * 4 + (kk + 1))
                act.activation(f_parts[:, :, 1, 0:FR], fres.rearrange("p (j v) -> p j v", j=4), ACT.Copy)\
                   .then_inc(f_mid, 1)

            def filt_keep(b, i, kk):
                act.wait_ge(f_turned, b * NC1 + i * 4 + (kk + 1))
                act.activation(sf_st[:, kk % 2, :], fst_ps, ACT.Copy).then_inc(f_split, 1)

            def lift(b, i, kk):
                act.wait_ge(sumb_done, b * (NDVE * NC1) + i * (4 * NDVE) + (kk * NDVE + NDVE))
                if not (isinstance(i, int) and 4 * i + kk == 0):
                    act.wait_ge(leaked_done, b * NC1 + i * 4 + kk)
                act.activation(lifted, sumb, ACT.Relu, scale=-0.9).then_inc(lifted_done, 1)

            def pair_rows(b, i, kk):
                act.wait_ge(leaked_done, b * NC1 + i * 4 + (kk + 1))
                if not (isinstance(i, int) and 4 * i + kk < YSLOTS):
                    act.wait_ge(conv_ready, b * NO1 + i * 4 + (kk - 3))
                for s in range(2):
                    for r in range(2):
                        if isinstance(i, int) and (4 * i + kk, s, r) in ((0, 0, 0), (NC1 - 1, 1, 1)):
                            continue
                        op = act.activation(y1[C * r:C * r + C, kk % YSLOTS, s, 1:1 + W],
                                            leaked[C * s:C * s + C, W * r:W * r + W], ACT.Copy)
                op.then_inc(y1_ready, 1)

            def keep_conv(b, i, kk):
                act.wait_ge(conv_ready, b * NO1 + i * 4 + kk)
                if not (isinstance(i, int) and 4 * i + kk < 3):
                    act.wait_ge(stored[(kk - 1) % 2], b * (16 * NO1) + i * 64 + 32 * ((kk - 1) // 2))
                for s in range(2):
                    for r in range(2):
                        op = act.activation(stage[C * s:C * s + C, (kk - 1) % 2, W * r:W * r + W],
                                            conv_ps[kk % 2][C * r:C * r + C, W * s:W * s + W], ACT.Identity,
                                            bias=bconv_c[C * r:C * r + C])
                op.then_inc(conv_kept, 1)

            def l1_step(b, i, kk):
                k = 4 * i + kk if isinstance(i, int) else 0
                if k + 2 < NC1:
                    filt_bias(b, i, kk + 2)
                if not isinstance(i, int) or k >= 4:
                    keep_conv(b, i, kk - 3)
                if k + 1 < NC1:
                    filt_split(b, i, kk + 1)
                if not isinstance(i, int) or k >= 1:
                    lift(b, i, kk - 1)
                if k + 2 < NC1:
                    filt_square(b, i, kk + 2)
                if not isinstance(i, int) or k >= 1:
                    pair_rows(b, i, kk - 1)
                if k + 1 < NC1:
                    filt_keep(b, i, kk + 1)
                if k + 2 < NC1:
                    filt_sqrt(b, i, kk + 2)

            with act.Fori(0, B) as b:
                for q in range(NQ):
                    relu(b, 0, 0, q)
                square(b, 0, 0)
                for g in range(3):
                    keep_block(b, 0, 0, 0, g)
                tap_weights(b, 0, 0, 0)
                for u in range(2):
                    weights(b, 0, 0, u)
                for k in range(1, NP):
                    tap_weights(b, 0, 0, k)
                weight_sums(b, 0, 0, 0, VA)
                for q in range(3):
                    relu(b, 0, 1, q)
                for nn in range(4):
                    band_steps(b, 0, nn, False)
                with act.Fori(1, 3) as i:
                    for nn in range(4):
                        band_steps(b, i, nn, False)
                for nn in range(4):
                    band_steps(b, 3, nn, nn == 3)
                keep_r(b, 3, 3, NQ - 1)
                act.wait_ge(nvar_done, b + 1)
                act.activation(sd_c, var_c, ACT.Sqrt).then_inc(nsd_done, 1)
                act.wait_ge(ncoef_done, b + 1)
                for j in range(5):
                    rows = E[:, 2 + 16 * j:18 + 16 * j, 1:1 + W]
                    act.activation(rows, rows, ACT.Identity, bias=nmr_c, scale=rstd_c,
                                   accum_out=sums[:, j:j + 1]).then_inc(norm_act, 1)
                    if j == 2:
                        filt_bias(b, 0, 0)
                    if j == 3:
                        filt_square(b, 0, 0)
                        filt_bias(b, 0, 1)
                filt_sqrt(b, 0, 0)
                filt_square(b, 0, 1)
                act.wait_ge(mlp1_ready, b + 1)
                act.activation(h12_c, small_ps[0:MID, 8:9], ACT.Relu, bias=mb1_c[0:MID],
                               scale=1.0 / NPIX).then_inc(h12_done, 1)
                filt_split(b, 0, 0)
                filt_sqrt(b, 0, 1)
                filt_keep(b, 0, 0)
                act.wait_ge(css_done, b + 1)
                act.activation(csd_c, css_c, ACT.Sqrt, scale=1.0 / (TAPS - 1)).then_inc(csd_done, 1)
                for kk in range(5):
                    l1_step(b, 0, kk)
                with act.Fori(1, 15) as i:
                    for kk in range(1, 5):
                        l1_step(b, i, kk)
                for kk in range(1, 5):
                    l1_step(b, 15, kk)
                lift(b, 15, 4)
                pair_rows(b, 15, 4)
                keep_conv(b, 15, 2)
                keep_conv(b, 15, 3)
                keep_conv(b, 15, 4)
                all_stored(act, b)

        @block.vector
        def _(dve):
            dve.wait_ge(const_in, 16 * N_CONST)
            gflat = g_neg[:, :, :].rearrange("p k o -> p (k o)")
            dve.tensor_tensor(gflat, graw_sb, gin_sb, ALU.mult).then_inc(setup_dve, 1)
            dve.tensor_scalar(g81_neg[:, :], g81_neg[:, :], -1.0, None, ALU.mult).then_inc(setup_dve, 1)
            wv = ws_sb[:, :].rearrange("p (s t) -> p s t", t=TAPS)
            dve.tensor_reduce(wmean, wv, AX_X, ALU.add).then_inc(nd, 1)
            dve.wait_ge(setup_dve, 2)
            dve.scalar_tensor_tensor(gflat, gflat, -1.0, gout_sb, ALU.mult, ALU.add).then_inc(setup_dve, 1)
            dve.wait_ge(nd, 1)
            dve.tensor_scalar(wmean, wmean, -1.0 / TAPS, None, ALU.mult).then_inc(nd, 1)
            dve.wait_ge(nd, 2)
            dve.tensor_tensor(wv, wv, wmean.unsqueeze(2).to_broadcast([128, 2, TAPS]), ALU.add)\
               .then_inc(setup_dve, 1)
            dve.wait_ge(center_ready, 1)
            dve.tensor_scalar(bs_c[0:FR], small_ps[0:FR, 0:1], STD_SPATIAL, None, ALU.mult)\
               .then_inc(nd, 1)
            dve.wait_ge(setup_dve, 4)
            dve.wait_ge(nd, 3)

            def width_a(b, i, nn):
                dve.wait_ge(ks_ready, b * NBAND + i * 4 + (nn + 1))
                dve.tensor_scalar(ka, k_ps, b2_c, 0.0, ALU.add, ALU.max).then_inc(k1_done, 1)
                dve.wait_ge(k1_done, b * NBAND + i * 4 + (nn + 1))
                dve.tensor_scalar(kb, ka, 20.0, 1.0, ALU.mult, ALU.add).then_inc(k2_done, 1)

            def split(b, i, nn, k, src):
                n = b * NBAND + i * 4 + (nn + 1)
                if not (isinstance(i, int) and 4 * i + nn == 0):
                    dve.wait_ge(parts_turned[k], b * NBAND + i * 4 + nn)
                dve.tensor_copy(a_parts[:, k, 0], src).then_inc(hi_done[k], 1)
                dve.wait_ge(hi_done[k], n)
                dve.tensor_tensor(res_pix, src, a_parts[:, k, 0], ALU.subtract).then_inc(res_done[k], 1)
                dve.wait_ge(res_done[k], n)
                dve.tensor_copy(a_parts[:, k, 1], res_pix).then_inc(mid_done[k], 1)
                dve.wait_ge(mid_done[k], n)
                dve.tensor_tensor(a_parts[:, k, 2], res_pix, a_parts[:, k, 1], ALU.subtract)\
                   .then_inc(parts_done[k], 1)

            def width_b(b, i, nn):
                dve.wait_ge(ksq_done, b * NBAND + i * 4 + (nn + 1))
                dve.reciprocal(a_pix, ka).then_inc(a_ready, 1)
                dve.wait_ge(a_ready, b * NBAND + i * 4 + (nn + 1))
                split(b, i, nn, 0, a_pix)

            def tap_argument(b, i, nn, k):
                if not (isinstance(i, int) and 4 * i + nn == 0 and k < 2):
                    dve.wait_ge(s_ready, b * (NBAND * NP) + i * (4 * NP) + (nn * NP + k - 1))
                dve.tensor_tensor(taps[:, k % 2], g81_neg[:, :].unsqueeze(1).to_broadcast([128, VP, K0 * K0]),
                                  a_pix[:, VA + VP * k:VA + VP * k + VP].unsqueeze(2).to_broadcast([128, VP, K0 * K0]),
                                  ALU.mult).then_inc(taparg_done, 1)

            def tap_sum(b, i, nn, k):
                dve.wait_ge(tapexp_done, b * (NBAND * NP) + i * (4 * NP) + (nn * NP + k + 1))
                dve.tensor_reduce(s_pix[:, VA + VP * k:VA + VP * k + VP], taps[:, k % 2], AX_X, ALU.add).then_inc(s_ready, 1)

            def sum_reciprocal(b, i, nn):
                dve.wait_ge(s_ready, b * (NBAND * NP) + i * (4 * NP) + (nn * NP + NP))
                dve.wait_ge(s_act, b * (NBAND * VA) + i * (4 * VA) + (nn * VA + VA))
                dve.reciprocal(r_pix, s_pix).then_inc(r_ready, 1)
                dve.wait_ge(r_ready, b * NBAND + i * 4 + (nn + 1))
                split(b, i, nn, 1, r_pix)

            def keep_parts(b, i, nn, k):
                dve.wait_ge(parts_turned[k], b * NBAND + i * 4 + (nn + 1))
                dve.tensor_copy(a_st[:, nn % 2, k, :], turned_a[k]).then_inc(stack_done[k], 1)

            def argument(b, i, nn, u):
                dve.wait_ge(abc_ready, b * 128 + i * 32 + (nn * 8 + u + 1))
                if not (isinstance(i, int) and 32 * i + 8 * nn + u < NBUF):
                    dve.wait_ge(bands_done, b * 128 + i * 32 + (nn * 8 + u + 1 - NBUF))
                a = abc_ps[u % 2][:, :].rearrange("p (g o) -> p g o", g=NG)
                dve.tensor_tensor(band[:, buffer(nn % 4, u)], g_neg[:, :, :].unsqueeze(1).to_broadcast([128, NG, 2, 64]),
                                  a.unsqueeze(2).to_broadcast([128, NG, 2, 64]), ALU.mult)\
                   .then_inc(arg_done, 1)

            def enhance(b, i, nn, q):
                done = b * 64 + i * 16 + (nn * 4 + q + 1)
                dve.wait_ge(rs_done, done)
                dve.wait_ge(bands_done, b * 128 + i * 32 + (nn * 8 + 2 * q + 2))
                c0 = COLS * q

                dve.tensor_tensor(place(i, nn, q, 0, BAND),
                                  low_ps[q % 2][:, :].rearrange("p (g r c) -> p g r c", g=8, r=BAND),
                                  place(i, nn, q, 0, BAND), ALU.mult).then_inc(blur_done, 1)
                dve.wait_ge(blur_done, done)
                for ring, row, n in pieces8(nn % XSLOTS):
                    res = xr[:, ring:ring + n, R0 + c0:R0 + c0 + COLS].rearrange("p r (g c) -> p g r c", c=8)
                    op = dve.tensor_tensor(place(i, nn, q, row, n), place(i, nn, q, row, n), res, ALU.add)
                op.then_inc(e_done, 1)
                dve.wait_ge(e_done, done)
                r0 = BAND * nn + 2
                rows = slice(4 * BAND * i + r0, 4 * BAND * i + r0 + BAND) if isinstance(i, int) else \
                    bass.ds(i * (4 * BAND) + r0, BAND)
                at = slice(16 * i + 4 * nn + q, 16 * i + 4 * nn + q + 1) if isinstance(i, int) else \
                    bass.ds(i * 16 + (4 * nn + q), 1)
                dve.bn_stats(stats[:, at, :].rearrange("p a s -> p (a s)"), E[:, rows, 1 + c0:1 + c0 + COLS])\
                   .then_inc(stats_done, 1)

            def band_steps(b, i, nn, last):
                first = isinstance(i, int) and 4 * i + nn == 0
                for u in range(UB):
                    if u + 2 < UB:
                        argument(b, i, nn, u + 2)
                    elif not last:
                        argument(b, i, nn + 1, u + 2 - UB)
                    if u == 2 and not last:
                        width_b(b, i, nn + 1)
                    if u == 4 and not last:
                        keep_parts(b, i, nn + 1, 0)
                    if u % 2 and u > 1:
                        enhance(b, i, nn, (u - 3) // 2)
                    elif u == 1 and not first:
                        enhance(b, i, nn - 1, NQ - 1)
                    if u == 1:
                        keep_parts(b, i, nn, 1)
                    if u == 1 and not last:
                        width_a(b, i, nn + 1)
                    if not last:
                        if 4 <= u < 4 + NP:
                            tap_sum(b, i, nn + 1, u - 4)
                        if 2 <= u < 2 + NP:
                            tap_argument(b, i, nn + 1, u - 2)
                        if u == 7:
                            sum_reciprocal(b, i, nn + 1)

            def square_sum(b, i, kk):
                dve.wait_ge(fq_done, b * NC1 + i * 4 + (kk + 1))
                if not (isinstance(i, int) and 4 * i + kk == 0):
                    dve.wait_ge(fsd_done, b * NC1 + i * 4 + kk)
                dve.tensor_reduce(fsum, fq.rearrange("p (v t) -> p v t", t=TAPS), AX_X, ALU.add)\
                   .then_inc(fsum_done, 1)

            def reciprocal(b, i, kk):
                n = b * NC1 + i * 4 + (kk + 1)
                dve.wait_ge(fsd_done, n)
                dve.tensor_scalar(fsd[:, kk % 2], fsd[:, kk % 2], EPS1, None, ALU.add).then_inc(feps_done, 1)
                dve.wait_ge(feps_done, n)
                if not (isinstance(i, int) and 4 * i + kk == 0):
                    dve.wait_ge(f_res, b * NC1 + i * 4 + kk)
                dve.reciprocal(frec, fsd[:, kk % 2]).then_inc(frec_done, 1)
                dve.wait_ge(frec_done, n)
                dve.tensor_tensor(fn.rearrange("p (v t) -> p v t", t=TAPS), fx[:, kk % 2],
                                  frec.unsqueeze(2).to_broadcast([128, 8, TAPS]), ALU.mult)\
                   .then_inc(fnorm_done, 1)

            def tap(b, i, kk, t):
                k0 = b * (NC1 * TAPS) + i * (4 * TAPS) + kk * TAPS
                if t < NPOOL and not (isinstance(i, int) and 4 * i + kk == 0):
                    dve.wait_ge(suma_done, b * ((NPOOL - 1) * NC1) + i * (4 * (NPOOL - 1)) +
                                ((NPOOL - 1) * (kk - 1) + max(1, t)))
                dve.wait_ge(spread_ready, k0 + (t + 1))
                if t == NPOOL and not (isinstance(i, int) and 4 * i + kk == 0):
                    dve.wait_ge(leaked_done, b * NC1 + i * 4 + kk)
                if t > NPOOL + 2:
                    dve.wait_ge(sumb_done, b * (NDVE * NC1) + i * (4 * NDVE) + (NDVE * kk + t - NPOOL - 2))
                dst = prod[:, t, :] if t < NPOOL else sumb if t == NPOOL else tmp[:, t % 2, :]
                dy, dx = t // 3, t % 3
                r0 = 2 * kk + dy
                rows = slice(8 * i + r0, 8 * i + r0 + 2) if isinstance(i, int) else bass.ds(i * 8 + r0, 2)
                dve.scalar_tensor_tensor(dst.rearrange("p (r w) -> p r w", w=W),
                                         spread_ps[t % 3][:, :].rearrange("p (r w) -> p r w", w=W),
                                         cf[:, t:t + 1], E[:, rows, dx:dx + W], ALU.mult, ALU.mult)\
                   .then_inc(prod_done, 1)

            def add(b, i, kk, n, src, t):
                dve.wait_ge(prod_done, b * (NC1 * TAPS) + i * (4 * TAPS) + (kk * TAPS + t + 1))
                if n:
                    dve.wait_ge(sumb_done, b * (NDVE * NC1) + i * (4 * NDVE) + (NDVE * kk + n))
                dve.tensor_tensor(sumb, sumb, src, ALU.add).then_inc(sumb_done, 1)

            def add_a(b, i, kk):
                dve.wait_ge(suma_done, b * ((NPOOL - 1) * NC1) + i * (4 * (NPOOL - 1)) + (NPOOL - 1) * (kk + 1))
                add(b, i, kk, NDVE - 1, suma, TAPS - 1)

            def final(b, i, kk):
                dve.wait_ge(conv_kept, b * NO1 + i * 4 + kk)
                r0 = 2 * kk
                rows = slice(8 * i + r0, 8 * i + r0 + 2) if isinstance(i, int) else bass.ds(i * 8 + r0, 2)
                rows_out = stage[:, (kk - 1) % 2, :].rearrange("p (r w) -> p r w", w=W)
                dve.tensor_tensor(rows_out, rows_out, E[:, rows, 1:1 + W], ALU.add).then_inc(out_done, 1)

            def l1_step(b, i, kk):
                k = 4 * i + kk if isinstance(i, int) else None
                for t in range(TAPS):
                    tap(b, i, kk, t)
                    if t == 0 and (k is None or k + 1 < NC1):
                        reciprocal(b, i, kk + 1)
                    if t == 5 and (k is None or k >= 4):
                        final(b, i, kk - 3)
                    if t == 7 and (k is None or k + 2 < NC1):
                        square_sum(b, i, kk + 2)
                    if t > NPOOL + 1:
                        add(b, i, kk, t - NPOOL - 2, tmp[:, (t - 1) % 2, :], t - 1)
                    if t == 0 and (k is None or k > 0):
                        add(b, i, kk - 1, NDVE - 2, tmp[:, (TAPS - 1) % 2, :], TAPS - 1)
                    if t == LAST_ADD and (k is None or k > 0):
                        add_a(b, i, kk - 1)
                if k == NC1 - 1:
                    add(b, i, kk, NDVE - 2, tmp[:, (TAPS - 1) % 2, :], TAPS - 1)
                    add_a(b, i, kk)

            with dve.Fori(0, B) as b:
                width_a(b, 0, 0)
                width_b(b, 0, 0)
                for k in range(NP):
                    tap_argument(b, 0, 0, k)
                    if k == 0:
                        keep_parts(b, 0, 0, 0)
                        for u in range(2):
                            argument(b, 0, 0, u)
                    tap_sum(b, 0, 0, k)
                sum_reciprocal(b, 0, 0)
                for nn in range(4):
                    band_steps(b, 0, nn, False)
                with dve.Fori(1, 3) as i:
                    for nn in range(4):
                        band_steps(b, i, nn, False)
                for nn in range(4):
                    band_steps(b, 3, nn, nn == 3)
                enhance(b, 3, 3, NQ - 1)
                n0 = b * 5 + 3
                hold(dve, (stats_done, b * 64 + 64))
                dve.bn_aggr(mv, stats[:, :, :].rearrange("p a s -> p (a s)")).then_inc(mv_done, 1)
                dve.wait_ge(pair_ready, b + 1)
                dve.tensor_copy(pv, small_ps[:, 0:4]).then_inc(nd, 1)
                dve.wait_ge(nd, n0 + 1)
                dve.tensor_tensor(var_c, pv[:, 2:3], pv[:, 2:3], ALU.mult).then_inc(nd, 1)
                dve.wait_ge(nd, n0 + 2)
                dve.tensor_tensor(var_c, var_c, pv[:, 1:2], ALU.add).then_inc(nd, 1)
                dve.wait_ge(nd, n0 + 3)
                dve.tensor_scalar(var_c, var_c, 1e-5, None, ALU.add).then_inc(nvar_done, 1)
                dve.wait_ge(nsd_done, b + 1)
                dve.reciprocal(rstd_c, sd_c).then_inc(nd, 1)
                dve.wait_ge(nd, n0 + 4)
                dve.tensor_scalar(nmr_c, pv[:, 0:1], -1.0, rstd_c, ALU.mult, ALU.mult).then_inc(ncoef_done, 1)
                dve.wait_ge(ncoef_done, b + 1)
                for j in (7, 5, 6):
                    rows = E[:, 2 + 16 * j:18 + 16 * j, 1:1 + W]
                    dve.tensor_scalar(rows, rows, rstd_c, nmr_c, ALU.mult, ALU.add).then_inc(norm_dve, 1)
                for n, j in enumerate((7, 5, 6)):
                    dve.wait_ge(norm_dve, 3 * b + (n + 1))
                    dve.tensor_reduce(sums[:, j:j + 1], E[:, 2 + 16 * j:18 + 16 * j, 1:1 + W],
                                      mybir.AxisListType.XY, ALU.add).then_inc(sums_dve, 1)
                    if n == 1:
                        square_sum(b, 0, 0)
                dve.wait_ge(norm_act, 5 * b + 5)
                dve.wait_ge(sums_dve, 3 * b + 3)
                dve.tensor_reduce(pooled_c, sums, AX_X, ALU.add).then_inc(pooled_done, 1)
                reciprocal(b, 0, 0)
                square_sum(b, 0, 1)
                c0 = b * 7
                dve.wait_ge(mlp2_ready, b + 1)
                dve.tensor_tensor(cc, small_ps[:, 16:16 + TAPS], mb2_sb, ALU.add).then_inc(cf_steps, 1)
                dve.wait_ge(cf_steps, c0 + 1)
                dve.tensor_reduce(cm_c, cc, AX_X, ALU.add).then_inc(cf_steps, 1)
                dve.wait_ge(cf_steps, c0 + 2)
                dve.tensor_scalar(cm_c, cm_c, -1.0 / TAPS, None, ALU.mult).then_inc(cf_steps, 1)
                dve.wait_ge(cf_steps, c0 + 3)
                dve.tensor_scalar(cc, cc, cm_c, None, ALU.add).then_inc(cf_steps, 1)
                dve.wait_ge(cf_steps, c0 + 4)
                dve.tensor_tensor(cf, cc, cc, ALU.mult).then_inc(cf_steps, 1)
                dve.wait_ge(cf_steps, c0 + 5)
                dve.tensor_reduce(css_c, cf, AX_X, ALU.add).then_inc(css_done, 1)
                dve.wait_ge(csd_done, b + 1)
                dve.tensor_scalar(csd_c, csd_c, EPS1, None, ALU.add).then_inc(cf_steps, 1)
                dve.wait_ge(cf_steps, c0 + 6)
                dve.reciprocal(cr_c, csd_c).then_inc(cf_steps, 1)
                dve.wait_ge(cf_steps, c0 + 7)
                dve.scalar_tensor_tensor(cf, cc, cr_c, std_sb[:, 0:TAPS], ALU.mult, ALU.mult)\
                   .then_inc(nd, 1)
                dve.wait_ge(nd, n0 + 5)
                for kk in range(5):
                    l1_step(b, 0, kk)
                with dve.Fori(1, 15) as i:
                    for kk in range(1, 5):
                        l1_step(b, i, kk)
                for kk in range(1, 5):
                    l1_step(b, 15, kk)
                final(b, 15, 2)
                final(b, 15, 3)
                final(b, 15, 4)
                all_stored(dve, b)

        @block.gpsimd
        def _(pool):
            pool.wait_ge(setup_dve, 4)
            pool.wait_ge(center_ready, 1)
            pool.memset(E[:, 0:2, :], 0.0).then_inc(setup_pool, 1)
            pool.memset(E[:, ER - 2:ER, :], 0.0).then_inc(setup_pool, 1)
            pool.memset(E[:, 2:ER - 2, 0:1], 0.0).then_inc(setup_pool, 1)
            pool.memset(E[:, 2:ER - 2, EW - 1:EW], 0.0).then_inc(setup_pool, 1)

            def pack(b, i, nn, q):
                for g in range(3):
                    first = isinstance(i, int) and 4 * i + nn == 0 and q == 0 and g < 2
                    if not first:
                        hold(pool, (xt_ready, b * 192 + i * 48 + (nn * 12 + q * 3 + g - 1)))
                    c0 = COLS * q + 24 * g
                    dst = xb[:, (q + g) % 2].rearrange("p j (r c) -> p j r c", c=8)
                    lo = BAND * (nn % XSLOTS)
                    parts = [(lo, 0, 16)] if nn % XSLOTS < XSLOTS - 1 else [(lo, 0, 8), (0, 8, 8)]
                    for ring, row, n in parts:
                        src = xr[:, ring:ring + n, c0:c0 + 24].rearrange("p r (j c) -> p j r c", c=8)
                        op = pool.tensor_copy(dst[:, :, row:row + n, :], src)
                    op.then_inc(xb_done, 1)

            def band_steps(b, i, nn, last):
                for q in range(NQ):
                    nq, nb = (q + 1, nn) if q + 1 < NQ else (0, nn + 1)
                    if nq == 0 and not last:
                        pool.wait_ge(*x_loaded(b, i, nb + 1))
                        if isinstance(i, int) and 4 * i + nb + 1 == NBAND:
                            pool.wait_ge(pad16_done, b + 1)
                    if not (last and nq == 0):
                        pack(b, i, nb, nq)
                    if isinstance(i, int) and 4 * i + nn == 13 and q == 0:
                        hold(pool, (e_done, b * 64 + 13 * NQ), (xb_done, b * 192 + (13 * 12 + 6)))
                        pool.memset(xr[C:2 * C, R0:BAND, R0:R0 + W], 0.0).then_inc(pad16_done, 1)
                        pool.wait_ge(pad16_done, b + 1)

            def split_f(b, i, kk):
                n = b * NC1 + i * 4 + (kk + 1)
                pool.wait_ge(f_hi, n)
                res = fres.rearrange("p (j v) -> p j v", j=4)
                pool.tensor_tensor(res, fn.rearrange("p (j v) -> p j v", j=4), f_parts[:, :, 0, 0:FR],
                                   ALU.subtract).then_inc(f_res, 1)
                pool.wait_ge(f_mid, n)
                pool.tensor_tensor(f_parts[:, :, 2, 0:FR], res, f_parts[:, :, 1, 0:FR], ALU.subtract)\
                    .then_inc(f_parts_done, 1)

            def sum_a(b, i, kk):
                p0 = b * (NC1 * TAPS) + i * (4 * TAPS) + kk * TAPS
                s0 = b * ((NPOOL - 1) * NC1) + i * (4 * (NPOOL - 1)) + (NPOOL - 1) * kk
                pool.wait_ge(prod_done, p0 + 2)
                if not (isinstance(i, int) and 4 * i + kk == 0):
                    pool.wait_ge(sumb_done, b * (NDVE * NC1) + i * (4 * NDVE) + NDVE * kk)
                pool.tensor_tensor(suma, prod[:, 0, :], prod[:, 1, :], ALU.add).then_inc(suma_done, 1)
                for t in range(2, NPOOL):
                    pool.wait_ge(prod_done, p0 + (t + 1))
                    pool.wait_ge(suma_done, s0 + (t - 1))
                    pool.tensor_tensor(suma, suma, prod[:, t, :], ALU.add).then_inc(suma_done, 1)

            def leaky(b, i, kk):
                pool.wait_ge(lifted_done, b * NC1 + i * 4 + (kk + 1))
                if not (isinstance(i, int) and 4 * i + kk == 0):
                    pool.wait_ge(y1_ready, b * NC1 + i * 4 + kk)
                pool.tensor_tensor(leaked, sumb, lifted, ALU.add).then_inc(leaked_done, 1)

            def l1_step(b, i, kk):
                if not (isinstance(i, int) and 4 * i + kk == NC1 - 1):
                    split_f(b, i, kk + 1)
                if not isinstance(i, int) or 4 * i + kk > 0:
                    leaky(b, i, kk - 1)
                sum_a(b, i, kk)

            with pool.Fori(0, B) as b:
                hold(pool, (ring_free, b + 1))
                pool.memset(xr[:, :, 0:R0], 0.0).then_inc(pads_done, 1)
                pool.memset(xr[:, :, R0 + W:XW], 0.0).then_inc(pads_done, 1)
                pool.memset(xr[0:C, 0:R0, R0:R0 + W], 0.0).then_inc(pads_done, 1)
                hold(pool, (pads_done, 3 * b + 3), x_loaded(b, 0, 0), x_loaded(b, 0, 1))
                pack(b, 0, 0, 0)
                for nn in range(4):
                    band_steps(b, 0, nn, False)
                with pool.Fori(1, 3) as i:
                    for nn in range(4):
                        band_steps(b, i, nn, False)
                for nn in range(4):
                    band_steps(b, 3, nn, nn == 3)
                hold(pool, (e_done, b * 64 + 64))
                pool.memset(y1[:, :, :, 0:1], 0.0).then_inc(y1_edge, 1)
                pool.memset(y1[:, :, :, EW - 1:EW], 0.0).then_inc(y1_edge, 1)
                pool.memset(y1[0:C, 0, 0, 1:1 + W], 0.0).then_inc(y1_edge, 1)
                pool.memset(f_parts[:, :, :, FR:32], 0.0).then_inc(fpad_done, 1)
                split_f(b, 0, 0)
                split_f(b, 0, 1)
                sum_a(b, 0, 0)
                for kk in range(1, 5):
                    l1_step(b, 0, kk)
                with pool.Fori(1, 15) as i:
                    for kk in range(1, 5):
                        l1_step(b, i, kk)
                for kk in range(1, 5):
                    l1_step(b, 15, kk)
                leaky(b, 15, 4)
                hold(pool, (conv_ready, b * NO1 + (NO1 - 3)), (leaked_done, b * NC1 + NC1))
                pool.memset(y1[C:2 * C, 0, 1, 1:1 + W], 0.0).then_inc(y1_edge, 1)
                all_stored(pool, b)


def _window_index():
    p, o = np.arange(128), np.arange(64)
    ir, ic, r, c = p // 8, p % 8, o // 8, o % 8
    u = ir[:, None] - r[None, :]
    index = np.zeros((128, 2, 64), np.int64)
    inside = np.zeros((128, 2, 64), bool)
    for kind in range(2):
        v = (ic[:, None] - c[None, :]) + 8 * kind
        ok = (u >= 0) & (u < K0) & (v >= 0) & (v < K0)
        inside[:, kind] = ok
        index[:, kind] = np.where(ok, u * K0 + v, 0)
    return index.reshape(128, 128), inside.reshape(128, 128)


def _layout(i):
    f = np.float32
    index, inside = _window_index()
    d = {"x": np.asarray(i["x"])}
    d["graw"] = np.asarray(i["L0_conv_gauss_kernel"]).reshape(-1)[index]
    d["gin"] = inside.astype(f)
    d["gout"] = np.where(inside, f(0), f(FAR)).astype(f)
    d["g81"] = np.broadcast_to(np.asarray(i["L0_conv_gauss_kernel"]).reshape(1, K0 * K0), (128, K0 * K0))
    sel = np.zeros((AROWS, NV), np.uint16)
    for g in range(3):
        for v in range(NV):
            sel[32 * g + v, v] = BF16_ONE
    d["sel_a"] = sel
    d["ident16"] = np.where(np.eye(128, dtype=bool), np.uint16(BF16_ONE), np.uint16(0))
    d["ident"] = np.eye(128, dtype=f)
    w1 = np.zeros((128, 2 * HID), f)
    w2 = np.zeros((2 * HID, 2), f)
    for s in range(2):
        w1[C * s:C * s + C, HID * s:HID * s + HID] = np.asarray(i["L0_conv_w1"])
        w2[HID * s:HID * s + HID, s] = np.asarray(i["L0_conv_w2"])[:, 0]
    d["w1"], d["w2"] = w1, w2
    pair = np.zeros((128, 2, 128), f)
    for m in range(128):
        pair[m, 0, m] = pair[(m + 64) % 128, 0, m] = 0.5
        pair[m, 1, m], pair[(m + 64) % 128, 1, m] = 0.5, -0.5
    d["pair"] = pair
    ws = np.zeros((128, FR), f)
    bs = np.zeros((FR, 1), f)
    center = np.zeros((FR, FR), f)
    sel_sf = np.zeros((AROWS, TAPS, 128), np.uint16)
    for s in range(2):
        r = slice(TAPS * s, TAPS * s + TAPS)
        ws[C * s:C * s + C, r] = np.asarray(i["L1_conv_Ws"]).T
        bs[r, 0] = np.asarray(i["L1_conv_bs"])
        center[r, r] = np.eye(TAPS, dtype=f) - f(1.0 / TAPS)
        for g in range(3):
            for t in range(TAPS):
                sel_sf[32 * g + TAPS * s + t, t, C * s:C * s + C] = BF16_ONE
    d["ws"], d["bs"], d["center"], d["sel_sf"] = ws, bs, center, sel_sf
    wc = np.zeros((2, C, 2, 3, 2, C), f)
    taps = np.asarray(i["L1_conv_Wc"]).transpose(1, 2, 3, 0)
    for pair in range(2):
        for row in range(2):
            for o in range(2):
                ky = 2 * pair + row - o
                if 0 <= ky < 3:
                    wc[row, :, pair, :, o, :] = taps[:, ky]
    d["wconv"] = wc.reshape(128, CTAPS, 128)
    small = np.zeros((128, 5), f)
    small[0:HID, 0] = small[HID:2 * HID, 0] = np.asarray(i["L0_conv_b1"])
    small[:, 1] = np.asarray(i["L0_conv_b2"])[0]
    small[0:C, 3] = small[C:, 3] = np.asarray(i["L1_conv_bc"])
    small[0:MID, 4] = np.asarray(i["L1_conv_b1"])
    d["small"] = small
    d["mlp1"] = np.concatenate([np.asarray(i["L1_conv_W1"]).T] * 2, axis=0)
    w2t = np.asarray(i["L1_conv_W2"]).reshape(C, TAPS, MID).transpose(2, 1, 0)
    d["mlp2"] = np.concatenate([w2t, w2t], axis=2)
    d["mb2"] = np.concatenate([np.asarray(i["L1_conv_b2"]).reshape(C, TAPS)] * 2, axis=0)
    d["stdch"] = np.concatenate([np.asarray(i["L1_conv_std_ch"]).reshape(C, TAPS)] * 2, axis=0)
    return d


_ORDER = ["x", "graw", "gin", "gout", "g81", "sel_a", "ident", "ident16", "w1", "w2", "pair", "ws", "bs", "center",
          "sel_sf", "wconv", "small", "mlp1", "mlp2", "mb2", "stdch"]


def kernel(**inputs):
    import concourse.bacc as _bacc
    from concourse.bass_utils import run_bass_kernel_spmd as _run

    nc = _bacc.Bacc("TRN2", target_bir_lowering=False, num_devices=1)
    laid = _layout(inputs)
    arrays, args = {}, {}
    for name in _ORDER:
        a = np.ascontiguousarray(laid[name])
        arrays[f"in_{name}"] = a
        args[name] = nc.dram_tensor(f"in_{name}", a.shape, mybir.dt.from_np(a.dtype), kind="ExternalInput").ap()
    o = nc.dram_tensor("out_0", (B, C, H, W), F32, kind="ExternalOutput").ap()
    build(nc, out=o, **args)
    r = _run(nc, [arrays], core_ids=[0])
    return r.results[0]["out_0"]
```
